# Optimizing a Trainium2 kernel written in Bass

```python
import numpy as np
import jax
import jax.numpy as jnp

def _softmax(x, axis=-1):
    return jax.nn.softmax(x, axis=axis)

def _gelu(x):
    return jax.nn.gelu(x, approximate=True)

def _silu(x):
    return jax.nn.silu(x)

def _sigmoid(x):
    return jax.nn.sigmoid(x)

def _layernorm(x, axis=-1, eps=1e-05):
    m = jnp.mean(x, axis=axis, keepdims=True)
    v = jnp.var(x, axis=axis, keepdims=True)
    return (x - m) / jnp.sqrt(v + eps)

def _scatter_add(tgt, idx, src, axis=0):
    return tgt.at[idx].add(src)

def _segment_sum(src, seg, n):
    return jax.ops.segment_sum(src, seg, n)
kernel_name = 'mk_recurrent_d1_jaxref_r4_31ef1f'

def setup_inputs(seed: int=0):
    np.random.seed(seed)
    _w = jnp.asarray

    def _L0_attn_setup():
        import jax, jax.numpy as jnp
        import numpy as np
        import math
        B, T, D, H = (4, 512, 256, 16)
        HD = D // H
        ROPE_BASE = 10000.0

        def apply_rope(x):
            t, hd = (x.shape[2], x.shape[3])
            half = hd // 2
            theta = 1.0 / ROPE_BASE ** (jnp.arange(0, hd, 2, dtype=jnp.float32) / hd)
            pos = jnp.arange(1, t + 1, dtype=jnp.float32)
            ang = pos[:, None] * theta[None, :]
            ang = jnp.concatenate([ang, ang], axis=-1)
            sin, cos = (jnp.sin(ang), jnp.cos(ang))
            rot = jnp.concatenate([-x[..., half:], x[..., :half]], axis=-1)
            return x * cos[None, None, :, :] + rot * sin[None, None, :, :]
        key = jax.random.key(seed)
        ks = jax.random.split(key, 9)
        s = 1.0 / math.sqrt(D)
        return {'x': jax.random.normal(ks[0], (B, T, D), dtype=jnp.float32), 'Wq': jax.random.normal(ks[1], (D, D), dtype=jnp.float32) * s, 'bq': jax.random.normal(ks[2], (D,), dtype=jnp.float32) * 0.01, 'Wk': jax.random.normal(ks[3], (D, D), dtype=jnp.float32) * s, 'bk': jax.random.normal(ks[4], (D,), dtype=jnp.float32) * 0.01, 'Wv': jax.random.normal(ks[5], (D, D), dtype=jnp.float32) * s, 'bv': jax.random.normal(ks[6], (D,), dtype=jnp.float32) * 0.01, 'Wo': jax.random.normal(ks[7], (D, D), dtype=jnp.float32) * s, 'bo': jax.random.normal(ks[8], (D,), dtype=jnp.float32) * 0.01}
    _L0_attn_in = _L0_attn_setup()

    def _L0_ffn_setup():
        import jax, jax.numpy as jnp
        import numpy as np
        TOP_K = 2
        CAPACITY = 1024
        EPS = 1e-06
        W_SCALE = 0.02

        def _rms(x, w):
            return x * jax.lax.rsqrt(jnp.mean(x * x, axis=-1, keepdims=True) + EPS) * w
        key = jax.random.key(seed)
        ks = jax.random.split(key, 8)
        B, S, H, F, E = (8, 1024, 256, 512, 8)
        F4 = F // 4
        return {'hidden_states': jax.random.normal(ks[0], (B, S, H), jnp.float32), 'Wr': jax.random.normal(ks[1], (H, E), jnp.float32) * W_SCALE, 'norm_w': jnp.ones((E, H), jnp.float32), 'Wg': jax.random.normal(ks[2], (E, H, F), jnp.float32) * W_SCALE, 'Wu': jax.random.normal(ks[3], (E, H, F), jnp.float32) * W_SCALE, 'Wd': jax.random.normal(ks[4], (E, F, H), jnp.float32) * W_SCALE, 'f_norm': jnp.ones((H,), jnp.float32), 'fWg': jax.random.normal(ks[5], (H, F4), jnp.float32) * W_SCALE, 'fWu': jax.random.normal(ks[6], (H, F4), jnp.float32) * W_SCALE, 'fWd': jax.random.normal(ks[7], (F4, H), jnp.float32) * W_SCALE}
    _L0_ffn_in = _L0_ffn_setup()
    _d = {'L0_attn_x': _L0_attn_in['x'], 'L0_attn_Wq': _L0_attn_in['Wq'], 'L0_attn_bq': _L0_attn_in['bq'], 'L0_attn_Wk': _L0_attn_in['Wk'], 'L0_attn_bk': _L0_attn_in['bk'], 'L0_attn_Wv': _L0_attn_in['Wv'], 'L0_attn_bv': _L0_attn_in['bv'], 'L0_attn_Wo': _L0_attn_in['Wo'], 'L0_attn_bo': _L0_attn_in['bo'], 'L0_ffn_Wr': _L0_ffn_in['Wr'], 'L0_ffn_norm_w': _L0_ffn_in['norm_w'], 'L0_ffn_Wg': _L0_ffn_in['Wg'], 'L0_ffn_Wu': _L0_ffn_in['Wu'], 'L0_ffn_Wd': _L0_ffn_in['Wd'], 'L0_ffn_f_norm': _L0_ffn_in['f_norm'], 'L0_ffn_fWg': _L0_ffn_in['fWg'], 'L0_ffn_fWu': _L0_ffn_in['fWu'], 'L0_ffn_fWd': _L0_ffn_in['fWd']}
    _x0 = _d['L0_attn_x']
    _d['L0_attn_x'] = jax.random.normal(jax.random.fold_in(jax.random.key(seed), 1), (2, 2048, 256), dtype=_x0.dtype)
    del _x0
    return _d

def reference(L0_attn_x, L0_attn_Wq, L0_attn_bq, L0_attn_Wk, L0_attn_bk, L0_attn_Wv, L0_attn_bv, L0_attn_Wo, L0_attn_bo, L0_ffn_Wr, L0_ffn_norm_w, L0_ffn_Wg, L0_ffn_Wu, L0_ffn_Wd, L0_ffn_f_norm, L0_ffn_fWg, L0_ffn_fWu, L0_ffn_fWd):

    def _L0_attn_ref(x, Wq, bq, Wk, bk, Wv, bv, Wo, bo):
        import jax, jax.numpy as jnp
        import numpy as np
        import math
        B, T, D, H = (4, 512, 256, 16)
        HD = D // H
        ROPE_BASE = 10000.0

        def apply_rope(x):
            t, hd = (x.shape[2], x.shape[3])
            half = hd // 2
            theta = 1.0 / ROPE_BASE ** (jnp.arange(0, hd, 2, dtype=jnp.float32) / hd)
            pos = jnp.arange(1, t + 1, dtype=jnp.float32)
            ang = pos[:, None] * theta[None, :]
            ang = jnp.concatenate([ang, ang], axis=-1)
            sin, cos = (jnp.sin(ang), jnp.cos(ang))
            rot = jnp.concatenate([-x[..., half:], x[..., :half]], axis=-1)
            return x * cos[None, None, :, :] + rot * sin[None, None, :, :]
        b, t, d = x.shape
        h, hd = (H, HD)
        q = x @ Wq.T + bq
        k = x @ Wk.T + bk
        v = x @ Wv.T + bv
        split = lambda z: z.reshape(b, t, h, hd).transpose(0, 2, 1, 3)
        q, k, v = (split(q), split(k), split(v))
        q = apply_rope(q)
        k = apply_rope(k)
        scale = math.sqrt(hd)
        att = jnp.einsum('bhqd,bhkd->bhqk', q, k) / scale
        mask = jnp.tril(jnp.ones((t, t), dtype=bool))
        att = jnp.where(mask[None, None, :, :], att, -jnp.inf)
        att = jax.nn.softmax(att, axis=-1)
        y = jnp.einsum('bhqk,bhkd->bhqd', att, v)
        y = y.transpose(0, 2, 1, 3).reshape(b, t, d)
        y = y @ Wo.T + bo
        return y

    def _L0_ffn_ref(hidden_states, Wr, norm_w, Wg, Wu, Wd, f_norm, fWg, fWu, fWd):
        import jax, jax.numpy as jnp
        import numpy as np
        TOP_K = 2
        CAPACITY = 1024
        EPS = 1e-06
        W_SCALE = 0.02

        def _rms(x, w):
            return x * jax.lax.rsqrt(jnp.mean(x * x, axis=-1, keepdims=True) + EPS) * w
        B, S, H = hidden_states.shape
        E = Wr.shape[1]
        N = B * S
        x = hidden_states.reshape(N, H)
        probs = jax.nn.softmax(x @ Wr, axis=-1)
        w_topk, e_topk = jax.lax.top_k(probs, TOP_K)
        e_flat = e_topk.reshape(-1)
        oh = jax.nn.one_hot(e_flat, E, dtype=jnp.int32)
        pos = jnp.take_along_axis(jnp.cumsum(oh, axis=0) - 1, e_flat[:, None], axis=1)[:, 0]
        keep = pos < CAPACITY
        x_rep = jnp.repeat(x, TOP_K, axis=0)
        buf = jnp.zeros((E, CAPACITY, H), x.dtype).at[e_flat, pos].set(x_rep, mode='drop')
        h = _rms(buf, norm_w[:, None, :])
        gate = jax.nn.gelu(jnp.einsum('ech,ehf->ecf', h, Wg), approximate=False)
        up = jnp.einsum('ech,ehf->ecf', h, Wu)
        buf_out = jnp.einsum('ecf,efh->ech', gate * up, Wd) + buf
        exp_out = buf_out[e_flat, jnp.minimum(pos, CAPACITY - 1)]
        contrib = w_topk.reshape(-1)[:, None] * exp_out * keep[:, None].astype(x.dtype)
        combined = x + contrib.reshape(N, TOP_K, H).sum(axis=1)
        overflow = (~keep).reshape(N, TOP_K).any(axis=1)
        fh = _rms(x, f_norm)
        fout = jax.nn.gelu(fh @ fWg, approximate=False) * (fh @ fWu) @ fWd + x
        out = jnp.where(overflow[:, None], fout, combined)
        return out.reshape(B, S, H)
    x = L0_attn_x
    xn = _layernorm(x, axis=-1)
    s = _L0_attn_ref(xn, L0_attn_Wq, L0_attn_bq, L0_attn_Wk, L0_attn_bk, L0_attn_Wv, L0_attn_bv, L0_attn_Wo, L0_attn_bo)
    g = _silu(_L0_ffn_ref(xn, L0_ffn_Wr, L0_ffn_norm_w, L0_ffn_Wg, L0_ffn_Wu, L0_ffn_Wd, L0_ffn_f_norm, L0_ffn_fWg, L0_ffn_fWu, L0_ffn_fWd))
    x = x + s * g
    return x

_drawn_inputs = setup_inputs


def setup_inputs(seed=0):
    import zlib

    import numpy as np

    out = dict(_drawn_inputs(seed))
    spreads = {'L0_ffn_norm_w': (1.0, 0.6), 'L0_ffn_f_norm': (1.0, 0.6)}
    factors = {'L0_attn_bq': 8.0,
     'L0_attn_bk': 8.0,
     'L0_attn_bv': 6.734,
     'L0_attn_bo': 7.011,
     'L0_ffn_Wr': 8.0,
     'L0_ffn_Wg': 8.0,
     'L0_ffn_Wu': 8.0,
     'L0_ffn_Wd': 8.0,
     'L0_ffn_fWg': 8.0,
     'L0_ffn_fWu': 8.0,
     'L0_ffn_fWd': 8.0}
    for name, (base, spread) in spreads.items():
        noise = np.random.default_rng([zlib.crc32(name.encode()), seed]).standard_normal(out[name].shape)
        drawn = base * np.exp(spread * noise) if base else spread * noise
        out[name] = jnp.asarray(drawn.astype(out[name].dtype))
    for name, factor in factors.items():
        out[name] = (out[name] * factor).astype(out[name].dtype)
    return out
```

```python
import math
from contextlib import ExitStack

import concourse.bass as bass
from concourse import mybir

F32 = mybir.dt.float32
F32R = mybir.dt.float32r
BF16 = mybir.dt.bfloat16
I32 = mybir.dt.int32
ALU = mybir.AluOpType
ACT = mybir.ActivationFunctionType
AX = mybir.AxisListType

P = 128
B, T, D = 2, 2048, 256
N = B * T
NT = N // P
CH = 512
TC = CH // P
CPB = T // CH
KD = D // P
H, HD = 16, 16
HG = 4
NG = H // HG
E, F, CAP = 8, 512, 1024
F4 = F // 4
KF = F // P
SLOTS = E * CAP
LN_EPS, RMS_EPS = 1e-5, 1e-6
NEG = -3.0e38


class Steps:

    def __init__(self, eng, sem):
        self.eng, self.sem, self.k, self.base, self.per, self.i = eng, sem, 0, 0, 0, None

    def mark(self, ins):
        ins.then_inc(self.sem, 1)
        self.k += 1
        return self.k

    def wait(self, k=None):
        k = self.k if k is None else k
        self.eng.wait_ge(self.sem, self.base + k if self.i is None else self.i * self.per + (self.base + k))

    def link(self, ins):
        self.mark(ins)
        self.wait()

    def enter(self, i, per):
        self.base, self.k, self.per, self.i = self.base + self.k, 0, per, i

    def leave(self, turns):
        assert self.k == self.per, (self.k, self.per)
        self.base, self.k, self.per, self.i = self.base + turns * self.per, 0, 0, None


def three_products(pe, out, weights, moving, first, last):
    terms = [(0, 0), (0, 1), (1, 0)]
    for n, (a, b) in enumerate(terms):
        mm = pe.matmul(out, weights[a], moving[b], start=first and n == 0, stop=last and n == 2)
    return mm


def normalise_route_project(nc, a, keep):
    with ExitStack() as ctx:
        def sb(name, shape, dt=F32):
            return ctx.enter_context(nc.sbuf_tensor(name, shape, dt))

        def ps(name, shape, dt=F32):
            return ctx.enter_context(nc.psum_tensor(name, shape, dt))

        def sem(name):
            return ctx.enter_context(nc.semaphore(name))

        xr_all = sb("xr_all", [P, NT, D])
        mv = sb("mv", [P, NT, 2])
        small = sb("small", [P, 6, NT])
        ident = sb("ident1", [P, P])
        wqkv = sb("wqkv", [P, 3, KD, D])
        wqkv_h = sb("wqkv_h", [P, 3, KD, D], F32R)
        wqkv_l = sb("wqkv_l", [P, 3, KD, D], F32R)
        wf = sb("wf", [P, 2, KD, F4])
        wf_h = sb("wf_h", [P, 2, KD, F4], F32R)
        wf_l = sb("wf_l", [P, 2, KD, F4], F32R)
        wfd = sb("wfd", [P, D])
        wfd_h = sb("wfd_h", [P, D], F32R)
        wfd_l = sb("wfd_l", [P, D], F32R)
        wr = sb("wr", [P, KD, E])
        wr_h = sb("wr_h", [P, KD, E], F32R)
        wr_l = sb("wr_l", [P, KD, E], F32R)
        bqk = sb("bqk", [P, 2, KD])
        bqs = sb("bqs", [P, 2, KD])
        bv = sb("bv", [1, D])
        bv_h = sb("bv_h", [1, D], F32R)
        bv_l = sb("bv_l", [1, D], F32R)
        ones_row = sb("ones_row", [1, P])
        ones_rowr = sb("ones_rowr", [1, P], F32R)
        fnorm = sb("fnorm", [P, KD])
        cos = sb("cos", [P, T])
        sin = sb("sin", [P, T])

        x_loaded = [sem(f"x_loaded{c}") for c in range(4)]
        w_loaded = sem("w_loaded")
        consts_loaded = sem("consts_loaded")
        zeros_set = sem("zeros_set")
        xb_zeroed = sem("xb_zeroed")
        w_high = sem("w_high")
        w_split = sem("w_split")
        stats_sqrt = sem("stats_sqrt")
        dve_steps = sem("dve_steps1")
        var_ready = sem("var_ready")
        ms_ready = sem("ms_ready")
        xn_ready = sem("xn_ready")
        xt_turned = sem("xt_turned")
        xt_high = sem("xt_high")
        xt_low = sem("xt_low")
        xt_high_stored = [sem(f"xt_high_stored{u}") for u in range(2)]
        xt_low_stored = [sem(f"xt_low_stored{u}") for u in range(2)]
        logits_made = sem("logits_made")
        logits_kept = sem("logits_kept")

        x_t = a["x"].rearrange("(t p) d -> p t d", p=P)
        WLOADS = 13

        with ExitStack() as c1:
            xn = [c1.enter_context(nc.sbuf_tensor(f"xn{u}", [P, TC, D], F32)) for u in range(2)]
            xh = [c1.enter_context(nc.sbuf_tensor(f"xh{u}", [P, KD, CH], F32R)) for u in range(2)]
            xl = [c1.enter_context(nc.sbuf_tensor(f"xl{u}", [P, KD, CH], F32R)) for u in range(2)]
            p_xt = [c1.enter_context(nc.psum_tensor(f"p_xt{u}", [P, KD, CH], F32)) for u in range(2)]
            p_lg = [c1.enter_context(nc.psum_tensor(f"p_lg{u}", [P, CH], F32)) for u in range(2)]
            x_all = c1.enter_context(nc.sbuf_tensor("x_all", [P, NT, D], F32))
            stats = c1.enter_context(nc.sbuf_tensor("stats", [P, NT, 6], F32))
            zeros = c1.enter_context(nc.sbuf_tensor("zeros", [P, 8 * D], F32))
            logits = keep["logits"]
            block = c1.enter_context(nc.Block())

            @block.sync
            def _(sp):
                for c in range(4):
                    n = NT // 4
                    sp.dma_start(x_all[:, c * n:(c + 1) * n, :], x_t[:, c * n:(c + 1) * n, :]).then_inc(x_loaded[c], 16)
                sp.dma_start(ident[:], a["ident"]).then_inc(consts_loaded, 16)
                sp.dma_start(wr[:], a["wr"].rearrange("(k p) e -> p k e", p=P)).then_inc(w_loaded, 16)
                for n, w in enumerate(("wqT", "wkT", "wvT")):
                    sp.dma_start(wqkv[:, n], a[w].rearrange("(k p) o -> p k o", p=P)).then_inc(w_loaded, 16)
                for n, w in enumerate(("fwg", "fwu")):
                    sp.dma_start(wf[:, n], a[w].rearrange("(k p) o -> p k o", p=P)).then_inc(w_loaded, 16)
                sp.dma_start(wfd[:], a["fwd"]).then_inc(w_loaded, 16)
                for n, w in enumerate(("bq", "bk")):
                    sp.dma_start(bqk[:, n], a[w]).then_inc(w_loaded, 16)
                sp.dma_start(bv[:], a["bv"]).then_inc(w_loaded, 16)
                sp.dma_start(fnorm[:], a["fnorm"]).then_inc(w_loaded, 16)
                sp.dma_start(cos[:], a["cos"]).then_inc(w_loaded, 16)
                sp.dma_start(sin[:], a["sin"]).then_inc(w_loaded, 16)
                sp.wait_ge(zeros_set, 1)
                for r in range(SLOTS // (8 * P)):
                    sp.dma_start(a["xb"][r * 8 * P:(r + 1) * 8 * P, :].rearrange("(p r) d -> p (r d)", p=P),
                                 zeros[:]).then_inc(xb_zeroed, 16)
                with sp.Fori(0, NT // TC // 2) as i:
                    for u in range(2):
                        at = bass.ds(i * (2 * CH) + u * CH, CH)
                        sp.wait_ge(xt_high, i * 2 + (u + 1))
                        sp.dma_start(a["xth"][:, :, at], xh[u][:].bitcast(F32)).then_inc(xt_high_stored[u], 16)
                        sp.wait_ge(xt_low, i * 2 + (u + 1))
                        sp.dma_start(a["xtl"][:, :, at], xl[u][:].bitcast(F32)).then_inc(xt_low_stored[u], 16)
                for u in range(2):
                    sp.wait_ge(xt_high_stored[u], 16 * (NT // TC // 2))
                    sp.wait_ge(xt_low_stored[u], 16 * (NT // TC // 2))
                sp.wait_ge(xb_zeroed, 16 * (SLOTS // (8 * P)))

            @block.gpsimd
            def _(pool):
                nc.gpsimd.memset(zeros[:], 0.0).then_inc(zeros_set, 1)

            @block.scalar
            def _(act):
                act.wait_ge(var_ready, 1)
                nc.scalar.activation(small[:, 1], small[:, 0], ACT.Sqrt).then_inc(stats_sqrt, 1)
                act.wait_ge(ms_ready, 1)
                nc.scalar.activation(small[:, 4], small[:, 3], ACT.Sqrt).then_inc(stats_sqrt, 1)
                act.wait_ge(w_loaded, 16 * WLOADS)
                for h, w in ((wr_h, wr), (wqkv_h, wqkv), (wf_h, wf), (wfd_h, wfd), (bv_h, bv)):
                    nc.scalar.copy(h[:], w[:]).then_inc(w_high, 1)
                with act.Fori(0, NT // TC // 2) as i:
                    for u in range(2):
                        act.wait_ge(xt_turned, i * 2 + (u + 1))
                        act.wait_ge(xt_high_stored[u], i * 16)
                        act.wait_ge(logits_made, i * 2)
                        nc.scalar.copy(xh[u][:], p_xt[u][:]).then_inc(xt_high, 1)

            @block.vector
            def _(dve):
                v = nc.vector
                st = Steps(dve, dve_steps)
                for c in range(4):
                    dve.wait_ge(x_loaded[c], 16)
                    for t in range(c * NT // 4, (c + 1) * NT // 4):
                        st.mark(v.bn_stats(stats[:, t, :], x_all[:, t, :]))
                st.wait()
                for t in range(NT):
                    st.mark(v.bn_aggr(mv[:, t, :], stats[:, t, :]))
                st.wait()
                var = mv[:, :, 1:2].rearrange("p t o -> p (t o)")
                mean = mv[:, :, 0:1].rearrange("p t o -> p (t o)")
                st.mark(v.tensor_copy(keep["mean"][:], mean))
                v.tensor_scalar(small[:, 0], var, LN_EPS, None, ALU.add).then_inc(var_ready, 1)

                def inverse_root(out, value, root, scratch):
                    st.link(v.reciprocal(out, root))
                    st.link(v.tensor_tensor(scratch, out, out, ALU.mult))
                    st.link(v.tensor_tensor(scratch, scratch, value, ALU.mult))
                    st.link(v.tensor_scalar(scratch, scratch, -0.5, 1.5, ALU.mult, ALU.add))
                    st.link(v.tensor_tensor(out, out, scratch, ALU.mult))

                dve.wait_ge(stats_sqrt, 1)
                dve.wait_ge(var_ready, 1)
                rstd, rr = keep["rstd"], small[:, 5]
                inverse_root(rstd[:], small[:, 0], small[:, 1], small[:, 2])
                st.link(v.tensor_tensor(small[:, 2], rstd[:], rstd[:], ALU.mult))
                st.link(v.tensor_tensor(small[:, 2], small[:, 2], var, ALU.mult))
                v.tensor_scalar(small[:, 3], small[:, 2], RMS_EPS, None, ALU.add).then_inc(ms_ready, 1)
                dve.wait_ge(ms_ready, 1)
                dve.wait_ge(stats_sqrt, 2)
                inverse_root(rr, small[:, 3], small[:, 4], small[:, 2])
                st.link(v.tensor_tensor(rr, rr, rstd[:], ALU.mult))
                for n, (w, h, low) in enumerate(((wr, wr_h, wr_l), (wqkv, wqkv_h, wqkv_l), (wf, wf_h, wf_l),
                                                 (wfd, wfd_h, wfd_l), (bv, bv_h, bv_l))):
                    dve.wait_ge(w_high, n + 1)
                    v.tensor_tensor(low[:], w[:], h[:].bitcast(F32), ALU.subtract).then_inc(w_split, 1)
                v.memset(ones_row[:], 1.0).then_inc(w_split, 1)
                dve.wait_ge(w_split, 6)
                v.tensor_copy(ones_rowr[:], ones_row[:]).then_inc(w_split, 1)
                v.tensor_scalar(bqs[:, 0], bqk[:, 0], 1.0 / math.sqrt(HD), None, ALU.mult).then_inc(w_split, 1)
                v.tensor_copy(bqs[:, 1], bqk[:, 1]).then_inc(w_split, 1)
                with dve.Fori(0, NT // TC // 2) as i:
                    for u in range(2):
                        dve.wait_ge(xt_turned, i * 2)
                        for t in range(TC):
                            tile = i * (2 * TC) + (u * TC + t)
                            cur = x_all[:, bass.ds(tile, 1), :].rearrange("p a d -> p (a d)")
                            v.tensor_scalar(xn[u][:, t, :], cur, keep["mean"][:, bass.ds(tile, 1)],
                                            rstd[:, bass.ds(tile, 1)], ALU.subtract, ALU.mult).then_inc(xn_ready, 1)
                        for t in range(TC):
                            tile = i * (2 * TC) + (u * TC + t)
                            cur = x_all[:, bass.ds(tile, 1), :].rearrange("p a d -> p (a d)")
                            dst = xr_all[:, bass.ds(tile, 1), :].rearrange("p a d -> p (a d)")
                            v.tensor_scalar(dst, cur, keep["mean"][:, bass.ds(tile, 1)],
                                            rr[:, bass.ds(tile, 1)], ALU.subtract, ALU.mult)
                        dve.wait_ge(xt_high, i * 2 + (u + 1))
                        dve.wait_ge(xt_low_stored[u], i * 16)
                        dve.wait_ge(logits_made, i * 2)
                        v.tensor_tensor(xl[u][:], p_xt[u][:], xh[u][:].bitcast(F32), ALU.subtract).then_inc(xt_low, 1)
                        dve.wait_ge(logits_made, i * 2 + (u + 1))
                        v.tensor_copy(logits[:, bass.ds(i * (2 * TC * E) + u * TC * E, TC * E)],
                                      p_lg[u][:, 0:TC * E]).then_inc(logits_kept, 1)

            @block.tensor
            def _(pe):
                t_ = nc.tensor
                pe.wait_ge(consts_loaded, 16)
                pe.wait_ge(w_split, 1)
                with pe.Fori(0, NT // TC // 2) as i:
                    for u in range(2):
                        pe.wait_ge(xn_ready, i * (2 * TC) + TC * (u + 1))
                        pe.wait_ge(xt_low, i * 2)
                        for k in range(KD):
                            for t in range(TC):
                                mm = t_.transpose(p_xt[u][:, k, t * P:(t + 1) * P], xn[u][:, t, k * P:(k + 1) * P], ident[:])
                        mm.then_inc(xt_turned, 1)
                        pe.wait_ge(xt_low, i * 2 + (u + 1))
                        pe.wait_ge(logits_kept, i * 2)
                        for t in range(TC):
                            for k in range(KD):
                                tok = slice(t * P, (t + 1) * P)
                                mm = three_products(t_, p_lg[u][:, t * E:(t + 1) * E], (xh[u][:, k, tok], xl[u][:, k, tok]),
                                                    (wr_h[:, k], wr_l[:, k]), k == 0, k == KD - 1)
                        mm.then_inc(logits_made, 1)


        xh = [sb(f"xh_in{u}", [P, KD, CH], F32R) for u in range(2)]
        xl = [sb(f"xl_in{u}", [P, KD, CH], F32R) for u in range(2)]
        xr = [sb(f"xr_in{u}", [P, TC, D]) for u in range(2)]
        v_out = [sb(f"v_out{u}", [P, TC, H, 2 * HD]) for u in range(2)]
        qf = [sb(f"qf{s}", [P, CH]) for s in range(2)]
        turned = [sb(f"turned{s}", [P, CH]) for s in range(2)]
        with_cos = [sb(f"with_cos{s}", [P, CH]) for s in range(2)]
        with_sin = [sb(f"with_sin{s}", [P, CH]) for s in range(2)]
        q = [sb(f"q{s}", [P, CH]) for s in range(2)]
        q_rest = [sb(f"q_rest{s}", [P, CH]) for s in range(2)]
        q_part = [[sb(f"q_part{m}{s}", [P, CH], BF16) for s in range(2)] for m in range(3)]
        fr_h = sb("fr_h", [P, KD, CH], F32R)
        fr_l = sb("fr_l", [P, KD, CH], F32R)
        gelu = sb("gelu", [P, CH])
        hid = sb("hid", [P, CH])
        hid_h = sb("hid_h", [P, CH], F32R)
        hid_l = sb("hid_l", [P, CH], F32R)
        f_out = sb("f_out", [P, TC, D])
        rt = sb("rt", [P, 10, NT * E])
        idx_m = sb("idx_m", [P, NT * E])
        runs = sb("runs", [P, NT * E])
        taken = sb("taken", [P, NT * E], BF16)
        tri = sb("tri", [P, P], BF16)
        ones_b = sb("ones_b", [P, P], BF16)
        trash = sb("trash", [P, 2, NT])
        pick = sb("pick", [P, 12, NT])
        pair = sb("pair", [P, 4, 2, NT])
        send = sb("send", [P, 2, NT], I32)

        p_qk = [ps(f"p_qk{s}", [P, CH]) for s in range(2)]
        p_vd = [ps(f"p_vd{s}", [P, 2, D]) for s in range(2)]
        p_fr = ps("p_fr", [P, KD, CH])
        p_g = ps("p_g", [P, CH])
        p_u = ps("p_u", [P, CH])

        rc_loaded = sem("rc_loaded")
        x_in = [sem(f"x_in{u}") for u in range(2)]
        ones_set = sem("ones_set")
        taken_ready = sem("taken_ready")
        counted = sem("counted")
        counts_read = sem("counts_read")
        route_max = sem("route_max")
        route_exp = sem("route_exp")
        send_ready = sem("send_ready")
        sent = sem("sent")
        fr_turned = sem("fr_turned")
        fr_high = sem("fr_high")
        fr_low = sem("fr_low")
        qk_made = sem("qk_made")
        qf_ready = sem("qf_ready")
        qf_used = sem("qf_used")
        q_ready = sem("q_ready")
        q_rest_ready = sem("q_rest_ready")
        q_part_ready = [sem(f"q_part_ready{m}") for m in range(3)]
        q_stored = [[sem(f"q_stored{m}{s}") for s in range(2)] for m in range(3)]
        gu_made = sem("gu_made")
        gelu_ready = sem("gelu_ready")
        hid_ready = sem("hid_ready")
        hid_high = sem("hid_high")
        hid_low = sem("hid_low")
        v_made = sem("v_made")
        v_kept = sem("v_kept")
        v_stored = [sem(f"v_stored{u}") for u in range(2)]
        down_made = sem("down_made")
        down_kept = sem("down_kept")
        down_stored = sem("down_stored")
        rope_steps = sem("rope_steps")

        block = ctx.enter_context(nc.Block())

        @block.sync
        def _(sp):
            for dst, src in ((idx_m, "idx_m"), (runs, "runs"), (tri, "tri"), (ones_b, "ones_b"), (trash, "trash")):
                sp.dma_start(dst[:], a[src]).then_inc(rc_loaded, 16)
            with sp.Fori(0, CPB) as i:
                for u in range(2):
                    tok = bass.ds(i * CH + u * T, CH)
                    sp.wait_ge(down_made, i * 4)
                    sp.dma_start(xh[u][:].bitcast(F32), a["xth"][:, :, tok]).then_inc(x_in[u], 16)
                    sp.dma_start(xl[u][:].bitcast(F32), a["xtl"][:, :, tok]).then_inc(x_in[u], 16)
                    sp.dma_start(xr[u][:], xr_all[:, bass.ds(i * TC + u * (T // P), TC), :]).then_inc(x_in[u], 16)
                for u in range(2):
                    tok = bass.ds(i * CH + u * T, CH)
                    pairs = bass.ds(i * (CH // 2) + u * (T // 2), CH // 2)
                    for n in range(2 * KD):
                        w, k = divmod(n, KD)
                        piece = sp.snap(i * 8 + (4 * u + n + 1))
                        for m in range(3):
                            sp.wait_ge(q_part_ready[m], piece)
                            sp.dma_start(a[f"qk{m}"][w, k].rearrange("p (n two) -> p n two", two=2)[:, pairs],
                                         q_part[m][n % 2][:].rearrange("p (n two) -> p n two", two=2)).then_inc(q_stored[m][n % 2], 16)
                    sp.wait_ge(v_kept, i * 4 + (2 * u + 2))
                    sp.dma_start(a["v"][tok, :].rearrange("(t p) c -> p t c", p=P),
                                 v_out[u][:].rearrange("p t h c -> p t (h c)")).then_inc(v_stored[u], 16)
                    sp.wait_ge(down_kept, i * 4 + (2 * u + 2))
                    sp.dma_start(a["fd"][tok, :].rearrange("(t p) c -> p t c", p=P), f_out[:]).then_inc(down_stored, 16)
            for s in range(2):
                for m in range(3):
                    sp.wait_ge(q_stored[m][s], 16 * 2 * 2 * CPB)
                sp.wait_ge(v_stored[s], 16 * CPB)
            sp.wait_ge(down_stored, 16 * 2 * CPB)

        @block.gpsimd
        def _(pool):
            for u in range(2):
                nc.gpsimd.memset(v_out[u][:], 1.0).then_inc(ones_set, 1)
            pool.wait_ge(send_ready, 1)
            for k in range(2):
                for t in range(NT):
                    nc.gpsimd.indirect_dma_start(
                        a["xb"], bass.IndirectOffsetOnAxis(ap=send[:, k, t:t + 1], axis=0), xr_all[:, t, :],
                        None).then_inc(sent, 16)
            pool.wait_ge(sent, 16 * 2 * NT)

        @block.scalar
        def _(act):
            s_ = nc.scalar
            act.wait_ge(ones_set, 2)
            with act.Fori(0, CPB) as i:
                for u in range(2):
                    def bias(n):
                        w, k = divmod(n, KD)
                        act.wait_ge(qk_made, i * 8 + (4 * u + n + 1))
                        if n >= 2:
                            act.wait_ge(qf_used, i * 8 + (4 * u + n - 1))
                        else:
                            act.wait_ge(qf_used, i * 8 + 4 * u)
                        s_.activation(qf[n % 2][:], p_qk[n % 2][:], ACT.Identity, bias=bqs[:, w, k:k + 1],
                                      scale=1.0 / math.sqrt(HD) if w == 0 else 1.0).then_inc(qf_ready, 1)

                    def first(n):
                        act.wait_ge(q_ready, i * 8 + (4 * u + n + 1))
                        act.wait_ge(q_stored[0][n % 2], i * (16 * 4) + 16 * (2 * u + n // 2))
                        s_.copy(q_part[0][n % 2][:], q[n % 2][:]).then_inc(q_part_ready[0], 1)

                    def second(n):
                        act.wait_ge(q_rest_ready, i * 8 + (4 * u + n + 1))
                        act.wait_ge(q_stored[1][n % 2], i * (16 * 4) + 16 * (2 * u + n // 2))
                        s_.copy(q_part[1][n % 2][:], q_rest[n % 2][:]).then_inc(q_part_ready[1], 1)

                    def values(n):
                        act.wait_ge(v_made, i * 4 + (2 * u + n + 1))
                        act.wait_ge(v_stored[u], i * 16)
                        s_.copy(v_out[u][:, 2 * n:2 * n + 2, :, 0:HD],
                                p_vd[n][:].rearrange("p t (h c) -> p t h c", c=HD)).then_inc(v_kept, 1)

                    act.wait_ge(fr_turned, i * 2 + (u + 1))
                    act.wait_ge(gu_made, i * 2 + u)
                    for k in range(KD):
                        s_.activation(fr_h[:, k], p_fr[:, k], ACT.Identity, scale=fnorm[:, k:k + 1]).then_inc(fr_high, 1)
                    bias(0)
                    bias(1)
                    first(0)
                    act.wait_ge(gu_made, i * 2 + (u + 1))
                    act.wait_ge(hid_ready, i * 2 + u)
                    s_.activation(gelu[:], p_g[:], ACT.Gelu).then_inc(gelu_ready, 1)
                    first(1)
                    bias(2)
                    second(0)
                    act.wait_ge(hid_ready, i * 2 + (u + 1))
                    act.wait_ge(down_made, i * 4 + 2 * u)
                    s_.copy(hid_h[:], hid[:]).then_inc(hid_high, 1)
                    second(1)
                    bias(3)
                    first(2)
                    values(0)
                    second(2)
                    values(1)
                    first(3)
                    second(3)
                    for n in range(2):
                        act.wait_ge(down_made, i * 4 + (2 * u + n + 1))
                        act.wait_ge(down_stored, i * 32 + 16 * u)
                        s_.copy(f_out[:, 2 * n:2 * n + 2, :], p_vd[n][:]).then_inc(down_kept, 1)

        @block.vector
        def _(dve):
            v = nc.vector
            st = Steps(dve, rope_steps)
            mask = [(j // HD) * HD + (j % HD + HD // 2) % HD for j in range(32)]

            def te(ap):
                return ap.rearrange("p (t e) -> p t e", e=E)

            def et(ap):
                return ap.rearrange("p (e t) -> p t e", e=E)

            def wide(ap):
                return ap.unsqueeze(2).broadcast_to([P, NT, E])

            lg, idx = te(keep["logits"][:]), te(idx_m[:])
            dve.wait_ge(rc_loaded, 16 * 5)
            best, second = pick[:, 0], pick[:, 1]
            st.link(v.tensor_reduce(best, lg, AX.X, ALU.max))
            below = te(rt[:, 0])
            st.link(v.tensor_tensor(below, lg, wide(best), ALU.subtract))

            def one_hot(out, values, top, scratch, low):
                st.link(v.tensor_tensor(scratch, values, wide(top), ALU.is_equal))
                st.link(v.tensor_tensor(scratch, scratch, idx, ALU.mult))
                st.link(v.tensor_reduce(low, scratch, AX.X, ALU.min))
                st.link(v.tensor_tensor(out, idx, wide(low), ALU.is_equal))

            hot1, hot2, scratch, rest = te(rt[:, 1]), te(rt[:, 2]), te(rt[:, 3]), te(rt[:, 4])
            one_hot(hot1, lg, best, scratch, pick[:, 2])
            st.link(v.scalar_tensor_tensor(out=rt[:, 4], in0=rt[:, 1], scalar=NEG, in1=rt[:, 0],
                                           op0=ALU.mult, op1=ALU.add))
            st.link(v.tensor_reduce(second, rest, AX.X, ALU.max))
            one_hot(hot2, rest, second, scratch, pick[:, 3])
            v.tensor_tensor(taken[:].rearrange("p (e t) -> p t e", e=E), hot1, hot2, ALU.add).then_inc(taken_ready, 1)
            dve.wait_ge(counted, 1)
            st.link(v.tensor_copy(rt[:, 5], p_u[:, 0:NT * E]))
            st.link(v.tensor_tensor_scan(rt[:, 6], runs[:], rt[:, 5], 0.0, ALU.mult, ALU.add))
            st.link(v.tensor_tensor(rt[:, 6], rt[:, 6], rt[:, 5], ALU.subtract))
            v.tensor_tensor(rt[:, 7], p_g[:, 0:NT * E], rt[:, 6], ALU.add).then_inc(counts_read, 1)
            dve.wait_ge(counts_read, 1)
            place, expert, kept, slot = pair[:, 0], pair[:, 1], pair[:, 2], pair[:, 3]
            for k, hot in enumerate((hot1, hot2)):
                st.link(v.tensor_tensor(scratch, hot, et(rt[:, 7]), ALU.mult))
                st.link(v.tensor_reduce(place[:, k], scratch, AX.X, ALU.add))
            st.link(v.tensor_scalar(expert, pick[:, 2:4], float(E), float(CAP), ALU.add, ALU.mult))
            st.link(v.tensor_scalar(kept, place, float(CAP), None, ALU.is_lt))
            st.link(v.tensor_scalar(slot, place, float(CAP - 1), None, ALU.min))
            st.link(v.tensor_tensor(slot, slot, expert, ALU.add))
            st.link(v.tensor_copy(keep["fetch"][:], slot))
            st.link(v.tensor_tensor(slot, slot, trash[:], ALU.subtract))
            st.link(v.tensor_tensor(slot, slot, kept, ALU.mult))
            st.link(v.tensor_tensor(slot, slot, trash[:], ALU.add))
            v.tensor_copy(send[:], slot).then_inc(send_ready, 1)
            st.link(v.tensor_tensor(keep["fits"][:], kept[:, 0], kept[:, 1], ALU.mult))
            st.link(v.tensor_copy(keep["second"][:], second))
            st.link(v.tensor_copy(keep["below"][:], rt[:, 0]))

            with dve.Fori(0, CPB) as i:
                st.enter(i, 2 * (2 * KD * 2))
                for u in range(2):
                    pos = bass.ds(i * CH, CH)

                    def rope(n):
                        dve.wait_ge(qf_ready, i * 8 + (4 * u + n + 1))
                        st.mark(v.tensor_tensor(with_cos[n % 2][:], qf[n % 2][:], cos[:, pos], ALU.mult))
                        v.stream_shuffle(turned[n % 2][:], qf[n % 2][:], mask).then_inc(qf_used, 1)
                        dve.wait_ge(qf_used, i * 8 + (4 * u + n + 1))
                        st.mark(v.tensor_tensor(with_sin[n % 2][:], turned[n % 2][:], sin[:, pos], ALU.mult))
                        st.wait()
                        dve.wait_ge(q_rest_ready, i * 8 + (4 * u + max(n - 1, 0)))
                        v.tensor_tensor(q[n % 2][:], with_cos[n % 2][:], with_sin[n % 2][:], ALU.add).then_inc(q_ready, 1)

                    def rest(n):
                        dve.wait_ge(q_part_ready[0], i * 8 + (4 * u + n + 1))
                        dve.wait_ge(q_part_ready[2], i * 8 + (4 * u + max(n - 1, 0)))
                        v.tensor_tensor(q_rest[n % 2][:], q[n % 2][:], q_part[0][n % 2][:],
                                        ALU.subtract).then_inc(q_rest_ready, 1)

                    def third(n):
                        dve.wait_ge(q_part_ready[1], i * 8 + (4 * u + n + 1))
                        dve.wait_ge(q_stored[2][n % 2], i * (16 * 4) + 16 * (2 * u + n // 2))
                        v.tensor_tensor(q_part[2][n % 2][:], q_rest[n % 2][:], q_part[1][n % 2][:],
                                        ALU.subtract).then_inc(q_part_ready[2], 1)

                    dve.wait_ge(gu_made, i * 2 + u)
                    for k in range(KD):
                        dve.wait_ge(fr_high, i * 4 + (2 * u + k + 1))
                        v.scalar_tensor_tensor(out=fr_l[:, k], in0=p_fr[:, k], scalar=fnorm[:, k:k + 1],
                                               in1=fr_h[:, k].bitcast(F32), op0=ALU.mult,
                                               op1=ALU.subtract).then_inc(fr_low, 1)
                    rope(0)
                    rope(1)
                    rest(0)
                    dve.wait_ge(gelu_ready, i * 2 + (u + 1))
                    dve.wait_ge(hid_low, i * 2 + u)
                    v.tensor_tensor(hid[:], p_u[:], gelu[:], ALU.mult).then_inc(hid_ready, 1)
                    rest(1)
                    rope(2)
                    third(0)
                    dve.wait_ge(hid_high, i * 2 + (u + 1))
                    dve.wait_ge(down_made, i * 4 + 2 * u)
                    v.tensor_tensor(hid_l[:], hid[:], hid_h[:].bitcast(F32), ALU.subtract).then_inc(hid_low, 1)
                    third(1)
                    rope(3)
                    rest(2)
                    rest(3)
                    third(2)
                    third(3)
            st.leave(CPB)

        @block.tensor
        def _(pe):
            t_ = nc.tensor
            pe.wait_ge(rc_loaded, 16 * 5)
            pe.wait_ge(taken_ready, 1)
            t_.matmul(p_g[:, 0:NT * E], tri[:], taken[:], start=True, stop=True)
            t_.matmul(p_u[:, 0:NT * E], ones_b[:], taken[:], start=True, stop=True).then_inc(counted, 1)
            pe.wait_ge(counts_read, 1)
            with pe.Fori(0, CPB) as i:
                for u in range(2):
                    xx = [(xh[u][:, k], xl[u][:, k]) for k in range(KD)]

                    def piece(n):
                        w, k = divmod(n, KD)
                        if n >= 2:
                            pe.wait_ge(qf_ready, i * 8 + (4 * u + n - 1))
                        else:
                            pe.wait_ge(qf_ready, i * 8 + 4 * u)
                        out = slice(k * P, (k + 1) * P)
                        for c in range(KD):
                            mm = three_products(t_, p_qk[n % 2][:], (wqkv_h[:, w, c, out], wqkv_l[:, w, c, out]),
                                                xx[c], c == 0, c == KD - 1)
                        mm.then_inc(qk_made, 1)

                    pe.wait_ge(x_in[u], i * 48 + 48)
                    pe.wait_ge(fr_low, i * 4 + 2 * u)
                    for k in range(KD):
                        for t in range(TC):
                            mm = t_.transpose(p_fr[:, k, t * P:(t + 1) * P], xr[u][:, t, k * P:(k + 1) * P], ident[:])
                    mm.then_inc(fr_turned, 1)
                    piece(0)
                    piece(1)
                    pe.wait_ge(fr_low, i * 4 + (2 * u + 2))
                    pe.wait_ge(hid_ready, i * 2 + u)
                    for m, out in enumerate((p_g, p_u)):
                        for c in range(KD):
                            mm = three_products(t_, out[:], (wf_h[:, m, c], wf_l[:, m, c]), (fr_h[:, c], fr_l[:, c]),
                                                c == 0, c == KD - 1)
                    mm.then_inc(gu_made, 1)
                    piece(2)
                    piece(3)
                    for n in range(2):
                        pe.wait_ge(down_kept, i * 4 + 2 * u)
                        for t in range(2):
                            tok = slice((2 * n + t) * P, (2 * n + t + 1) * P)
                            for c in range(KD):
                                three_products(t_, p_vd[n][:, t], (xx[c][0][:, tok], xx[c][1][:, tok]),
                                               (wqkv_h[:, 2, c], wqkv_l[:, 2, c]), c == 0, False)
                            t_.matmul(p_vd[n][:, t], ones_rowr[:], bv_h[:], start=False, stop=False)
                            mm = t_.matmul(p_vd[n][:, t], ones_rowr[:], bv_l[:], start=False, stop=True)
                        mm.then_inc(v_made, 1)
                    pe.wait_ge(hid_low, i * 2 + (u + 1))
                    for n in range(2):
                        pe.wait_ge(v_kept, i * 4 + (2 * u + n + 1))
                        for t in range(2):
                            tok = slice((2 * n + t) * P, (2 * n + t + 1) * P)
                            mm = three_products(t_, p_vd[n][:, t], (hid_h[:, tok], hid_l[:, tok]),
                                                (wfd_h[:], wfd_l[:]), True, True)
                        mm.then_inc(down_made, 1)


def run_experts(nc, a, keep):
    with ExitStack() as ctx:
        def sb(name, shape, dt=F32):
            return ctx.enter_context(nc.sbuf_tensor(name, shape, dt))

        def ps(name, shape, dt=F32):
            return ctx.enter_context(nc.psum_tensor(name, shape, dt))

        def sem(name):
            return ctx.enter_context(nc.semaphore(name))

        RT = CAP // P
        RC = CAP // CH
        WW = 2 * KD * F + KF * D
        ident = sb("ident2", [P, P])
        rows = [sb(f"rows{u}", [P, RT, D]) for u in range(2)]
        w = [sb(f"w{u}", [P, WW]) for u in range(2)]
        w_h = [sb(f"w_h{u}", [P, WW], F32R) for u in range(2)]
        w_l = [sb(f"w_l{u}", [P, WW], F32R) for u in range(2)]
        nw = [sb(f"nw{u}", [P, KD]) for u in range(2)]
        xt_h = [sb(f"xt_h{c}", [P, KD, CH], F32R) for c in range(RC)]
        xt_l = [sb(f"xt_l{c}", [P, KD, CH], F32R) for c in range(RC)]
        gelu = [sb(f"gelu_e{s}", [P, CH]) for s in range(2)]
        hid = [sb(f"hid_e{s}", [P, CH]) for s in range(2)]
        hid_h = [sb(f"hid_eh{c}", [P, KF, CH], F32R) for c in range(RC)]
        hid_l = [sb(f"hid_el{c}", [P, KF, CH], F32R) for c in range(RC)]
        e_out = sb("e_out", [P, RT, D])

        p_t = ps("p_t", [P, KD, CH])
        p_g = [ps(f"p_eg{s}", [P, CH]) for s in range(2)]
        p_u = [ps(f"p_eu{s}", [P, CH]) for s in range(2)]
        p_d = [ps(f"p_d{s}", [P, 2, D]) for s in range(2)]

        id_loaded = sem("id_loaded")
        rows_loaded = [sem(f"rows_loaded{u}") for u in range(2)]
        w_loaded = [sem(f"w_loaded_e{u}") for u in range(2)]
        w_high = sem("w_high_e")
        w_low = sem("w_low_e")
        turned = sem("turned_e")
        xt_high = sem("xt_high_e")
        xt_low = sem("xt_low_e")
        gu_made = sem("gu_made_e")
        gelu_ready = sem("gelu_ready_e")
        hid_ready = sem("hid_ready_e")
        hid_high = sem("hid_high_e")
        hid_low = sem("hid_low_e")
        down_made = sem("down_made_e")
        down_kept = sem("down_kept_e")
        out_stored = sem("out_stored_e")
        block = ctx.enter_context(nc.Block())

        GU, DN = RC * KF, RT // 2

        def count(i, e, per, k):
            return i * (2 * per) + (e * per + k)

        def pairs(eng, pair):
            with eng.Fori(0, E // 2 - 1) as i:
                pair(i, E)
            pair(E // 2 - 1, 2)

        @block.sync
        def _(sp):
            sp.dma_start(ident[:], a["ident"]).then_inc(id_loaded, 16)

            def load(i, n, u):
                e = i * 2 + n
                sp.dma_start(rows[u][:], a["xb"][bass.ds(i * (2 * CAP) + n * CAP, CAP), :].rearrange("(t p) d -> p t d", p=P)
                             ).then_inc(rows_loaded[u], 16)
                sp.dma_start(nw[u][:], a["normw"][bass.ds(e, 1)].rearrange("e p k -> p (e k)")
                             ).then_inc(rows_loaded[u], 16)
                for n, name in enumerate(("wg", "wu")):
                    sp.dma_start(w[u][:, n * KD * F:(n + 1) * KD * F].rearrange("p (k f) -> p k f", k=KD),
                                 a[name][bass.ds(e, 1)].rearrange("e (k p) f -> p (e k) f", p=P)
                                 ).then_inc(w_loaded[u], 16)
                sp.dma_start(w[u][:, 2 * KD * F:].rearrange("p (k d) -> p k d", k=KF),
                             a["wd"][bass.ds(e, 1)].rearrange("e (k p) d -> p (e k) d", p=P)
                             ).then_inc(w_loaded[u], 16)

            load(0, 0, 0)
            load(0, 1, 1)

            def pair(i, left):
                for u in range(2):
                    if u + 2 < left:
                        sp.wait_ge(xt_low, count(i, u, RC, RC))
                        sp.wait_ge(w_low, count(i, u, 1, 1))
                        load(i, u + 2, u)
                    sp.wait_ge(down_kept, count(i, u, DN, DN))
                    sp.dma_start(a["ob"][bass.ds(i * (2 * CAP) + u * CAP, CAP), :].rearrange("(t p) d -> p t d", p=P),
                                 e_out[:]).then_inc(out_stored, 16)

            pairs(sp, pair)
            sp.wait_ge(out_stored, 16 * E)

        @block.gpsimd
        def _(pool):
            with pool.Fori(0, E // 2) as i:
                for u in range(2):
                    pool.wait_ge(w_high, count(i, u, 1, 1))
                    nc.gpsimd.tensor_tensor(w_l[u][:], w[u][:], w_h[u][:].bitcast(F32), ALU.subtract).then_inc(w_low, 1)

        @block.scalar
        def _(act):
            s_ = nc.scalar

            def rows_high(i, e, c):
                act.wait_ge(turned, count(i, e, RC, c + 1))
                act.wait_ge(gu_made, count(i, e, GU, 0))
                for k in range(KD):
                    s_.activation(xt_h[c][:, k], p_t[:, k], ACT.Identity, scale=nw[e % 2][:, k:k + 1]).then_inc(xt_high, 1)

            for u in range(2):
                act.wait_ge(w_loaded[u], 48)
                s_.copy(w_h[u][:], w[u][:]).then_inc(w_high, 1)
            for c in range(RC):
                rows_high(0, 0, c)

            def pair(i, left):
                for u in range(2):
                    for n in range(GU + 1):
                        if n < GU:
                            act.wait_ge(gu_made, count(i, u, GU, n + 1))
                            act.wait_ge(hid_ready, count(i, u, GU, max(n - 1, 0)))
                            s_.activation(gelu[n % 2][:], p_g[n % 2][:], ACT.Gelu).then_inc(gelu_ready, 1)
                        if n:
                            c, f = divmod(n - 1, KF)
                            act.wait_ge(hid_ready, count(i, u, GU, n))
                            act.wait_ge(down_made, count(i, u, DN, 0))
                            s_.copy(hid_h[c][:, f], hid[(n - 1) % 2][:]).then_inc(hid_high, 1)
                    for n in range(DN):
                        if n % 2 == 0 and u + 1 < left:
                            rows_high(i, u + 1, n // 2)
                        act.wait_ge(down_made, count(i, u, DN, n + 1))
                        act.wait_ge(out_stored, count(i, u, 16, 0))
                        s_.copy(e_out[:, 2 * n:2 * n + 2, :], p_d[n % 2][:]).then_inc(down_kept, 1)
                    if u + 2 < left:
                        act.wait_ge(w_loaded[u], i * 48 + 96)
                        s_.copy(w_h[u][:], w[u][:]).then_inc(w_high, 1)

            pairs(act, pair)

        @block.vector
        def _(dve):
            v = nc.vector

            def rows_low(i, e, c):
                dve.wait_ge(xt_high, count(i, e, 2 * RC, 2 * c + 2))
                for k in range(KD):
                    ins = v.scalar_tensor_tensor(out=xt_l[c][:, k], in0=p_t[:, k], scalar=nw[e % 2][:, k:k + 1],
                                                 in1=xt_h[c][:, k].bitcast(F32), op0=ALU.mult, op1=ALU.subtract)
                ins.then_inc(xt_low, 1)

            for c in range(RC):
                rows_low(0, 0, c)

            def pair(i, left):
                for u in range(2):
                    for n in range(GU + 1):
                        if n < GU:
                            dve.wait_ge(gelu_ready, count(i, u, GU, n + 1))
                            dve.wait_ge(hid_low, count(i, u, GU, max(n - 1, 0)))
                            v.tensor_tensor(hid[n % 2][:], p_u[n % 2][:], gelu[n % 2][:], ALU.mult).then_inc(hid_ready, 1)
                        if n:
                            c, f = divmod(n - 1, KF)
                            dve.wait_ge(hid_high, count(i, u, GU, n))
                            v.tensor_tensor(hid_l[c][:, f], hid[(n - 1) % 2][:], hid_h[c][:, f].bitcast(F32),
                                            ALU.subtract).then_inc(hid_low, 1)
                    if u + 1 < left:
                        for c in range(RC):
                            rows_low(i, u + 1, c)

            pairs(dve, pair)

        @block.tensor
        def _(pe):
            t_ = nc.tensor

            def turn(i, e, c):
                if c == 0:
                    pe.wait_ge(rows_loaded[e % 2], i * 32 + 32 * (e // 2 + 1))
                pe.wait_ge(xt_low, count(i, e, RC, c))
                for k in range(KD):
                    for t in range(TC):
                        mm = t_.transpose(p_t[:, k, t * P:(t + 1) * P], rows[e % 2][:, c * TC + t, k * P:(k + 1) * P], ident[:])
                mm.then_inc(turned, 1)

            pe.wait_ge(id_loaded, 16)
            for c in range(RC):
                turn(0, 0, c)

            def pair(i, left):
                for u in range(2):
                    wg = [(w_h[u][:, k * F:(k + 1) * F], w_l[u][:, k * F:(k + 1) * F]) for k in range(2 * KD)]
                    wd = [(w_h[u][:, 2 * KD * F + k * D:2 * KD * F + (k + 1) * D],
                           w_l[u][:, 2 * KD * F + k * D:2 * KD * F + (k + 1) * D]) for k in range(KF)]
                    pe.wait_ge(w_low, count(i, u, 1, 1))
                    for n in range(GU):
                        c, f = divmod(n, KF)
                        if f == 0:
                            pe.wait_ge(xt_low, count(i, u, RC, c + 1))
                        pe.wait_ge(hid_ready, count(i, u, GU, max(n - 1, 0)))
                        for m, out in enumerate((p_g, p_u)):
                            for k in range(KD):
                                mm = three_products(
                                    t_, out[n % 2][:], tuple(x[:, f * P:(f + 1) * P] for x in wg[m * KD + k]),
                                    (xt_h[c][:, k], xt_l[c][:, k]), k == 0, k == KD - 1)
                        mm.then_inc(gu_made, 1)
                    for n in range(DN):
                        if n % 2 == 0 and u + 1 < left:
                            turn(i, u + 1, n // 2)
                        c, t0 = divmod(2 * n, TC)
                        pe.wait_ge(hid_low, count(i, u, GU, KF * (c + 1)))
                        pe.wait_ge(down_kept, count(i, u, DN, max(n - 1, 0)))
                        for t in range(2):
                            tok = slice((t0 + t) * P, (t0 + t + 1) * P)
                            for k in range(KF):
                                mm = three_products(t_, p_d[n % 2][:, t], (hid_h[c][:, k, tok], hid_l[c][:, k, tok]),
                                                    wd[k], k == 0, k == KF - 1)
                        mm.then_inc(down_made, 1)

            pairs(pe, pair)


def attend(nc, a, keep):
    with ExitStack() as ctx:
        def sb(name, shape, dt=F32):
            return ctx.enter_context(nc.sbuf_tensor(name, shape, dt))

        def ps(name, shape, dt=F32):
            return ctx.enter_context(nc.psum_tensor(name, shape, dt))

        def sem(name):
            return ctx.enter_context(nc.semaphore(name))

        PAIRS = ((0, 0), (0, 1), (0, 2), (1, 0), (1, 1), (2, 0))
        KS = len(PAIRS) * HD
        KM = KS + 2
        R = 2 * HD
        LAG = 20
        STEPS = [(j, i) for j in range(CPB) for i in range(TC * (j + 1))]
        MAXES = [(j, TC * j + r, c) for j in range(CPB) for r in range(TC) for c in range(j + 1)]
        S = len(STEPS)
        assert S == len(MAXES)
        ENDS = [n for n in range(S) if n == S - 1 or MAXES[n + 1][0] != MAXES[n][0]]
        assert ENDS == [n for n in range(S) if n == S - 1 or STEPS[n + 1][0] != STEPS[n][0]]
        HEAD_TURNS = sum(e + 1 < LAG for e in ENDS)
        HEAD_UNITS = HG * LAG + HEAD_TURNS
        UNITS = HG * S + CPB
        assert HEAD_UNITS % 2 == 0 and UNITS % 2 == 0

        qs = [sb(f"qs{b}", [KM, HG, T], BF16) for b in range(B)]
        ks = [sb(f"ks{b}", [KM, HG, T], BF16) for b in range(B)]
        vs = [sb(f"vs{b}", [P, T // P, HG * R]) for b in range(B)]
        probs = [sb(f"probs{r}", [P, HG, CH]) for r in range(3)]
        tops = [sb(f"tops{r}", [P, HG, TC, CPB]) for r in range(2)]
        neg_top = [sb(f"neg_top{r}", [P, P]) for r in range(2)]
        top_part = [[sb(f"top_part{m}{r}", [HG * TC, P], BF16) for r in range(2)] for m in range(2)]
        ident_f = sb("ident_f", [P, P])
        ident_b = sb("ident_b", [P, P], BF16)
        hide_q = sb("hide_q", [P, P], BF16)
        hide_k = sb("hide_k", [P, P], BF16)
        first_col = sb("first_col", [P, 1])
        sums = sb("sums", [P, CH])
        inv_sums = sb("inv_sums", [P, CH])
        y = [sb(f"y{r}", [P, CH]) for r in range(2)]
        x_all, mix = keep["x"], keep["mix"]
        ex = sb("ex", [P, NT * E])
        ex2 = sb("ex2", [P, NT])
        cw = sb("cw", [P, 6, NT])
        got = [[sb(f"got{k}{r}", [P, D]) for r in range(2)] for k in range(2)]
        fall = [sb(f"fall{r}", [P, D]) for r in range(2)]
        part = [sb(f"part{n}", [P, D]) for n in range(3)]

        p_s = [ps(f"p_s{r}", [P, 2, CH]) for r in range(2)]
        p_m = [ps(f"p_m{r}", [P, CH]) for r in range(2)]
        p_y = [ps(f"p_y{r}", [P, CH]) for r in range(2)]

        c_loaded = sem("c_loaded")
        rows_set = sem("rows_set")
        in_loaded = [sem(f"in_loaded{b}") for b in range(B)]
        x_loaded = sem("x_loaded_c")
        max_made = sem("max_made")
        max_read = sem("max_read")
        neg_ready = sem("neg_ready")
        top_stored = [sem(f"top_stored{j}") for j in range(CPB)]
        s_made = sem("s_made")
        p_ready = sem("p_ready")
        pv_done = sem("pv_done")
        y_steps = sem("y_steps")
        y_ready = sem("y_ready")
        y_stored = [sem(f"y_stored{r}") for r in range(2)]
        exps = sem("exps")
        cw_steps = sem("cw_steps")
        got_in = [[sem(f"got_in{k}{r}") for r in range(2)] for k in range(2)]
        fall_in = [sem(f"fall_in{r}") for r in range(2)]
        mix_steps = sem("mix_steps")
        block = ctx.enter_context(nc.Block())

        LOADS = 2 * len(PAIRS) + 1

        def count(i, b, per, k, head=0):
            return i * (2 * per) + (head + b * per + k)

        def groups(eng, group):
            with eng.Fori(0, NG - 1) as i:
                for b in range(B):
                    group(i, b, True)
            for b in range(B):
                group(NG - 1, b, b == 0)

        def lead(follows):
            for s in range(S):
                n = s + LAG
                if n < S:
                    yield s, n, True
                elif follows:
                    yield s, n - S, False
                else:
                    yield s, (S if n == S else None), True

        def turns_at(n, own):
            return (n - 1) % S in ENDS and (n > 0 or not own)

        head_turn, group_turn, unit_now = {}, {}, 0
        for n in range(LAG):
            unit_now += HG
            if n - 1 in ENDS:
                unit_now += 1
                head_turn[MAXES[n - 1][0]] = unit_now
        unit_now = 0
        for s, n, own in lead(True):
            unit_now += HG
            if turns_at(n, own):
                unit_now += 1
                group_turn[MAXES[(n - 1) % S][0]] = unit_now
        TOPS = 16 * 2 * HG

        @block.sync
        def _(sp):
            for dst, src in ((ident_f, "ident"), (ident_b, "ident_b"), (hide_q, "hide_after_row"),
                             (hide_k, "hide_before_row")):
                sp.dma_start(dst[:], a[src]).then_inc(c_loaded, 16)

            def load(i, hg, b):
                for w, dst in enumerate((qs[b], ks[b])):
                    for n, pair in enumerate(PAIRS):
                        src = a[f"qk{pair[w]}"][w].rearrange("k p n -> (k p) n")
                        sp.dma_start(dst[n * HD:(n + 1) * HD],
                                     src[bass.ds(i * (HG * HD) + hg * (HG * HD), HG * HD), b * T:(b + 1) * T]
                                     .rearrange("(h d) n -> d h n", d=HD)).then_inc(in_loaded[b], 16)
                sp.dma_start(vs[b][:], a["v"][b * T:(b + 1) * T, bass.ds(i * (HG * R) + hg * (HG * R), HG * R)]
                             .rearrange("(t p) c -> p t c", p=P)).then_inc(in_loaded[b], 16)

            def tops_in(b, j, value):
                sp.wait_ge(max_read, value)
                for m in range(2):
                    for h in range(HG):
                        sp.dma_start(qs[b][KS + m:KS + m + 1, h, j * CH:(j + 1) * CH]
                                     .rearrange("o (t n) -> o t n", t=TC),
                                     top_part[m][j % 2][h * TC:(h + 1) * TC, :]).then_inc(top_stored[j], 16)

            def y_out(i, b, j):
                sp.wait_ge(y_ready, count(i, b, CPB, j + 1))
                for h in reversed(range(HG)):
                    sp.dma_start(a["yt"][bass.ds(i * (HG * HD) + h * HD, HD), b * T + j * CH:b * T + (j + 1) * CH],
                                 y[j % 2][h * R:h * R + HD, :]).then_inc(y_stored[j % 2], 16)

            load(0, 0, 0)
            sp.dma_start(x_all[:], a["x"].rearrange("(t p) d -> p t d", p=P)).then_inc(x_loaded, 16)
            tops_in(0, 0, head_turn[0])
            tops_in(0, 1, head_turn[1])

            def group(i, b, follows):
                if follows:
                    sp.wait_ge(pv_done, count(i, b, S, 0))
                    load(i, b, 1 - b)
                tops_in(b, 2, count(i, b, UNITS, group_turn[2], HEAD_UNITS))
                y_out(i, b, 0)
                y_out(i, b, 1)
                tops_in(b, 3, count(i, b, UNITS, group_turn[3] - (0 if follows else HG), HEAD_UNITS))
                if follows:
                    tops_in(1 - b, 0, count(i, b, UNITS, group_turn[0], HEAD_UNITS))
                y_out(i, b, 2)
                if follows:
                    tops_in(1 - b, 1, count(i, b, UNITS, group_turn[1], HEAD_UNITS))
                y_out(i, b, 3)

            groups(sp, group)
            for r in range(2):
                sp.wait_ge(y_stored[r], 16 * HG * (CPB // 2) * B * NG)

        @block.gpsimd
        def _(pool):
            for n, (rows, what) in enumerate([(ks[b][KS:KM], 1.0) for b in range(B)] + [(t[:], 0.0) for t in neg_top]):
                nc.gpsimd.memset(rows, what).then_inc(rows_set, 1)
                pool.wait_ge(rows_set, n + 1)
            st = Steps(pool, mix_steps)
            fd = a["fd"].rearrange("(t p) d -> t p d", p=P)

            def fetch(t):
                for k in range(2):
                    nc.gpsimd.indirect_dma_start(
                        got[k][t % 2][:], None, a["ob"],
                        bass.IndirectOffsetOnAxis(ap=keep["fetch"][:, k, t:t + 1], axis=0)).then_inc(got_in[k][t % 2], 16)
                nc.gpsimd.dma_start(fall[t % 2][:], fd[t]).then_inc(fall_in[t % 2], 16)

            fetch(0)
            pool.wait_ge(x_loaded, 16)
            pool.wait_ge(cw_steps, 9)
            g = nc.gpsimd
            for t in range(NT):
                if t + 1 < NT:
                    fetch(t + 1)
                st.mark(g.tensor_scalar(mix[:, t], x_all[:, t], keep["mean"][:, t:t + 1], cw[:, 5, t:t + 1],
                                        ALU.subtract, ALU.mult))
                for k in range(2):
                    pool.wait_ge(got_in[k][t % 2], 16 * (t // 2 + 1))
                    st.mark(g.tensor_scalar(part[k][:], got[k][t % 2][:], cw[:, 2 + k, t:t + 1], None, ALU.mult))
                pool.wait_ge(fall_in[t % 2], 16 * (t // 2 + 1))
                st.link(g.tensor_scalar(part[2][:], fall[t % 2][:], cw[:, 4, t:t + 1], None, ALU.mult))
                st.mark(g.tensor_tensor(part[0][:], part[0][:], part[1][:], ALU.add))
                st.link(g.tensor_tensor(mix[:, t], mix[:, t], part[2][:], ALU.add))
                st.link(g.tensor_tensor(mix[:, t], mix[:, t], part[0][:], ALU.add))

        @block.scalar
        def _(act):
            s_ = nc.scalar
            s_.activation(ex[:], keep["below"][:], ACT.Exp).then_inc(exps, 1)
            s_.activation(ex2[:], keep["second"][:], ACT.Exp).then_inc(exps, 1)

            def group(i, b, follows):
                for s, (j, k) in enumerate(STEPS):
                    w = CH - P * max(k - TC * j, 0)
                    act.wait_ge(pv_done, count(i, b, S, max(s - 2, 0)))
                    for r in range(2):
                        act.wait_ge(s_made, count(i, b, 2 * S, 2 * s + r + 1))
                        s_.activation(probs[s % 3][:, 2 * r:2 * r + 2, 0:w], p_s[r][:, :, 0:w], ACT.Exp).then_inc(p_ready, 1)

            groups(act, group)

        @block.vector
        def _(dve):
            v = nc.vector
            cs = Steps(dve, cw_steps)
            dve.wait_ge(exps, 2)
            z, inv, w1, w2, over, scale = (cw[:, n] for n in range(6))
            cs.link(v.tensor_reduce(z, ex[:].rearrange("p (t e) -> p t e", e=E), AX.X, ALU.add))
            cs.link(v.reciprocal(inv, z))
            cs.link(v.tensor_tensor(inv, inv, keep["fits"][:], ALU.mult))
            cs.link(v.tensor_copy(w1, inv))
            cs.link(v.tensor_tensor(w2, inv, ex2[:], ALU.mult))
            cs.link(v.tensor_scalar(over, keep["fits"][:], -1.0, 1.0, ALU.mult, ALU.add))
            cs.link(v.tensor_tensor(scale, w1, w2, ALU.add))
            cs.link(v.tensor_scalar(scale, scale, 1.0, None, ALU.add))
            cs.link(v.tensor_tensor(scale, scale, keep["rstd"][:], ALU.mult))

            mask = [HD + j % HD for j in range(32)]
            ys = Steps(dve, y_steps)
            unit = [0]

            def value(i, b, k):
                return k if i is None else count(i, b, UNITS, k, HEAD_UNITS)

            def reduce(i, b, n):
                j, t, c = MAXES[n]
                w = min(CH, (t + 1) * P - c * CH)
                for h in range(HG):
                    dve.wait_ge(max_made, value(i, b, unit[0] + 1))
                    v.tensor_reduce(tops[j % 2][:, h, t % TC, c:c + 1], p_m[unit[0] % 2][:, 0:w], AX.X, ALU.max
                                    ).then_inc(max_read, 1)
                    unit[0] += 1
                if n in ENDS:
                    dve.wait_ge(max_read, value(i, b, unit[0]))
                    v.tensor_reduce(neg_top[j % 2][:, 0:HG * TC], tops[j % 2][:, :, :, 0:j + 1].rearrange(
                        "p h t c -> p (h t) c"), AX.X, ALU.max, negate=True).then_inc(neg_ready, 1)

            def turn(i, b, j):
                dve.wait_ge(max_made, value(i, b, unit[0] + 1))
                if i is not None:
                    dve.wait_ge(top_stored[(j - 2) % CPB], count(i, b, TOPS, TOPS))
                top = p_m[unit[0] % 2][0:HG * TC, 0:P]
                ys.link(v.tensor_copy(top_part[0][j % 2][:], top))
                v.tensor_tensor(top_part[1][j % 2][:], top, top_part[0][j % 2][:], ALU.subtract).then_inc(max_read, 1)
                unit[0] += 1

            def finish_y(i, b, j):
                e = ENDS[j]
                dve.wait_ge(pv_done, count(i, b, S, e + 1))
                dve.wait_ge(y_stored[j % 2], i * (16 * HG * CPB // 2 * B) + 16 * HG * (b * CPB // 2 + j // 2))
                ys.mark(v.tensor_copy(first_col[:], p_y[j % 2][:, 0:1]))
                ys.link(v.stream_shuffle(sums[:], p_y[j % 2][:], mask))
                ys.link(v.reciprocal(inv_sums[:], sums[:]))
                v.tensor_tensor(y[j % 2][:], p_y[j % 2][:], inv_sums[:], ALU.mult).then_inc(y_ready, 1)

            for n in range(LAG):
                reduce(None, 0, n)
                if n - 1 in ENDS:
                    turn(None, 0, MAXES[n - 1][0])

            def group(i, b, follows):
                unit[0] = 0
                for s, n, own in lead(follows):
                    if n is not None:
                        if n < S:
                            reduce(i, b, n)
                        if turns_at(n, own):
                            turn(i, b, MAXES[(n - 1) % S][0])
                    if s - 3 in ENDS:
                        finish_y(i, b, STEPS[s - 3][0])
                finish_y(i, b, CPB - 1)

            with dve.Fori(0, NG - 1) as i:
                ys.enter(i, B * CPB * 4)
                for b in range(B):
                    group(i, b, True)
            ys.leave(NG - 1)
            for b in range(B):
                group(NG - 1, b, b == 0)

        @block.tensor
        def _(pe):
            t_ = nc.tensor
            unit = [0]

            def value(i, b, k):
                return k if i is None else count(i, b, UNITS, k, HEAD_UNITS)

            def bank_free(i, b):
                if i is not None or unit[0] >= 2:
                    pe.wait_ge(max_read, value(i, b, unit[0] - 1))

            def maxima(i, b, n, bb):
                j, t, c = MAXES[n]
                w = min(CH, (t + 1) * P - c * CH)
                diagonal = c == j
                for h in range(HG):
                    bank_free(i, b)
                    out = p_m[unit[0] % 2]
                    mm = t_.matmul(out[:, 0:w], qs[bb][0:KS, h, t * P:(t + 1) * P], ks[bb][0:KS, h, c * CH:c * CH + w],
                                   start=True, stop=not diagonal)
                    if diagonal:
                        mm = t_.matmul(out[:, w - P:w], ident_b[:], hide_q[:], start=False, stop=True)
                    mm.then_inc(max_made, 1)
                    unit[0] += 1

            def turn(i, b, j, nth):
                bank_free(i, b)
                pe.wait_ge(neg_ready, nth)
                t_.transpose(p_m[unit[0] % 2][:, 0:P], neg_top[j % 2][:], ident_f[:]).then_inc(max_made, 1)
                unit[0] += 1

            def scores(i, b, s):
                j, k = STEPS[s]
                skip = P * max(k - TC * j, 0)
                diagonal = k >= TC * j
                for r in range(2):
                    pe.wait_ge(p_ready, count(i, b, 2 * S, 2 * (s - 1) + r + 1) if b or s else i * (4 * S))
                    for hh in range(2):
                        h = 2 * r + hh
                        mm = t_.matmul(p_s[r][:, hh, 0:CH - skip], ks[b][:, h, k * P:(k + 1) * P],
                                       qs[b][:, h, j * CH + skip:(j + 1) * CH], start=True, stop=not diagonal)
                        if diagonal:
                            mm = t_.matmul(p_s[r][:, hh, 0:P], ident_b[:], hide_k[:], start=False, stop=True)
                    mm.then_inc(s_made, 1)

            def values(i, b, s):
                j, k = STEPS[s]
                skip = P * max(k - TC * j, 0)
                pe.wait_ge(p_ready, count(i, b, 2 * S, 2 * s + 2))
                if k == 0:
                    pe.wait_ge(y_ready, count(i, b, CPB, j - 1) if b or j else i * (2 * CPB))
                for h in range(HG):
                    mm = t_.matmul(p_y[j % 2][h * R:(h + 1) * R, skip:CH], vs[b][:, k, h * R:(h + 1) * R],
                                   probs[s % 3][:, h, 0:CH - skip], start=(k == 0), stop=(s in ENDS))
                mm.then_inc(pv_done, 1)

            pe.wait_ge(c_loaded, 16 * 4)
            pe.wait_ge(rows_set, 4)
            pe.wait_ge(in_loaded[0], 16 * LOADS)
            for n in range(LAG):
                maxima(None, 0, n, 0)
                if n - 1 in ENDS:
                    turn(None, 0, MAXES[n - 1][0], MAXES[n - 1][0] + 1)

            def group(i, b, follows):
                unit[0] = 0
                for s, n, own in lead(follows):
                    if n is not None:
                        bb = b if own else 1 - b
                        if n == 0:
                            pe.wait_ge(in_loaded[bb], i * (16 * LOADS) + 16 * LOADS * (b + 1 if bb == 0 else 1))
                        if n < S:
                            maxima(i, b, n, bb)
                        if turns_at(n, own):
                            j = MAXES[(n - 1) % S][0]
                            turn(i, b, j, count(i, b, CPB, {2: 1, 3: 2, 0: 3, 1: 4}[j], HEAD_TURNS))
                    if STEPS[s][1] == 0:
                        pe.wait_ge(top_stored[STEPS[s][0]], count(i, b, TOPS, TOPS))
                    scores(i, b, s)
                    if s >= 2:
                        values(i, b, s - 2)
                values(i, b, S - 2)
                values(i, b, S - 1)

            groups(pe, group)


def finish(nc, a, keep):
    with ExitStack() as ctx:
        def sb(name, shape, dt=F32):
            return ctx.enter_context(nc.sbuf_tensor(name, shape, dt))

        def sem(name):
            return ctx.enter_context(nc.semaphore(name))

        TB = 4
        wo = sb("wo", [P, KD, D])
        bo = sb("bo", [1, D])
        ones = sb("ones_f", [1, P])
        yt = sb("yt_in", [P, KD, N])
        gate = [sb(f"gate{r}", [P, TB, D]) for r in range(2)]
        x_all, mix = keep["x"], keep["mix"]
        p_o = [ctx.enter_context(nc.psum_tensor(f"p_o{r}", [P, TB, D], F32)) for r in range(2)]

        w_in = sem("w_in")
        yt_in = [sem(f"yt_in{n}") for n in range(2)]
        ones_set = sem("ones_set_f")
        gate_ready = sem("gate_ready")
        proj_made = sem("proj_made")
        scaled = sem("scaled")
        summed = sem("summed")
        out_stored = sem("out_stored_f")
        block = ctx.enter_context(nc.Block())
        NS = NT // TB

        @block.sync
        def _(sp):
            sp.dma_start(wo[:], a["woT"].rearrange("(k p) o -> p k o", p=P)).then_inc(w_in, 16)
            sp.dma_start(bo[:], a["bo"]).then_inc(w_in, 16)
            for n in range(2):
                sp.dma_start(yt[:, :, n * N // 2:(n + 1) * N // 2],
                             a["yt"][:, n * N // 2:(n + 1) * N // 2].rearrange("(k p) n -> p k n", p=P)).then_inc(yt_in[n], 16)
            for s in range(NS):
                sp.wait_ge(summed, s + 1)
                sp.dma_start(a["out"][s * TB * P:(s + 1) * TB * P].rearrange("(t p) d -> p t d", p=P),
                             mix[:, s * TB:(s + 1) * TB]).then_inc(out_stored, 16)
            sp.wait_ge(out_stored, 16 * NS)

        @block.tensor
        def _(pe):
            t_ = nc.tensor
            pe.wait_ge(w_in, 32)
            pe.wait_ge(ones_set, 1)
            for s in range(NS):
                if s % (NS // 2) == 0:
                    pe.wait_ge(yt_in[s // (NS // 2)], 16)
                if s >= 2:
                    pe.wait_ge(scaled, s - 1)
                for t in range(TB):
                    tile = s * TB + t
                    for k in range(KD):
                        t_.matmul(p_o[s % 2][:, t], yt[:, k, tile * P:(tile + 1) * P], wo[:, k], start=(k == 0), stop=False)
                    mm = t_.matmul(p_o[s % 2][:, t], ones[:], bo[:], start=False, stop=True)
                mm.then_inc(proj_made, 1)

        @block.scalar
        def _(act):
            for s in range(NS):
                cur = slice(s * TB, (s + 1) * TB)
                if s >= 2:
                    act.wait_ge(scaled, s - 1)
                nc.scalar.activation(gate[s % 2][:], mix[:, cur], ACT.Silu).then_inc(gate_ready, 1)

        @block.vector
        def _(dve):
            v = nc.vector
            v.memset(ones[:], 1.0).then_inc(ones_set, 1)
            for s in range(NS):
                cur = slice(s * TB, (s + 1) * TB)
                dve.wait_ge(gate_ready, s + 1)
                dve.wait_ge(proj_made, s + 1)
                v.tensor_tensor(mix[:, cur], p_o[s % 2][:], gate[s % 2][:], ALU.mult).then_inc(scaled, 1)

        @block.gpsimd
        def _(pool):
            for s in range(NS):
                cur = slice(s * TB, (s + 1) * TB)
                pool.wait_ge(scaled, s + 1)
                nc.gpsimd.tensor_tensor(mix[:, cur], mix[:, cur], x_all[:, cur], ALU.add).then_inc(summed, 1)


def build(nc, a):
    with ExitStack() as ctx:
        def sb(name, shape, dt=F32):
            return ctx.enter_context(nc.sbuf_tensor(name, shape, dt))

        keep = {
            "logits": sb("logits", [P, NT * E]), "below": sb("below", [P, NT * E]),
            "mean": sb("mean", [P, NT]), "rstd": sb("rstd", [P, NT]), "second": sb("second", [P, NT]),
            "fits": sb("fits", [P, NT]), "fetch": sb("fetch", [P, 2, NT], I32),
        }
        normalise_route_project(nc, a, keep)
        run_experts(nc, a, keep)
        keep["x"], keep["mix"] = sb("x_kept", [P, NT, D]), sb("mix", [P, NT, D])
        attend(nc, a, keep)
        finish(nc, a, keep)


SCRATCH = {
    "xth": (P, KD, N), "xtl": (P, KD, N), "qk0": (2, KD, P, N), "qk1": (2, KD, P, N), "qk2": (2, KD, P, N),
    "v": (N, H * 2 * HD), "fd": (N, D), "xb": (2 * SLOTS, D), "ob": (SLOTS, D), "yt": (D, N),
}


def tables():
    import numpy as np
    theta = (1.0 / np.float32(10000.0) ** (np.arange(0, HD, 2, dtype=np.float32) / np.float32(HD))).astype(np.float32)
    angle = np.arange(1, T + 1, dtype=np.float32)[None, :] * np.tile(theta, P // (HD // 2))[:, None]
    sign = np.where(np.arange(P) % HD < HD // 2, -1.0, 1.0).astype(np.float32)
    row, col = np.arange(P)[:, None], np.arange(P)[None, :]
    bf16 = mybir.dt.np(BF16)
    tok = np.arange(NT)[None, None, :] * P + np.arange(P)[:, None, None]
    return {
        "cos": np.cos(angle).astype(np.float32), "sin": (np.sin(angle) * sign[:, None]).astype(np.float32),
        "ident": np.eye(P, dtype=np.float32), "ident_b": np.eye(P).astype(bf16),
        "tri": (row < col).astype(bf16), "ones_b": np.ones((P, P), bf16),
        "hide_after_row": np.where(col > row, NEG, 0.0).astype(bf16),
        "hide_before_row": np.where(col < row, NEG, 0.0).astype(bf16),
        "idx_m": np.tile(np.arange(E, dtype=np.float32) - E, (P, NT)),
        "runs": np.tile((np.arange(NT * E) % NT != 0).astype(np.float32), (P, 1)),
        "trash": (SLOTS + 2 * tok + np.arange(2)[None, :, None]).astype(np.float32),
    }


def laid_out(i):
    import numpy as np
    c = np.ascontiguousarray
    i = {k: np.asarray(v) for k, v in i.items()}
    col = lambda v: c(v.reshape(KD, P).T)
    return {
        "x": c(i["L0_attn_x"].reshape(N, D)),
        "wqT": c(i["L0_attn_Wq"].T), "wkT": c(i["L0_attn_Wk"].T), "wvT": c(i["L0_attn_Wv"].T), "woT": c(i["L0_attn_Wo"].T),
        "bq": col(i["L0_attn_bq"]), "bk": col(i["L0_attn_bk"]),
        "bv": c(i["L0_attn_bv"][None, :]), "bo": c(i["L0_attn_bo"][None, :]),
        "wr": i["L0_ffn_Wr"], "normw": c(i["L0_ffn_norm_w"].reshape(E, KD, P).transpose(0, 2, 1)),
        "wg": i["L0_ffn_Wg"], "wu": i["L0_ffn_Wu"], "wd": i["L0_ffn_Wd"],
        "fnorm": col(i["L0_ffn_f_norm"]), "fwg": i["L0_ffn_fWg"], "fwu": i["L0_ffn_fWu"], "fwd": i["L0_ffn_fWd"],
    }


def kernel(**inputs):
    import numpy as np
    import concourse.bacc as bacc
    from concourse.bass_utils import run_bass_kernel_spmd

    nc = bacc.Bacc("TRN2", target_bir_lowering=False, num_devices=1)
    arrays, a = {}, {}
    for name, v in {**laid_out(inputs), **tables()}.items():
        v = np.ascontiguousarray(v)
        arrays["in_" + name] = v
        a[name] = nc.dram_tensor("in_" + name, v.shape, mybir.dt.from_np(v.dtype), kind="ExternalInput").ap()
    for name, shape in SCRATCH.items():
        a[name] = nc.dram_tensor(name, shape, BF16 if name.startswith("qk") else F32).ap()
    a["out"] = nc.dram_tensor("out", (N, D), F32, kind="ExternalOutput").ap()
    build(nc, a)
    r = run_bass_kernel_spmd(nc, [arrays], core_ids=[0])
    return r.results[0]["out"].reshape(B, T, D)
```

```python
import math
from contextlib import ExitStack

import concourse.bass as bass
from concourse import mybir

F32 = mybir.dt.float32
F32R = mybir.dt.float32r
BF16 = mybir.dt.bfloat16
I32 = mybir.dt.int32
ALU = mybir.AluOpType
ACT = mybir.ActivationFunctionType
AX = mybir.AxisListType

P = 128
B, T, D = 2, 2048, 256
N = B * T
NT = N // P
CH = 512
TC = CH // P
CPB = T // CH
KD = D // P
H, HD = 16, 16
HG = 4
NG = H // HG
E, F, CAP = 8, 512, 1024
F4 = F // 4
KF = F // P
SLOTS = E * CAP
LN_EPS, RMS_EPS = 1e-5, 1e-6
NEG = -3.0e38


CREDIT = 1


def open_up(eng, *sems):
    for s in sems:
        eng.sem_inc(s, CREDIT)


class Steps:

    def __init__(self, eng, sem):
        self.eng, self.sem, self.k, self.base, self.per, self.i = eng, sem, 0, 0, 0, None

    def mark(self, ins):
        ins.then_inc(self.sem, 1)
        self.k += 1
        return self.k

    def wait(self, k=None):
        k = self.k if k is None else k
        self.eng.wait_ge(self.sem, self.base + k if self.i is None else self.i * self.per + (self.base + k))

    def link(self, ins):
        self.mark(ins)
        self.wait()

    def enter(self, i, per):
        self.base, self.k, self.per, self.i = self.base + self.k, 0, per, i

    def leave(self, turns):
        assert self.k == self.per, (self.k, self.per)
        self.base, self.k, self.per, self.i = self.base + turns * self.per, 0, 0, None


def three_products(pe, out, weights, moving, first, last):
    terms = [(0, 0), (0, 1), (1, 0)]
    for n, (a, b) in enumerate(terms):
        mm = pe.matmul(out, weights[a], moving[b], start=first and n == 0, stop=last and n == 2)
    return mm


def normalise_route_project(nc, a, keep):
    with ExitStack() as ctx:
        def sb(name, shape, dt=F32):
            return ctx.enter_context(nc.sbuf_tensor(name, shape, dt))

        def ps(name, shape, dt=F32):
            return ctx.enter_context(nc.psum_tensor(name, shape, dt))

        def sem(name):
            return ctx.enter_context(nc.semaphore(name))

        xr_all = sb("xr_all", [P, NT, D])
        mv = sb("mv", [P, NT, 2])
        small = sb("small", [P, 6, NT])
        ident = sb("ident1", [P, P])
        wqkv = sb("wqkv", [P, 3, KD, D])
        wqkv_h = sb("wqkv_h", [P, 3, KD, D], F32R)
        wqkv_l = sb("wqkv_l", [P, 3, KD, D], F32R)
        wf = sb("wf", [P, 2, KD, F4])
        wf_h = sb("wf_h", [P, 2, KD, F4], F32R)
        wf_l = sb("wf_l", [P, 2, KD, F4], F32R)
        wfd = sb("wfd", [P, D])
        wfd_h = sb("wfd_h", [P, D], F32R)
        wfd_l = sb("wfd_l", [P, D], F32R)
        wr = sb("wr", [P, KD, E])
        wr_h = sb("wr_h", [P, KD, E], F32R)
        wr_l = sb("wr_l", [P, KD, E], F32R)
        bqk = sb("bqk", [P, 2, KD])
        bqs = sb("bqs", [P, 2, KD])
        bv = sb("bv", [1, D])
        bv_h = sb("bv_h", [1, D], F32R)
        bv_l = sb("bv_l", [1, D], F32R)
        ones_row = sb("ones_row", [1, P])
        ones_rowr = sb("ones_rowr", [1, P], F32R)
        fnorm = sb("fnorm", [P, KD])
        cos = sb("cos", [P, T])
        sin = sb("sin", [P, T])

        x_loaded = [sem(f"x_loaded{c}") for c in range(4)]
        w_loaded = sem("w_loaded")
        consts_loaded = sem("consts_loaded")
        zeros_set = sem("zeros_set")
        xb_zeroed = sem("xb_zeroed")
        w_high = sem("w_high")
        w_split = sem("w_split")
        stats_sqrt = sem("stats_sqrt")
        dve_steps = sem("dve_steps1")
        var_ready = sem("var_ready")
        ms_ready = sem("ms_ready")
        xn_ready = sem("xn_ready")
        xt_turned = sem("xt_turned")
        xt_high = sem("xt_high")
        xt_low = sem("xt_low")
        xt_high_stored = [sem(f"xt_high_stored{u}") for u in range(2)]
        xt_low_stored = [sem(f"xt_low_stored{u}") for u in range(2)]
        logits_made = sem("logits_made")
        logits_kept = sem("logits_kept")

        x_t = a["x"].rearrange("(t p) d -> p t d", p=P)
        WLOADS = 13

        with ExitStack() as c1:
            xn = [c1.enter_context(nc.sbuf_tensor(f"xn{u}", [P, TC, D], F32)) for u in range(2)]
            xh = [c1.enter_context(nc.sbuf_tensor(f"xh{u}", [P, KD, CH], F32R)) for u in range(2)]
            xl = [c1.enter_context(nc.sbuf_tensor(f"xl{u}", [P, KD, CH], F32R)) for u in range(2)]
            p_xt = [c1.enter_context(nc.psum_tensor(f"p_xt{u}", [P, KD, CH], F32)) for u in range(2)]
            p_lg = [c1.enter_context(nc.psum_tensor(f"p_lg{u}", [P, CH], F32)) for u in range(2)]
            x_all = c1.enter_context(nc.sbuf_tensor("x_all", [P, NT, D], F32))
            stats = c1.enter_context(nc.sbuf_tensor("stats", [P, NT, 6], F32))
            zeros = c1.enter_context(nc.sbuf_tensor("zeros", [P, 8 * D], F32))
            logits = keep["logits"]
            block = c1.enter_context(nc.Block())

            @block.sync
            def _(sp):
                open_up(sp, *xt_high_stored, *xt_low_stored)
                for c in range(4):
                    n = NT // 4
                    sp.dma_start(x_all[:, c * n:(c + 1) * n, :], x_t[:, c * n:(c + 1) * n, :]).then_inc(x_loaded[c], 16)
                sp.dma_start(ident[:], a["ident"]).then_inc(consts_loaded, 16)
                sp.dma_start(wr[:], a["wr"].rearrange("(k p) e -> p k e", p=P)).then_inc(w_loaded, 16)
                for n, w in enumerate(("wqT", "wkT", "wvT")):
                    sp.dma_start(wqkv[:, n], a[w].rearrange("(k p) o -> p k o", p=P)).then_inc(w_loaded, 16)
                for n, w in enumerate(("fwg", "fwu")):
                    sp.dma_start(wf[:, n], a[w].rearrange("(k p) o -> p k o", p=P)).then_inc(w_loaded, 16)
                sp.dma_start(wfd[:], a["fwd"]).then_inc(w_loaded, 16)
                for n, w in enumerate(("bq", "bk")):
                    sp.dma_start(bqk[:, n], a[w]).then_inc(w_loaded, 16)
                sp.dma_start(bv[:], a["bv"]).then_inc(w_loaded, 16)
                sp.dma_start(fnorm[:], a["fnorm"]).then_inc(w_loaded, 16)
                sp.dma_start(cos[:], a["cos"]).then_inc(w_loaded, 16)
                sp.dma_start(sin[:], a["sin"]).then_inc(w_loaded, 16)
                sp.wait_ge(zeros_set, 1)
                for r in range(SLOTS // (8 * P)):
                    sp.dma_start(a["xb"][r * 8 * P:(r + 1) * 8 * P, :].rearrange("(p r) d -> p (r d)", p=P),
                                 zeros[:]).then_inc(xb_zeroed, 16)
                with sp.Fori(0, NT // TC // 2) as i:
                    for u in range(2):
                        at = bass.ds(i * (2 * CH) + u * CH, CH)
                        sp.wait_ge(xt_high, i * 2 + (u + 1))
                        sp.dma_start(a["xth"][:, :, at], xh[u][:].bitcast(F32)).then_inc(xt_high_stored[u], 16)
                        sp.wait_ge(xt_low, i * 2 + (u + 1 + CREDIT))
                        sp.dma_start(a["xtl"][:, :, at], xl[u][:].bitcast(F32)).then_inc(xt_low_stored[u], 16)
                for u in range(2):
                    sp.wait_ge(xt_high_stored[u], 16 * (NT // TC // 2) + CREDIT)
                    sp.wait_ge(xt_low_stored[u], 16 * (NT // TC // 2) + CREDIT)
                sp.wait_ge(xb_zeroed, 16 * (SLOTS // (8 * P)))

            @block.gpsimd
            def _(pool):
                nc.gpsimd.memset(zeros[:], 0.0).then_inc(zeros_set, 1)

            @block.scalar
            def _(act):
                act.wait_ge(var_ready, 1)
                nc.scalar.activation(small[:, 1], small[:, 0], ACT.Sqrt).then_inc(stats_sqrt, 1)
                act.wait_ge(ms_ready, 1)
                nc.scalar.activation(small[:, 4], small[:, 3], ACT.Sqrt).then_inc(stats_sqrt, 1)
                act.wait_ge(w_loaded, 16 * WLOADS)
                for h, w in ((wr_h, wr), (wqkv_h, wqkv), (wf_h, wf), (wfd_h, wfd), (bv_h, bv)):
                    nc.scalar.copy(h[:], w[:]).then_inc(w_high, 1)
                with act.Fori(0, NT // TC // 2) as i:
                    for u in range(2):
                        act.wait_ge(xt_turned, i * 2 + (u + 1 + CREDIT))
                        act.wait_ge(xt_high_stored[u], i * 16 + CREDIT)
                        act.wait_ge(logits_made, i * 2 + CREDIT)
                        nc.scalar.copy(xh[u][:], p_xt[u][:]).then_inc(xt_high, 1)

            @block.vector
            def _(dve):
                open_up(dve, xt_low, logits_kept)
                v = nc.vector
                st = Steps(dve, dve_steps)
                for c in range(4):
                    dve.wait_ge(x_loaded[c], 16)
                    for t in range(c * NT // 4, (c + 1) * NT // 4):
                        st.mark(v.bn_stats(stats[:, t, :], x_all[:, t, :]))
                st.wait()
                for t in range(NT):
                    st.mark(v.bn_aggr(mv[:, t, :], stats[:, t, :]))
                st.wait()
                var = mv[:, :, 1:2].rearrange("p t o -> p (t o)")
                mean = mv[:, :, 0:1].rearrange("p t o -> p (t o)")
                st.mark(v.tensor_copy(keep["mean"][:], mean))
                v.tensor_scalar(small[:, 0], var, LN_EPS, None, ALU.add).then_inc(var_ready, 1)

                def inverse_root(out, value, root, scratch):
                    st.link(v.reciprocal(out, root))
                    st.link(v.tensor_tensor(scratch, out, out, ALU.mult))
                    st.link(v.tensor_tensor(scratch, scratch, value, ALU.mult))
                    st.link(v.tensor_scalar(scratch, scratch, -0.5, 1.5, ALU.mult, ALU.add))
                    st.link(v.tensor_tensor(out, out, scratch, ALU.mult))

                dve.wait_ge(stats_sqrt, 1)
                dve.wait_ge(var_ready, 1)
                rstd, rr = keep["rstd"], small[:, 5]
                inverse_root(rstd[:], small[:, 0], small[:, 1], small[:, 2])
                st.link(v.tensor_tensor(small[:, 2], rstd[:], rstd[:], ALU.mult))
                st.link(v.tensor_tensor(small[:, 2], small[:, 2], var, ALU.mult))
                v.tensor_scalar(small[:, 3], small[:, 2], RMS_EPS, None, ALU.add).then_inc(ms_ready, 1)
                dve.wait_ge(ms_ready, 1)
                dve.wait_ge(stats_sqrt, 2)
                inverse_root(rr, small[:, 3], small[:, 4], small[:, 2])
                st.link(v.tensor_tensor(rr, rr, rstd[:], ALU.mult))
                for n, (w, h, low) in enumerate(((wr, wr_h, wr_l), (wqkv, wqkv_h, wqkv_l), (wf, wf_h, wf_l),
                                                 (wfd, wfd_h, wfd_l), (bv, bv_h, bv_l))):
                    dve.wait_ge(w_high, n + 1)
                    v.tensor_tensor(low[:], w[:], h[:].bitcast(F32), ALU.subtract).then_inc(w_split, 1)
                v.memset(ones_row[:], 1.0).then_inc(w_split, 1)
                dve.wait_ge(w_split, 6)
                v.tensor_copy(ones_rowr[:], ones_row[:]).then_inc(w_split, 1)
                v.tensor_scalar(bqs[:, 0], bqk[:, 0], 1.0 / math.sqrt(HD), None, ALU.mult).then_inc(w_split, 1)
                v.tensor_copy(bqs[:, 1], bqk[:, 1]).then_inc(w_split, 1)
                with dve.Fori(0, NT // TC // 2) as i:
                    for u in range(2):
                        dve.wait_ge(xt_turned, i * 2 + CREDIT)
                        for t in range(TC):
                            tile = i * (2 * TC) + (u * TC + t)
                            cur = x_all[:, bass.ds(tile, 1), :].rearrange("p a d -> p (a d)")
                            v.tensor_scalar(xn[u][:, t, :], cur, keep["mean"][:, bass.ds(tile, 1)],
                                            rstd[:, bass.ds(tile, 1)], ALU.subtract, ALU.mult).then_inc(xn_ready, 1)
                        for t in range(TC):
                            tile = i * (2 * TC) + (u * TC + t)
                            cur = x_all[:, bass.ds(tile, 1), :].rearrange("p a d -> p (a d)")
                            dst = xr_all[:, bass.ds(tile, 1), :].rearrange("p a d -> p (a d)")
                            v.tensor_scalar(dst, cur, keep["mean"][:, bass.ds(tile, 1)],
                                            rr[:, bass.ds(tile, 1)], ALU.subtract, ALU.mult)
                        dve.wait_ge(xt_high, i * 2 + (u + 1))
                        dve.wait_ge(xt_low_stored[u], i * 16 + CREDIT)
                        dve.wait_ge(logits_made, i * 2 + CREDIT)
                        v.tensor_tensor(xl[u][:], p_xt[u][:], xh[u][:].bitcast(F32), ALU.subtract).then_inc(xt_low, 1)
                        dve.wait_ge(logits_made, i * 2 + (u + 1 + CREDIT))
                        v.tensor_copy(logits[:, bass.ds(i * (2 * TC * E) + u * TC * E, TC * E)],
                                      p_lg[u][:, 0:TC * E]).then_inc(logits_kept, 1)

            @block.tensor
            def _(pe):
                open_up(pe, xt_turned, logits_made)
                t_ = nc.tensor
                pe.wait_ge(consts_loaded, 16)
                pe.wait_ge(w_split, 1)
                with pe.Fori(0, NT // TC // 2) as i:
                    for u in range(2):
                        pe.wait_ge(xn_ready, i * (2 * TC) + TC * (u + 1))
                        pe.wait_ge(xt_low, i * 2 + CREDIT)
                        for k in range(KD):
                            for t in range(TC):
                                mm = t_.transpose(p_xt[u][:, k, t * P:(t + 1) * P], xn[u][:, t, k * P:(k + 1) * P], ident[:])
                        mm.then_inc(xt_turned, 1)
                        pe.wait_ge(xt_low, i * 2 + (u + 1 + CREDIT))
                        pe.wait_ge(logits_kept, i * 2 + CREDIT)
                        for t in range(TC):
                            for k in range(KD):
                                tok = slice(t * P, (t + 1) * P)
                                mm = three_products(t_, p_lg[u][:, t * E:(t + 1) * E], (xh[u][:, k, tok], xl[u][:, k, tok]),
                                                    (wr_h[:, k], wr_l[:, k]), k == 0, k == KD - 1)
                        mm.then_inc(logits_made, 1)


        xh = [sb(f"xh_in{u}", [P, KD, CH], F32R) for u in range(2)]
        xl = [sb(f"xl_in{u}", [P, KD, CH], F32R) for u in range(2)]
        xr = [sb(f"xr_in{u}", [P, TC, D]) for u in range(2)]
        v_out = [sb(f"v_out{u}", [P, TC, H, 2 * HD]) for u in range(2)]
        qf = [sb(f"qf{s}", [P, CH]) for s in range(2)]
        turned = [sb(f"turned{s}", [P, CH]) for s in range(2)]
        with_cos = [sb(f"with_cos{s}", [P, CH]) for s in range(2)]
        with_sin = [sb(f"with_sin{s}", [P, CH]) for s in range(2)]
        q = [sb(f"q{s}", [P, CH]) for s in range(2)]
        q_rest = [sb(f"q_rest{s}", [P, CH]) for s in range(2)]
        q_part = [[sb(f"q_part{m}{s}", [P, CH], BF16) for s in range(2)] for m in range(3)]
        fr_h = sb("fr_h", [P, KD, CH], F32R)
        fr_l = sb("fr_l", [P, KD, CH], F32R)
        gelu = sb("gelu", [P, CH])
        hid = sb("hid", [P, CH])
        hid_h = sb("hid_h", [P, CH], F32R)
        hid_l = sb("hid_l", [P, CH], F32R)
        f_out = sb("f_out", [P, TC, D])
        rt = sb("rt", [P, 10, NT * E])
        idx_m = sb("idx_m", [P, NT * E])
        runs = sb("runs", [P, NT * E])
        taken = sb("taken", [P, NT * E], BF16)
        tri = sb("tri", [P, P], BF16)
        ones_b = sb("ones_b", [P, P], BF16)
        trash = sb("trash", [P, 2, NT])
        pick = sb("pick", [P, 12, NT])
        pair = sb("pair", [P, 4, 2, NT])
        send = sb("send", [P, 2, NT], I32)

        p_qk = [ps(f"p_qk{s}", [P, CH]) for s in range(2)]
        p_vd = [ps(f"p_vd{s}", [P, 2, D]) for s in range(2)]
        p_fr = ps("p_fr", [P, KD, CH])
        p_g = ps("p_g", [P, CH])
        p_u = ps("p_u", [P, CH])

        rc_loaded = sem("rc_loaded")
        x_in = [sem(f"x_in{u}") for u in range(2)]
        ones_set = sem("ones_set")
        taken_ready = sem("taken_ready")
        counted = sem("counted")
        counts_read = sem("counts_read")
        route_max = sem("route_max")
        route_exp = sem("route_exp")
        send_ready = sem("send_ready")
        sent = sem("sent")
        fr_turned = sem("fr_turned")
        fr_high = sem("fr_high")
        fr_low = sem("fr_low")
        qk_made = sem("qk_made")
        qf_ready = sem("qf_ready")
        qf_used = sem("qf_used")
        q_ready = sem("q_ready")
        q_rest_ready = sem("q_rest_ready")
        q_part_ready = [sem(f"q_part_ready{m}") for m in range(3)]
        q_stored = [[sem(f"q_stored{m}{s}") for s in range(2)] for m in range(3)]
        gu_made = sem("gu_made")
        gelu_ready = sem("gelu_ready")
        hid_ready = sem("hid_ready")
        hid_high = sem("hid_high")
        hid_low = sem("hid_low")
        v_made = sem("v_made")
        v_kept = sem("v_kept")
        v_stored = [sem(f"v_stored{u}") for u in range(2)]
        down_made = sem("down_made")
        down_kept = sem("down_kept")
        down_stored = sem("down_stored")
        rope_steps = sem("rope_steps")

        block = ctx.enter_context(nc.Block())

        @block.sync
        def _(sp):
            open_up(sp, *q_stored[0], *q_stored[1], *q_stored[2], *v_stored, down_stored)
            for dst, src in ((idx_m, "idx_m"), (runs, "runs"), (tri, "tri"), (ones_b, "ones_b"), (trash, "trash")):
                sp.dma_start(dst[:], a[src]).then_inc(rc_loaded, 16)
            with sp.Fori(0, CPB) as i:
                for u in range(2):
                    tok = bass.ds(i * CH + u * T, CH)
                    sp.wait_ge(down_made, i * 4 + CREDIT)
                    sp.dma_start(xh[u][:].bitcast(F32), a["xth"][:, :, tok]).then_inc(x_in[u], 16)
                    sp.dma_start(xl[u][:].bitcast(F32), a["xtl"][:, :, tok]).then_inc(x_in[u], 16)
                    sp.dma_start(xr[u][:], xr_all[:, bass.ds(i * TC + u * (T // P), TC), :]).then_inc(x_in[u], 16)
                for u in range(2):
                    tok = bass.ds(i * CH + u * T, CH)
                    pairs = bass.ds(i * (CH // 2) + u * (T // 2), CH // 2)
                    for n in range(2 * KD):
                        w, k = divmod(n, KD)
                        piece = sp.snap(i * 8 + (4 * u + n + 1 + CREDIT))
                        for m in range(3):
                            sp.wait_ge(q_part_ready[m], piece)
                            sp.dma_start(a[f"qk{m}"][w, k].rearrange("p (n two) -> p n two", two=2)[:, pairs],
                                         q_part[m][n % 2][:].rearrange("p (n two) -> p n two", two=2)).then_inc(q_stored[m][n % 2], 16)
                    sp.wait_ge(v_kept, i * 4 + (2 * u + 2))
                    sp.dma_start(a["v"][tok, :].rearrange("(t p) c -> p t c", p=P),
                                 v_out[u][:].rearrange("p t h c -> p t (h c)")).then_inc(v_stored[u], 16)
                    sp.wait_ge(down_kept, i * 4 + (2 * u + 2 + CREDIT))
                    sp.dma_start(a["fd"][tok, :].rearrange("(t p) c -> p t c", p=P), f_out[:]).then_inc(down_stored, 16)
            for s in range(2):
                for m in range(3):
                    sp.wait_ge(q_stored[m][s], 16 * 2 * 2 * CPB + CREDIT)
                sp.wait_ge(v_stored[s], 16 * CPB + CREDIT)
            sp.wait_ge(down_stored, 16 * 2 * CPB + CREDIT)

        @block.gpsimd
        def _(pool):
            for u in range(2):
                nc.gpsimd.memset(v_out[u][:], 1.0).then_inc(ones_set, 1)
            pool.wait_ge(send_ready, 1)
            for k in range(2):
                for t in range(NT):
                    nc.gpsimd.indirect_dma_start(
                        a["xb"], bass.IndirectOffsetOnAxis(ap=send[:, k, t:t + 1], axis=0), xr_all[:, t, :],
                        None).then_inc(sent, 16)
            pool.wait_ge(sent, 16 * 2 * NT)

        @block.scalar
        def _(act):
            open_up(act, qf_ready, q_part_ready[0], q_part_ready[1], down_kept)
            s_ = nc.scalar
            act.wait_ge(ones_set, 2)
            with act.Fori(0, CPB) as i:
                for u in range(2):
                    def bias(n):
                        w, k = divmod(n, KD)
                        act.wait_ge(qk_made, i * 8 + (4 * u + n + 1))
                        if n >= 2:
                            act.wait_ge(qf_used, i * 8 + (4 * u + n - 1 + CREDIT))
                        else:
                            act.wait_ge(qf_used, i * 8 + (4 * u + CREDIT))
                        s_.activation(qf[n % 2][:], p_qk[n % 2][:], ACT.Identity, bias=bqs[:, w, k:k + 1],
                                      scale=1.0 / math.sqrt(HD) if w == 0 else 1.0).then_inc(qf_ready, 1)

                    def first(n):
                        act.wait_ge(q_ready, i * 8 + (4 * u + n + 1))
                        act.wait_ge(q_stored[0][n % 2], i * (16 * 4) + (16 * (2 * u + n // 2) + CREDIT))
                        s_.copy(q_part[0][n % 2][:], q[n % 2][:]).then_inc(q_part_ready[0], 1)

                    def second(n):
                        act.wait_ge(q_rest_ready, i * 8 + (4 * u + n + 1 + CREDIT))
                        act.wait_ge(q_stored[1][n % 2], i * (16 * 4) + (16 * (2 * u + n // 2) + CREDIT))
                        s_.copy(q_part[1][n % 2][:], q_rest[n % 2][:]).then_inc(q_part_ready[1], 1)

                    def values(n):
                        act.wait_ge(v_made, i * 4 + (2 * u + n + 1))
                        act.wait_ge(v_stored[u], i * 16 + CREDIT)
                        s_.copy(v_out[u][:, 2 * n:2 * n + 2, :, 0:HD],
                                p_vd[n][:].rearrange("p t (h c) -> p t h c", c=HD)).then_inc(v_kept, 1)

                    act.wait_ge(fr_turned, i * 2 + (u + 1))
                    act.wait_ge(gu_made, i * 2 + (u + CREDIT))
                    for k in range(KD):
                        s_.activation(fr_h[:, k], p_fr[:, k], ACT.Identity, scale=fnorm[:, k:k + 1]).then_inc(fr_high, 1)
                    bias(0)
                    bias(1)
                    first(0)
                    act.wait_ge(gu_made, i * 2 + (u + 1 + CREDIT))
                    act.wait_ge(hid_ready, i * 2 + (u + CREDIT))
                    s_.activation(gelu[:], p_g[:], ACT.Gelu).then_inc(gelu_ready, 1)
                    first(1)
                    bias(2)
                    second(0)
                    act.wait_ge(hid_ready, i * 2 + (u + 1 + CREDIT))
                    act.wait_ge(down_made, i * 4 + (2 * u + CREDIT))
                    s_.copy(hid_h[:], hid[:]).then_inc(hid_high, 1)
                    second(1)
                    bias(3)
                    first(2)
                    values(0)
                    second(2)
                    values(1)
                    first(3)
                    second(3)
                    for n in range(2):
                        act.wait_ge(down_made, i * 4 + (2 * u + n + 1 + CREDIT))
                        act.wait_ge(down_stored, i * 32 + (16 * u + CREDIT))
                        s_.copy(f_out[:, 2 * n:2 * n + 2, :], p_vd[n][:]).then_inc(down_kept, 1)

        @block.vector
        def _(dve):
            open_up(dve, qf_used, q_rest_ready, q_part_ready[2], fr_low, hid_ready, hid_low)
            v = nc.vector
            st = Steps(dve, rope_steps)
            mask = [(j // HD) * HD + (j % HD + HD // 2) % HD for j in range(32)]

            def te(ap):
                return ap.rearrange("p (t e) -> p t e", e=E)

            def et(ap):
                return ap.rearrange("p (e t) -> p t e", e=E)

            def wide(ap):
                return ap.unsqueeze(2).broadcast_to([P, NT, E])

            lg, idx = te(keep["logits"][:]), te(idx_m[:])
            dve.wait_ge(rc_loaded, 16 * 5)
            best, second = pick[:, 0], pick[:, 1]
            st.link(v.tensor_reduce(best, lg, AX.X, ALU.max))
            below = te(rt[:, 0])
            st.link(v.tensor_tensor(below, lg, wide(best), ALU.subtract))

            def one_hot(out, values, top, scratch, low):
                st.link(v.tensor_tensor(scratch, values, wide(top), ALU.is_equal))
                st.link(v.tensor_tensor(scratch, scratch, idx, ALU.mult))
                st.link(v.tensor_reduce(low, scratch, AX.X, ALU.min))
                st.link(v.tensor_tensor(out, idx, wide(low), ALU.is_equal))

            hot1, hot2, scratch, rest = te(rt[:, 1]), te(rt[:, 2]), te(rt[:, 3]), te(rt[:, 4])
            one_hot(hot1, lg, best, scratch, pick[:, 2])
            st.link(v.scalar_tensor_tensor(out=rt[:, 4], in0=rt[:, 1], scalar=NEG, in1=rt[:, 0],
                                           op0=ALU.mult, op1=ALU.add))
            st.link(v.tensor_reduce(second, rest, AX.X, ALU.max))
            one_hot(hot2, rest, second, scratch, pick[:, 3])
            v.tensor_tensor(taken[:].rearrange("p (e t) -> p t e", e=E), hot1, hot2, ALU.add).then_inc(taken_ready, 1)
            dve.wait_ge(counted, 1)
            st.link(v.tensor_copy(rt[:, 5], p_u[:, 0:NT * E]))
            st.link(v.tensor_tensor_scan(rt[:, 6], runs[:], rt[:, 5], 0.0, ALU.mult, ALU.add))
            st.link(v.tensor_tensor(rt[:, 6], rt[:, 6], rt[:, 5], ALU.subtract))
            v.tensor_tensor(rt[:, 7], p_g[:, 0:NT * E], rt[:, 6], ALU.add).then_inc(counts_read, 1)
            dve.wait_ge(counts_read, 1)
            place, expert, kept, slot = pair[:, 0], pair[:, 1], pair[:, 2], pair[:, 3]
            for k, hot in enumerate((hot1, hot2)):
                st.link(v.tensor_tensor(scratch, hot, et(rt[:, 7]), ALU.mult))
                st.link(v.tensor_reduce(place[:, k], scratch, AX.X, ALU.add))
            st.link(v.tensor_scalar(expert, pick[:, 2:4], float(E), float(CAP), ALU.add, ALU.mult))
            st.link(v.tensor_scalar(kept, place, float(CAP), None, ALU.is_lt))
            st.link(v.tensor_scalar(slot, place, float(CAP - 1), None, ALU.min))
            st.link(v.tensor_tensor(slot, slot, expert, ALU.add))
            st.link(v.tensor_copy(keep["fetch"][:], slot))
            st.link(v.tensor_tensor(slot, slot, trash[:], ALU.subtract))
            st.link(v.tensor_tensor(slot, slot, kept, ALU.mult))
            st.link(v.tensor_tensor(slot, slot, trash[:], ALU.add))
            v.tensor_copy(send[:], slot).then_inc(send_ready, 1)
            st.link(v.tensor_tensor(keep["fits"][:], kept[:, 0], kept[:, 1], ALU.mult))
            st.link(v.tensor_copy(keep["second"][:], second))
            st.link(v.tensor_copy(keep["below"][:], rt[:, 0]))

            with dve.Fori(0, CPB) as i:
                st.enter(i, 2 * (2 * KD * 2))
                for u in range(2):
                    pos = bass.ds(i * CH, CH)

                    def rope(n):
                        dve.wait_ge(qf_ready, i * 8 + (4 * u + n + 1 + CREDIT))
                        st.mark(v.tensor_tensor(with_cos[n % 2][:], qf[n % 2][:], cos[:, pos], ALU.mult))
                        v.stream_shuffle(turned[n % 2][:], qf[n % 2][:], mask).then_inc(qf_used, 1)
                        dve.wait_ge(qf_used, i * 8 + (4 * u + n + 1 + CREDIT))
                        st.mark(v.tensor_tensor(with_sin[n % 2][:], turned[n % 2][:], sin[:, pos], ALU.mult))
                        st.wait()
                        dve.wait_ge(q_rest_ready, i * 8 + (4 * u + max(n - 1, 0) + CREDIT))
                        v.tensor_tensor(q[n % 2][:], with_cos[n % 2][:], with_sin[n % 2][:], ALU.add).then_inc(q_ready, 1)

                    def rest(n):
                        dve.wait_ge(q_part_ready[0], i * 8 + (4 * u + n + 1 + CREDIT))
                        dve.wait_ge(q_part_ready[2], i * 8 + (4 * u + max(n - 1, 0) + CREDIT))
                        v.tensor_tensor(q_rest[n % 2][:], q[n % 2][:], q_part[0][n % 2][:],
                                        ALU.subtract).then_inc(q_rest_ready, 1)

                    def third(n):
                        dve.wait_ge(q_part_ready[1], i * 8 + (4 * u + n + 1 + CREDIT))
                        dve.wait_ge(q_stored[2][n % 2], i * (16 * 4) + (16 * (2 * u + n // 2) + CREDIT))
                        v.tensor_tensor(q_part[2][n % 2][:], q_rest[n % 2][:], q_part[1][n % 2][:],
                                        ALU.subtract).then_inc(q_part_ready[2], 1)

                    dve.wait_ge(gu_made, i * 2 + (u + CREDIT))
                    for k in range(KD):
                        dve.wait_ge(fr_high, i * 4 + (2 * u + k + 1))
                        v.scalar_tensor_tensor(out=fr_l[:, k], in0=p_fr[:, k], scalar=fnorm[:, k:k + 1],
                                               in1=fr_h[:, k].bitcast(F32), op0=ALU.mult,
                                               op1=ALU.subtract).then_inc(fr_low, 1)
                    rope(0)
                    rope(1)
                    rest(0)
                    dve.wait_ge(gelu_ready, i * 2 + (u + 1))
                    dve.wait_ge(hid_low, i * 2 + (u + CREDIT))
                    v.tensor_tensor(hid[:], p_u[:], gelu[:], ALU.mult).then_inc(hid_ready, 1)
                    rest(1)
                    rope(2)
                    third(0)
                    dve.wait_ge(hid_high, i * 2 + (u + 1))
                    dve.wait_ge(down_made, i * 4 + (2 * u + CREDIT))
                    v.tensor_tensor(hid_l[:], hid[:], hid_h[:].bitcast(F32), ALU.subtract).then_inc(hid_low, 1)
                    third(1)
                    rope(3)
                    rest(2)
                    rest(3)
                    third(2)
                    third(3)
            st.leave(CPB)

        @block.tensor
        def _(pe):
            open_up(pe, gu_made, down_made)
            t_ = nc.tensor
            pe.wait_ge(rc_loaded, 16 * 5)
            pe.wait_ge(taken_ready, 1)
            t_.matmul(p_g[:, 0:NT * E], tri[:], taken[:], start=True, stop=True)
            t_.matmul(p_u[:, 0:NT * E], ones_b[:], taken[:], start=True, stop=True).then_inc(counted, 1)
            pe.wait_ge(counts_read, 1)
            with pe.Fori(0, CPB) as i:
                for u in range(2):
                    xx = [(xh[u][:, k], xl[u][:, k]) for k in range(KD)]

                    def piece(n):
                        w, k = divmod(n, KD)
                        if n >= 2:
                            pe.wait_ge(qf_ready, i * 8 + (4 * u + n - 1 + CREDIT))
                        else:
                            pe.wait_ge(qf_ready, i * 8 + (4 * u + CREDIT))
                        out = slice(k * P, (k + 1) * P)
                        for c in range(KD):
                            mm = three_products(t_, p_qk[n % 2][:], (wqkv_h[:, w, c, out], wqkv_l[:, w, c, out]),
                                                xx[c], c == 0, c == KD - 1)
                        mm.then_inc(qk_made, 1)

                    pe.wait_ge(x_in[u], i * 48 + 48)
                    pe.wait_ge(fr_low, i * 4 + (2 * u + CREDIT))
                    for k in range(KD):
                        for t in range(TC):
                            mm = t_.transpose(p_fr[:, k, t * P:(t + 1) * P], xr[u][:, t, k * P:(k + 1) * P], ident[:])
                    mm.then_inc(fr_turned, 1)
                    piece(0)
                    piece(1)
                    pe.wait_ge(fr_low, i * 4 + (2 * u + 2 + CREDIT))
                    pe.wait_ge(hid_ready, i * 2 + (u + CREDIT))
                    for m, out in enumerate((p_g, p_u)):
                        for c in range(KD):
                            mm = three_products(t_, out[:], (wf_h[:, m, c], wf_l[:, m, c]), (fr_h[:, c], fr_l[:, c]),
                                                c == 0, c == KD - 1)
                    mm.then_inc(gu_made, 1)
                    piece(2)
                    piece(3)
                    for n in range(2):
                        pe.wait_ge(down_kept, i * 4 + (2 * u + CREDIT))
                        for t in range(2):
                            tok = slice((2 * n + t) * P, (2 * n + t + 1) * P)
                            for c in range(KD):
                                three_products(t_, p_vd[n][:, t], (xx[c][0][:, tok], xx[c][1][:, tok]),
                                               (wqkv_h[:, 2, c], wqkv_l[:, 2, c]), c == 0, False)
                            t_.matmul(p_vd[n][:, t], ones_rowr[:], bv_h[:], start=False, stop=False)
                            mm = t_.matmul(p_vd[n][:, t], ones_rowr[:], bv_l[:], start=False, stop=True)
                        mm.then_inc(v_made, 1)
                    pe.wait_ge(hid_low, i * 2 + (u + 1 + CREDIT))
                    for n in range(2):
                        pe.wait_ge(v_kept, i * 4 + (2 * u + n + 1))
                        for t in range(2):
                            tok = slice((2 * n + t) * P, (2 * n + t + 1) * P)
                            mm = three_products(t_, p_vd[n][:, t], (hid_h[:, tok], hid_l[:, tok]),
                                                (wfd_h[:], wfd_l[:]), True, True)
                        mm.then_inc(down_made, 1)


def run_experts(nc, a, keep):
    with ExitStack() as ctx:
        def sb(name, shape, dt=F32):
            return ctx.enter_context(nc.sbuf_tensor(name, shape, dt))

        def ps(name, shape, dt=F32):
            return ctx.enter_context(nc.psum_tensor(name, shape, dt))

        def sem(name):
            return ctx.enter_context(nc.semaphore(name))

        RT = CAP // P
        RC = CAP // CH
        WW = 2 * KD * F + KF * D
        ident = sb("ident2", [P, P])
        rows = [sb(f"rows{u}", [P, RT, D]) for u in range(2)]
        w = [sb(f"w{u}", [P, WW]) for u in range(2)]
        w_h = [sb(f"w_h{u}", [P, WW], F32R) for u in range(2)]
        w_l = [sb(f"w_l{u}", [P, WW], F32R) for u in range(2)]
        nw = [sb(f"nw{u}", [P, KD]) for u in range(2)]
        xt_h = [sb(f"xt_h{c}", [P, KD, CH], F32R) for c in range(RC)]
        xt_l = [sb(f"xt_l{c}", [P, KD, CH], F32R) for c in range(RC)]
        gelu = [sb(f"gelu_e{s}", [P, CH]) for s in range(2)]
        hid = [sb(f"hid_e{s}", [P, CH]) for s in range(2)]
        hid_h = [sb(f"hid_eh{c}", [P, KF, CH], F32R) for c in range(RC)]
        hid_l = [sb(f"hid_el{c}", [P, KF, CH], F32R) for c in range(RC)]
        e_out = sb("e_out", [P, RT, D])

        p_t = ps("p_t", [P, KD, CH])
        p_g = [ps(f"p_eg{s}", [P, CH]) for s in range(2)]
        p_u = [ps(f"p_eu{s}", [P, CH]) for s in range(2)]
        p_d = [ps(f"p_d{s}", [P, 2, D]) for s in range(2)]

        id_loaded = sem("id_loaded")
        rows_loaded = [sem(f"rows_loaded{u}") for u in range(2)]
        w_loaded = [sem(f"w_loaded_e{u}") for u in range(2)]
        w_high = sem("w_high_e")
        w_low = sem("w_low_e")
        turned = sem("turned_e")
        xt_high = sem("xt_high_e")
        xt_low = sem("xt_low_e")
        gu_made = sem("gu_made_e")
        gelu_ready = sem("gelu_ready_e")
        hid_ready = sem("hid_ready_e")
        hid_high = sem("hid_high_e")
        hid_low = sem("hid_low_e")
        down_made = sem("down_made_e")
        down_kept = sem("down_kept_e")
        out_stored = sem("out_stored_e")
        block = ctx.enter_context(nc.Block())

        GU, DN = RC * KF, RT // 2

        def count(i, e, per, k, head=0):
            return i * (2 * per) + (head + e * per + k)

        def pairs(eng, pair):
            with eng.Fori(0, E // 2 - 1) as i:
                pair(i, E)
            pair(E // 2 - 1, 2)

        @block.sync
        def _(sp):
            open_up(sp, out_stored)
            sp.dma_start(ident[:], a["ident"]).then_inc(id_loaded, 16)

            def load(i, n, u):
                e = i * 2 + n
                sp.dma_start(rows[u][:], a["xb"][bass.ds(i * (2 * CAP) + n * CAP, CAP), :].rearrange("(t p) d -> p t d", p=P)
                             ).then_inc(rows_loaded[u], 16)
                sp.dma_start(nw[u][:], a["normw"][bass.ds(e, 1)].rearrange("e p k -> p (e k)")
                             ).then_inc(rows_loaded[u], 16)
                for n, name in enumerate(("wg", "wu")):
                    sp.dma_start(w[u][:, n * KD * F:(n + 1) * KD * F].rearrange("p (k f) -> p k f", k=KD),
                                 a[name][bass.ds(e, 1)].rearrange("e (k p) f -> p (e k) f", p=P)
                                 ).then_inc(w_loaded[u], 16)
                sp.dma_start(w[u][:, 2 * KD * F:].rearrange("p (k d) -> p k d", k=KF),
                             a["wd"][bass.ds(e, 1)].rearrange("e (k p) d -> p (e k) d", p=P)
                             ).then_inc(w_loaded[u], 16)

            load(0, 0, 0)
            load(0, 1, 1)

            def pair(i, left):
                for u in range(2):
                    if u + 2 < left:
                        sp.wait_ge(xt_low, count(i, u, RC, RC, CREDIT))
                        sp.wait_ge(w_low, count(i, u, 1, 1))
                        load(i, u + 2, u)
                    sp.wait_ge(down_kept, count(i, u, DN, DN, CREDIT))
                    sp.dma_start(a["ob"][bass.ds(i * (2 * CAP) + u * CAP, CAP), :].rearrange("(t p) d -> p t d", p=P),
                                 e_out[:]).then_inc(out_stored, 16)

            pairs(sp, pair)
            sp.wait_ge(out_stored, 16 * E + CREDIT)

        @block.gpsimd
        def _(pool):
            with pool.Fori(0, E // 2) as i:
                for u in range(2):
                    pool.wait_ge(w_high, count(i, u, 1, 1))
                    nc.gpsimd.tensor_tensor(w_l[u][:], w[u][:], w_h[u][:].bitcast(F32), ALU.subtract).then_inc(w_low, 1)

        @block.scalar
        def _(act):
            open_up(act, down_kept)
            s_ = nc.scalar

            def rows_high(i, e, c):
                act.wait_ge(turned, count(i, e, RC, c + 1))
                act.wait_ge(gu_made, count(i, e, GU, 0, CREDIT))
                for k in range(KD):
                    s_.activation(xt_h[c][:, k], p_t[:, k], ACT.Identity, scale=nw[e % 2][:, k:k + 1]).then_inc(xt_high, 1)

            for u in range(2):
                act.wait_ge(w_loaded[u], 48)
                s_.copy(w_h[u][:], w[u][:]).then_inc(w_high, 1)
            for c in range(RC):
                rows_high(0, 0, c)

            def pair(i, left):
                for u in range(2):
                    for n in range(GU + 1):
                        if n < GU:
                            act.wait_ge(gu_made, count(i, u, GU, n + 1, CREDIT))
                            act.wait_ge(hid_ready, count(i, u, GU, max(n - 1, 0), CREDIT))
                            s_.activation(gelu[n % 2][:], p_g[n % 2][:], ACT.Gelu).then_inc(gelu_ready, 1)
                        if n:
                            c, f = divmod(n - 1, KF)
                            act.wait_ge(hid_ready, count(i, u, GU, n, CREDIT))
                            act.wait_ge(down_made, count(i, u, DN, 0, CREDIT))
                            s_.copy(hid_h[c][:, f], hid[(n - 1) % 2][:]).then_inc(hid_high, 1)
                    for n in range(DN):
                        if n % 2 == 0 and u + 1 < left:
                            rows_high(i, u + 1, n // 2)
                        act.wait_ge(down_made, count(i, u, DN, n + 1, CREDIT))
                        act.wait_ge(out_stored, count(i, u, 16, 0, CREDIT))
                        s_.copy(e_out[:, 2 * n:2 * n + 2, :], p_d[n % 2][:]).then_inc(down_kept, 1)
                    if u + 2 < left:
                        act.wait_ge(w_loaded[u], i * 48 + 96)
                        s_.copy(w_h[u][:], w[u][:]).then_inc(w_high, 1)

            pairs(act, pair)

        @block.vector
        def _(dve):
            open_up(dve, xt_low, hid_ready, hid_low)
            v = nc.vector

            def rows_low(i, e, c):
                dve.wait_ge(xt_high, count(i, e, 2 * RC, 2 * c + 2))
                for k in range(KD):
                    ins = v.scalar_tensor_tensor(out=xt_l[c][:, k], in0=p_t[:, k], scalar=nw[e % 2][:, k:k + 1],
                                                 in1=xt_h[c][:, k].bitcast(F32), op0=ALU.mult, op1=ALU.subtract)
                ins.then_inc(xt_low, 1)

            for c in range(RC):
                rows_low(0, 0, c)

            def pair(i, left):
                for u in range(2):
                    for n in range(GU + 1):
                        if n < GU:
                            dve.wait_ge(gelu_ready, count(i, u, GU, n + 1))
                            dve.wait_ge(hid_low, count(i, u, GU, max(n - 1, 0), CREDIT))
                            v.tensor_tensor(hid[n % 2][:], p_u[n % 2][:], gelu[n % 2][:], ALU.mult).then_inc(hid_ready, 1)
                        if n:
                            c, f = divmod(n - 1, KF)
                            dve.wait_ge(hid_high, count(i, u, GU, n))
                            v.tensor_tensor(hid_l[c][:, f], hid[(n - 1) % 2][:], hid_h[c][:, f].bitcast(F32),
                                            ALU.subtract).then_inc(hid_low, 1)
                    if u + 1 < left:
                        for c in range(RC):
                            rows_low(i, u + 1, c)

            pairs(dve, pair)

        @block.tensor
        def _(pe):
            open_up(pe, gu_made, down_made)
            t_ = nc.tensor

            def turn(i, e, c):
                if c == 0:
                    pe.wait_ge(rows_loaded[e % 2], i * 32 + 32 * (e // 2 + 1))
                pe.wait_ge(xt_low, count(i, e, RC, c, CREDIT))
                for k in range(KD):
                    for t in range(TC):
                        mm = t_.transpose(p_t[:, k, t * P:(t + 1) * P], rows[e % 2][:, c * TC + t, k * P:(k + 1) * P], ident[:])
                mm.then_inc(turned, 1)

            pe.wait_ge(id_loaded, 16)
            for c in range(RC):
                turn(0, 0, c)

            def pair(i, left):
                for u in range(2):
                    wg = [(w_h[u][:, k * F:(k + 1) * F], w_l[u][:, k * F:(k + 1) * F]) for k in range(2 * KD)]
                    wd = [(w_h[u][:, 2 * KD * F + k * D:2 * KD * F + (k + 1) * D],
                           w_l[u][:, 2 * KD * F + k * D:2 * KD * F + (k + 1) * D]) for k in range(KF)]
                    pe.wait_ge(w_low, count(i, u, 1, 1))
                    for n in range(GU):
                        c, f = divmod(n, KF)
                        if f == 0:
                            pe.wait_ge(xt_low, count(i, u, RC, c + 1, CREDIT))
                        pe.wait_ge(hid_ready, count(i, u, GU, max(n - 1, 0), CREDIT))
                        for m, out in enumerate((p_g, p_u)):
                            for k in range(KD):
                                mm = three_products(
                                    t_, out[n % 2][:], tuple(x[:, f * P:(f + 1) * P] for x in wg[m * KD + k]),
                                    (xt_h[c][:, k], xt_l[c][:, k]), k == 0, k == KD - 1)
                        mm.then_inc(gu_made, 1)
                    for n in range(DN):
                        if n % 2 == 0 and u + 1 < left:
                            turn(i, u + 1, n // 2)
                        c, t0 = divmod(2 * n, TC)
                        pe.wait_ge(hid_low, count(i, u, GU, KF * (c + 1), CREDIT))
                        pe.wait_ge(down_kept, count(i, u, DN, max(n - 1, 0), CREDIT))
                        for t in range(2):
                            tok = slice((t0 + t) * P, (t0 + t + 1) * P)
                            for k in range(KF):
                                mm = three_products(t_, p_d[n % 2][:, t], (hid_h[c][:, k, tok], hid_l[c][:, k, tok]),
                                                    wd[k], k == 0, k == KF - 1)
                        mm.then_inc(down_made, 1)

            pairs(pe, pair)


def attend(nc, a, keep):
    with ExitStack() as ctx:
        def sb(name, shape, dt=F32):
            return ctx.enter_context(nc.sbuf_tensor(name, shape, dt))

        def ps(name, shape, dt=F32):
            return ctx.enter_context(nc.psum_tensor(name, shape, dt))

        def sem(name):
            return ctx.enter_context(nc.semaphore(name))

        PAIRS = ((0, 0), (0, 1), (0, 2), (1, 0), (1, 1), (2, 0))
        KS = len(PAIRS) * HD
        KM = KS + 2
        R = 2 * HD
        LAG = 20
        STEPS = [(j, i) for j in range(CPB) for i in range(TC * (j + 1))]
        MAXES = [(j, TC * j + r, c) for j in range(CPB) for r in range(TC) for c in range(j + 1)]
        S = len(STEPS)
        assert S == len(MAXES)
        ENDS = [n for n in range(S) if n == S - 1 or MAXES[n + 1][0] != MAXES[n][0]]
        assert ENDS == [n for n in range(S) if n == S - 1 or STEPS[n + 1][0] != STEPS[n][0]]
        HEAD_TURNS = sum(e + 1 < LAG for e in ENDS)
        HEAD_UNITS = HG * LAG + HEAD_TURNS
        UNITS = HG * S + CPB
        assert HEAD_UNITS % 2 == 0 and UNITS % 2 == 0

        qs = [sb(f"qs{b}", [KM, HG, T], BF16) for b in range(B)]
        ks = [sb(f"ks{b}", [KM, HG, T], BF16) for b in range(B)]
        vs = [sb(f"vs{b}", [P, T // P, HG * R]) for b in range(B)]
        probs = [sb(f"probs{r}", [P, HG, CH]) for r in range(3)]
        tops = [sb(f"tops{r}", [P, HG, TC, CPB]) for r in range(2)]
        neg_top = [sb(f"neg_top{r}", [P, P]) for r in range(2)]
        top_part = [[sb(f"top_part{m}{r}", [HG * TC, P], BF16) for r in range(2)] for m in range(2)]
        ident_f = sb("ident_f", [P, P])
        ident_b = sb("ident_b", [P, P], BF16)
        hide_q = sb("hide_q", [P, P], BF16)
        hide_k = sb("hide_k", [P, P], BF16)
        y = [sb(f"y{r}", [P, CH]) for r in range(2)]
        x_all, mix = keep["x"], keep["mix"]
        ex = sb("ex", [P, NT * E])
        ex2 = sb("ex2", [P, NT])
        cw = sb("cw", [P, 6, NT])
        got = [[sb(f"got{k}{r}", [P, D]) for r in range(2)] for k in range(2)]
        fall = [sb(f"fall{r}", [P, D]) for r in range(2)]
        part = [sb(f"part{n}", [P, D]) for n in range(3)]

        p_s = [ps(f"p_s{r}", [P, 2, CH]) for r in range(2)]
        p_m = [ps(f"p_m{r}", [P, CH]) for r in range(2)]
        p_y = [ps(f"p_y{r}", [P, CH]) for r in range(2)]

        c_loaded = sem("c_loaded")
        rows_set = sem("rows_set")
        in_loaded = [sem(f"in_loaded{b}") for b in range(B)]
        x_loaded = sem("x_loaded_c")
        max_made = sem("max_made")
        max_read = sem("max_read")
        neg_ready = sem("neg_ready")
        top_stored = [sem(f"top_stored{j}") for j in range(CPB)]
        s_made = sem("s_made")
        p_ready = sem("p_ready")
        pv_done = sem("pv_done")
        y_steps = sem("y_steps")
        y_ready = sem("y_ready")
        y_stored = [sem(f"y_stored{r}") for r in range(2)]
        exps = sem("exps")
        cw_steps = sem("cw_steps")
        got_in = [[sem(f"got_in{k}{r}") for r in range(2)] for k in range(2)]
        fall_in = [sem(f"fall_in{r}") for r in range(2)]
        mix_steps = sem("mix_steps")
        block = ctx.enter_context(nc.Block())

        LOADS = 2 * len(PAIRS) + 1

        def count(i, b, per, k, head=0):
            return i * (2 * per) + (head + b * per + k)

        def groups(eng, group):
            with eng.Fori(0, NG - 1) as i:
                for b in range(B):
                    group(i, b, True)
            for b in range(B):
                group(NG - 1, b, b == 0)

        def lead(follows):
            for s in range(S):
                n = s + LAG
                if n < S:
                    yield s, n, True
                elif follows:
                    yield s, n - S, False
                else:
                    yield s, (S if n == S else None), True

        def turns_at(n, own):
            return (n - 1) % S in ENDS and (n > 0 or not own)

        head_turn, group_turn, unit_now = {}, {}, 0
        for n in range(LAG):
            unit_now += HG
            if n - 1 in ENDS:
                unit_now += 1
                head_turn[MAXES[n - 1][0]] = unit_now
        unit_now = 0
        for s, n, own in lead(True):
            unit_now += HG
            if turns_at(n, own):
                unit_now += 1
                group_turn[MAXES[(n - 1) % S][0]] = unit_now
        TOPS = 16 * 2 * HG

        @block.sync
        def _(sp):
            open_up(sp, *y_stored)
            for dst, src in ((ident_f, "ident"), (ident_b, "ident_b"), (hide_q, "hide_after_row"),
                             (hide_k, "hide_before_row")):
                sp.dma_start(dst[:], a[src]).then_inc(c_loaded, 16)

            def load(i, hg, b):
                for w, dst in enumerate((qs[b], ks[b])):
                    for n, pair in enumerate(PAIRS):
                        src = a[f"qk{pair[w]}"][w].rearrange("k p n -> (k p) n")
                        sp.dma_start(dst[n * HD:(n + 1) * HD],
                                     src[bass.ds(i * (HG * HD) + hg * (HG * HD), HG * HD), b * T:(b + 1) * T]
                                     .rearrange("(h d) n -> d h n", d=HD)).then_inc(in_loaded[b], 16)
                sp.dma_start(vs[b][:], a["v"][b * T:(b + 1) * T, bass.ds(i * (HG * R) + hg * (HG * R), HG * R)]
                             .rearrange("(t p) c -> p t c", p=P)).then_inc(in_loaded[b], 16)

            def tops_in(b, j, value):
                sp.wait_ge(max_read, value)
                for m in range(2):
                    for h in range(HG):
                        sp.dma_start(qs[b][KS + m:KS + m + 1, h, j * CH:(j + 1) * CH]
                                     .rearrange("o (t n) -> o t n", t=TC),
                                     top_part[m][j % 2][h * TC:(h + 1) * TC, :]).then_inc(top_stored[j], 16)

            def y_out(i, b, j):
                sp.wait_ge(y_ready, count(i, b, CPB, j + 1, CREDIT))
                sp.dma_start(a["yt"][bass.ds(i * (HG * R), HG * R), b * T + j * CH:b * T + (j + 1) * CH],
                             y[j % 2][:]).then_inc(y_stored[j % 2], 16)

            load(0, 0, 0)
            sp.dma_start(x_all[:], a["x"].rearrange("(t p) d -> p t d", p=P)).then_inc(x_loaded, 16)
            tops_in(0, 0, head_turn[0])
            tops_in(0, 1, head_turn[1])

            def group(i, b, follows):
                if follows:
                    sp.wait_ge(pv_done, count(i, b, S, 0, CREDIT))
                    load(i, b, 1 - b)
                tops_in(b, 2, count(i, b, UNITS, group_turn[2], HEAD_UNITS))
                y_out(i, b, 0)
                y_out(i, b, 1)
                tops_in(b, 3, count(i, b, UNITS, group_turn[3] - (0 if follows else HG), HEAD_UNITS))
                if follows:
                    tops_in(1 - b, 0, count(i, b, UNITS, group_turn[0], HEAD_UNITS))
                y_out(i, b, 2)
                if follows:
                    tops_in(1 - b, 1, count(i, b, UNITS, group_turn[1], HEAD_UNITS))
                y_out(i, b, 3)

            groups(sp, group)
            for r in range(2):
                sp.wait_ge(y_stored[r], 16 * (CPB // 2) * B * NG + CREDIT)

        @block.gpsimd
        def _(pool):
            for n, (rows, what) in enumerate([(ks[b][KS:KM], 1.0) for b in range(B)] + [(t[:], 0.0) for t in neg_top]):
                nc.gpsimd.memset(rows, what).then_inc(rows_set, 1)
                pool.wait_ge(rows_set, n + 1)
            st = Steps(pool, mix_steps)
            fd = a["fd"].rearrange("(t p) d -> t p d", p=P)

            def fetch(t):
                for k in range(2):
                    nc.gpsimd.indirect_dma_start(
                        got[k][t % 2][:], None, a["ob"],
                        bass.IndirectOffsetOnAxis(ap=keep["fetch"][:, k, t:t + 1], axis=0)).then_inc(got_in[k][t % 2], 16)
                nc.gpsimd.dma_start(fall[t % 2][:], fd[t]).then_inc(fall_in[t % 2], 16)

            fetch(0)
            pool.wait_ge(x_loaded, 16)
            pool.wait_ge(cw_steps, 9)
            g = nc.gpsimd
            for t in range(NT):
                if t + 1 < NT:
                    fetch(t + 1)
                st.mark(g.tensor_scalar(mix[:, t], x_all[:, t], keep["mean"][:, t:t + 1], cw[:, 5, t:t + 1],
                                        ALU.subtract, ALU.mult))
                for k in range(2):
                    pool.wait_ge(got_in[k][t % 2], 16 * (t // 2 + 1))
                    st.mark(g.tensor_scalar(part[k][:], got[k][t % 2][:], cw[:, 2 + k, t:t + 1], None, ALU.mult))
                pool.wait_ge(fall_in[t % 2], 16 * (t // 2 + 1))
                st.link(g.tensor_scalar(part[2][:], fall[t % 2][:], cw[:, 4, t:t + 1], None, ALU.mult))
                st.mark(g.tensor_tensor(part[0][:], part[0][:], part[1][:], ALU.add))
                st.link(g.tensor_tensor(mix[:, t], mix[:, t], part[2][:], ALU.add))
                st.link(g.tensor_tensor(mix[:, t], mix[:, t], part[0][:], ALU.add))

        @block.scalar
        def _(act):
            open_up(act, p_ready)
            s_ = nc.scalar
            s_.activation(ex[:], keep["below"][:], ACT.Exp).then_inc(exps, 1)
            s_.activation(ex2[:], keep["second"][:], ACT.Exp).then_inc(exps, 1)

            def group(i, b, follows):
                for s, (j, k) in enumerate(STEPS):
                    w = CH - P * max(k - TC * j, 0)
                    act.wait_ge(pv_done, count(i, b, S, max(s - 2, 0), CREDIT))
                    for r in range(2):
                        act.wait_ge(s_made, count(i, b, 2 * S, 2 * s + r + 1))
                        s_.activation(probs[s % 3][:, 2 * r:2 * r + 2, 0:w], p_s[r][:, :, 0:w], ACT.Exp).then_inc(p_ready, 1)

            groups(act, group)

        @block.vector
        def _(dve):
            open_up(dve, y_ready)
            v = nc.vector
            cs = Steps(dve, cw_steps)
            dve.wait_ge(exps, 2)
            z, inv, w1, w2, over, scale = (cw[:, n] for n in range(6))
            cs.link(v.tensor_reduce(z, ex[:].rearrange("p (t e) -> p t e", e=E), AX.X, ALU.add))
            cs.link(v.reciprocal(inv, z))
            cs.link(v.tensor_tensor(inv, inv, keep["fits"][:], ALU.mult))
            cs.link(v.tensor_copy(w1, inv))
            cs.link(v.tensor_tensor(w2, inv, ex2[:], ALU.mult))
            cs.link(v.tensor_scalar(over, keep["fits"][:], -1.0, 1.0, ALU.mult, ALU.add))
            cs.link(v.tensor_tensor(scale, w1, w2, ALU.add))
            cs.link(v.tensor_scalar(scale, scale, 1.0, None, ALU.add))
            cs.link(v.tensor_tensor(scale, scale, keep["rstd"][:], ALU.mult))

            ys = Steps(dve, y_steps)
            unit = [0]

            def value(i, b, k):
                return k if i is None else count(i, b, UNITS, k, HEAD_UNITS)

            def reduce(i, b, n):
                j, t, c = MAXES[n]
                w = min(CH, (t + 1) * P - c * CH)
                for h in range(HG):
                    dve.wait_ge(max_made, value(i, b, unit[0] + 1))
                    v.tensor_reduce(tops[j % 2][:, h, t % TC, c:c + 1], p_m[unit[0] % 2][:, 0:w], AX.X, ALU.max
                                    ).then_inc(max_read, 1)
                    unit[0] += 1
                if n in ENDS:
                    dve.wait_ge(max_read, value(i, b, unit[0]))
                    v.tensor_reduce(neg_top[j % 2][:, 0:HG * TC], tops[j % 2][:, :, :, 0:j + 1].rearrange(
                        "p h t c -> p (h t) c"), AX.X, ALU.max, negate=True).then_inc(neg_ready, 1)

            def turn(i, b, j):
                dve.wait_ge(max_made, value(i, b, unit[0] + 1))
                if i is not None:
                    dve.wait_ge(top_stored[(j - 2) % CPB], count(i, b, TOPS, TOPS))
                top = p_m[unit[0] % 2][0:HG * TC, 0:P]
                ys.link(v.tensor_copy(top_part[0][j % 2][:], top))
                v.tensor_tensor(top_part[1][j % 2][:], top, top_part[0][j % 2][:], ALU.subtract).then_inc(max_read, 1)
                unit[0] += 1

            def keep_y(i, b, j):
                dve.wait_ge(pv_done, count(i, b, S, ENDS[j] + 1, CREDIT))
                dve.wait_ge(y_stored[j % 2], i * (16 * B * CPB // 2) + (16 * (b * CPB // 2 + j // 2) + CREDIT))
                v.tensor_copy(y[j % 2][:], p_y[j % 2][:]).then_inc(y_ready, 1)

            for n in range(LAG):
                reduce(None, 0, n)
                if n - 1 in ENDS:
                    turn(None, 0, MAXES[n - 1][0])

            def group(i, b, follows):
                unit[0] = 0
                for s, n, own in lead(follows):
                    if n is not None:
                        if n < S:
                            reduce(i, b, n)
                        if turns_at(n, own):
                            turn(i, b, MAXES[(n - 1) % S][0])
                    if s - 3 in ENDS:
                        keep_y(i, b, STEPS[s - 3][0])
                keep_y(i, b, CPB - 1)

            with dve.Fori(0, NG - 1) as i:
                ys.enter(i, B * CPB)
                for b in range(B):
                    group(i, b, True)
            ys.leave(NG - 1)
            for b in range(B):
                group(NG - 1, b, b == 0)

        @block.tensor
        def _(pe):
            open_up(pe, pv_done)
            t_ = nc.tensor
            unit = [0]

            def value(i, b, k):
                return k if i is None else count(i, b, UNITS, k, HEAD_UNITS)

            def bank_free(i, b):
                if i is not None or unit[0] >= 2:
                    pe.wait_ge(max_read, value(i, b, unit[0] - 1))

            def maxima(i, b, n, bb, h):
                j, t, c = MAXES[n]
                w = min(CH, (t + 1) * P - c * CH)
                diagonal = c == j
                bank_free(i, b)
                out = p_m[unit[0] % 2]
                mm = t_.matmul(out[:, 0:w], qs[bb][0:KS, h, t * P:(t + 1) * P], ks[bb][0:KS, h, c * CH:c * CH + w],
                               start=True, stop=not diagonal)
                if diagonal:
                    mm = t_.matmul(out[:, w - P:w], ident_b[:], hide_q[:], start=False, stop=True)
                mm.then_inc(max_made, 1)
                unit[0] += 1

            def turn(i, b, j, nth):
                bank_free(i, b)
                pe.wait_ge(neg_ready, nth)
                t_.transpose(p_m[unit[0] % 2][:, 0:P], neg_top[j % 2][:], ident_f[:]).then_inc(max_made, 1)
                unit[0] += 1

            def scores(i, b, s, r):
                j, k = STEPS[s]
                skip = P * max(k - TC * j, 0)
                diagonal = k >= TC * j
                pe.wait_ge(p_ready, count(i, b, 2 * S, 2 * (s - 1) + r + 1 if b or s else 0, CREDIT))
                for hh in range(2):
                    h = 2 * r + hh
                    mm = t_.matmul(p_s[r][:, hh, 0:CH - skip], ks[b][:, h, k * P:(k + 1) * P],
                                   qs[b][:, h, j * CH + skip:(j + 1) * CH], start=True, stop=not diagonal)
                    if diagonal:
                        mm = t_.matmul(p_s[r][:, hh, 0:P], ident_b[:], hide_k[:], start=False, stop=True)
                mm.then_inc(s_made, 1)

            def values(i, b, s):
                j, k = STEPS[s]
                skip = P * max(k - TC * j, 0)
                pe.wait_ge(p_ready, count(i, b, 2 * S, 2 * s + 2, CREDIT))
                if k == 0:
                    pe.wait_ge(y_ready, count(i, b, CPB, j - 1 if b or j else 0, CREDIT))
                for h in range(HG):
                    mm = t_.matmul(p_y[j % 2][h * R:(h + 1) * R, skip:CH], vs[b][:, k, h * R:(h + 1) * R],
                                   probs[s % 3][:, h, 0:CH - skip], start=(k == 0), stop=(s in ENDS))
                mm.then_inc(pv_done, 1)

            pe.wait_ge(c_loaded, 16 * 4)
            pe.wait_ge(rows_set, 4)
            pe.wait_ge(in_loaded[0], 16 * LOADS)
            for n in range(LAG):
                for h in range(HG):
                    maxima(None, 0, n, 0, h)
                if n - 1 in ENDS:
                    turn(None, 0, MAXES[n - 1][0], MAXES[n - 1][0] + 1)

            def group(i, b, follows):
                unit[0] = 0
                for s, n, own in lead(follows):
                    bb = b if own else 1 - b
                    leads = n is not None and n < S
                    if n == 0:
                        pe.wait_ge(in_loaded[bb], i * (16 * LOADS) + 16 * LOADS * (b + 1 if bb == 0 else 1))
                    if STEPS[s][1] == 0:
                        pe.wait_ge(top_stored[STEPS[s][0]], count(i, b, TOPS, TOPS))
                    for r in range(2):
                        if leads:
                            maxima(i, b, n, bb, r)
                        scores(i, b, s, r)
                    if leads:
                        maxima(i, b, n, bb, 2)
                    if s >= 2:
                        values(i, b, s - 2)
                    if leads:
                        maxima(i, b, n, bb, 3)
                    if n is not None and turns_at(n, own):
                        j = MAXES[(n - 1) % S][0]
                        turn(i, b, j, count(i, b, CPB, {2: 1, 3: 2, 0: 3, 1: 4}[j], HEAD_TURNS))
                values(i, b, S - 2)
                values(i, b, S - 1)

            groups(pe, group)


def finish(nc, a, keep):
    with ExitStack() as ctx:
        def sb(name, shape, dt=F32):
            return ctx.enter_context(nc.sbuf_tensor(name, shape, dt))

        def sem(name):
            return ctx.enter_context(nc.semaphore(name))

        TB = 4
        wo = sb("wo", [P, KD, D])
        bo = sb("bo", [1, D])
        ones = sb("ones_f", [1, P])
        yt = sb("yt_in", [P, KD, N])
        sums = sb("sums", [P, H * N // P])
        inv = sb("inv_sums", [P, H * N // P])
        inv_wide = [sb(f"inv_wide{r}", [P, KD, TB * P]) for r in range(3)]
        gate = [sb(f"gate{r}", [P, TB, D]) for r in range(2)]
        x_all, mix = keep["x"], keep["mix"]
        p_o = [ctx.enter_context(nc.psum_tensor(f"p_o{r}", [P, TB, D], F32)) for r in range(2)]

        w_in = sem("w_in")
        yt_in = [sem(f"yt_in{n}") for n in range(2)]
        sums_in = sem("sums_in")
        inv_ready = sem("inv_ready")
        inv_stored = sem("inv_stored")
        inv_in = [sem(f"inv_in{r}") for r in range(3)]
        y_ready = sem("y_ready_f")
        ones_set = sem("ones_set_f")
        gate_ready = sem("gate_ready")
        proj_made = sem("proj_made")
        scaled = sem("scaled")
        summed = sem("summed")
        out_stored = sem("out_stored_f")
        block = ctx.enter_context(nc.Block())
        NS = NT // TB

        @block.sync
        def _(sp):
            R = 2 * HD
            by_head = a["yt"].rearrange("(h r) n -> h r n", r=R)
            C = P // H
            for h in range(H):
                sp.dma_start(sums[h * C:(h + 1) * C, :],
                             by_head[h, HD:HD + 1, :].rearrange("o (c n) -> (o c) n", c=C)).then_inc(sums_in, 16)
            sp.dma_start(wo[:], a["woT"].rearrange("(k p) o -> p k o", p=P)).then_inc(w_in, 16)
            sp.dma_start(bo[:], a["bo"]).then_inc(w_in, 16)
            HK = H // KD
            for n in range(2):
                for k in range(KD):
                    sp.dma_start(yt[:, k, n * N // 2:(n + 1) * N // 2],
                                 by_head[k * HK:(k + 1) * HK, 0:HD, n * N // 2:(n + 1) * N // 2]).then_inc(yt_in[n], 16)
            sp.wait_ge(inv_ready, 1)
            sp.dma_start(a["inv"], inv[:]).then_inc(inv_stored, 16)
            sp.wait_ge(inv_stored, 16)
            inv_rows = a["inv"].rearrange("(h c) n -> h (c n)", h=H)

            def widen(s):
                for k in range(KD):
                    sp.dma_start(inv_wide[s % 3][:, k], inv_rows[k * HK:(k + 1) * HK, s * TB * P:(s + 1) * TB * P]
                                 .unsqueeze(1).broadcast_to([HK, HD, TB * P])).then_inc(inv_in[s % 3], 16)

            for s in range(3):
                widen(s)
            for s in range(NS):
                if s + 3 < NS:
                    sp.wait_ge(y_ready, s + 1)
                    widen(s + 3)
                sp.wait_ge(summed, s + 1)
                sp.dma_start(a["out"][s * TB * P:(s + 1) * TB * P].rearrange("(t p) d -> p t d", p=P),
                             mix[:, s * TB:(s + 1) * TB]).then_inc(out_stored, 16)
            sp.wait_ge(out_stored, 16 * NS)

        @block.tensor
        def _(pe):
            t_ = nc.tensor
            pe.wait_ge(w_in, 32)
            pe.wait_ge(ones_set, 1)
            for s in range(NS):
                pe.wait_ge(y_ready, s + 1)
                if s >= 2:
                    pe.wait_ge(scaled, s - 1)
                for t in range(TB):
                    tile = s * TB + t
                    for k in range(KD):
                        t_.matmul(p_o[s % 2][:, t], yt[:, k, tile * P:(tile + 1) * P], wo[:, k], start=(k == 0), stop=False)
                    mm = t_.matmul(p_o[s % 2][:, t], ones[:], bo[:], start=False, stop=True)
                mm.then_inc(proj_made, 1)

        @block.scalar
        def _(act):
            for s in range(NS):
                cur = slice(s * TB, (s + 1) * TB)
                if s >= 2:
                    act.wait_ge(scaled, s - 1)
                nc.scalar.activation(gate[s % 2][:], mix[:, cur], ACT.Silu).then_inc(gate_ready, 1)

        @block.vector
        def _(dve):
            v = nc.vector
            v.memset(ones[:], 1.0).then_inc(ones_set, 1)
            dve.wait_ge(sums_in, 16 * H)
            v.reciprocal(inv[:], sums[:]).then_inc(inv_ready, 1)

            def normalise(s):
                if s % (NS // 2) == 0:
                    dve.wait_ge(yt_in[s // (NS // 2)], 16 * KD)
                dve.wait_ge(inv_in[s % 3], 16 * KD * (s // 3 + 1))
                cur = yt[:, :, s * TB * P:(s + 1) * TB * P]
                v.tensor_tensor(cur, cur, inv_wide[s % 3][:], ALU.mult).then_inc(y_ready, 1)

            normalise(0)
            for s in range(NS):
                cur = slice(s * TB, (s + 1) * TB)
                if s + 1 < NS:
                    normalise(s + 1)
                dve.wait_ge(gate_ready, s + 1)
                dve.wait_ge(proj_made, s + 1)
                v.tensor_tensor(mix[:, cur], p_o[s % 2][:], gate[s % 2][:], ALU.mult).then_inc(scaled, 1)

        @block.gpsimd
        def _(pool):
            for s in range(NS):
                cur = slice(s * TB, (s + 1) * TB)
                pool.wait_ge(scaled, s + 1)
                nc.gpsimd.tensor_tensor(mix[:, cur], mix[:, cur], x_all[:, cur], ALU.add).then_inc(summed, 1)


def build(nc, a):
    with ExitStack() as ctx:
        def sb(name, shape, dt=F32):
            return ctx.enter_context(nc.sbuf_tensor(name, shape, dt))

        keep = {
            "logits": sb("logits", [P, NT * E]), "below": sb("below", [P, NT * E]),
            "mean": sb("mean", [P, NT]), "rstd": sb("rstd", [P, NT]), "second": sb("second", [P, NT]),
            "fits": sb("fits", [P, NT]), "fetch": sb("fetch", [P, 2, NT], I32),
        }
        normalise_route_project(nc, a, keep)
        run_experts(nc, a, keep)
        keep["x"], keep["mix"] = sb("x_kept", [P, NT, D]), sb("mix", [P, NT, D])
        attend(nc, a, keep)
        finish(nc, a, keep)


SCRATCH = {
    "xth": (P, KD, N), "xtl": (P, KD, N), "qk0": (2, KD, P, N), "qk1": (2, KD, P, N), "qk2": (2, KD, P, N),
    "v": (N, H * 2 * HD), "fd": (N, D), "xb": (2 * SLOTS, D), "ob": (SLOTS, D), "yt": (2 * D, N), "inv": (P, H * N // P),
}


def tables():
    import numpy as np
    theta = (1.0 / np.float32(10000.0) ** (np.arange(0, HD, 2, dtype=np.float32) / np.float32(HD))).astype(np.float32)
    angle = np.arange(1, T + 1, dtype=np.float32)[None, :] * np.tile(theta, P // (HD // 2))[:, None]
    sign = np.where(np.arange(P) % HD < HD // 2, -1.0, 1.0).astype(np.float32)
    row, col = np.arange(P)[:, None], np.arange(P)[None, :]
    bf16 = mybir.dt.np(BF16)
    tok = np.arange(NT)[None, None, :] * P + np.arange(P)[:, None, None]
    return {
        "cos": np.cos(angle).astype(np.float32), "sin": (np.sin(angle) * sign[:, None]).astype(np.float32),
        "ident": np.eye(P, dtype=np.float32), "ident_b": np.eye(P).astype(bf16),
        "tri": (row < col).astype(bf16), "ones_b": np.ones((P, P), bf16),
        "hide_after_row": np.where(col > row, NEG, 0.0).astype(bf16),
        "hide_before_row": np.where(col < row, NEG, 0.0).astype(bf16),
        "idx_m": np.tile(np.arange(E, dtype=np.float32) - E, (P, NT)),
        "runs": np.tile((np.arange(NT * E) % NT != 0).astype(np.float32), (P, 1)),
        "trash": (SLOTS + 2 * tok + np.arange(2)[None, :, None]).astype(np.float32),
    }


def laid_out(i):
    import numpy as np
    c = np.ascontiguousarray
    i = {k: np.asarray(v) for k, v in i.items()}
    col = lambda v: c(v.reshape(KD, P).T)
    return {
        "x": c(i["L0_attn_x"].reshape(N, D)),
        "wqT": c(i["L0_attn_Wq"].T), "wkT": c(i["L0_attn_Wk"].T), "wvT": c(i["L0_attn_Wv"].T), "woT": c(i["L0_attn_Wo"].T),
        "bq": col(i["L0_attn_bq"]), "bk": col(i["L0_attn_bk"]),
        "bv": c(i["L0_attn_bv"][None, :]), "bo": c(i["L0_attn_bo"][None, :]),
        "wr": i["L0_ffn_Wr"], "normw": c(i["L0_ffn_norm_w"].reshape(E, KD, P).transpose(0, 2, 1)),
        "wg": i["L0_ffn_Wg"], "wu": i["L0_ffn_Wu"], "wd": i["L0_ffn_Wd"],
        "fnorm": col(i["L0_ffn_f_norm"]), "fwg": i["L0_ffn_fWg"], "fwu": i["L0_ffn_fWu"], "fwd": i["L0_ffn_fWd"],
    }


def kernel(**inputs):
    import numpy as np
    import concourse.bacc as bacc
    from concourse.bass_utils import run_bass_kernel_spmd

    nc = bacc.Bacc("TRN2", target_bir_lowering=False, num_devices=1)
    arrays, a = {}, {}
    for name, v in {**laid_out(inputs), **tables()}.items():
        v = np.ascontiguousarray(v)
        arrays["in_" + name] = v
        a[name] = nc.dram_tensor("in_" + name, v.shape, mybir.dt.from_np(v.dtype), kind="ExternalInput").ap()
    for name, shape in SCRATCH.items():
        a[name] = nc.dram_tensor(name, shape, BF16 if name.startswith("qk") else F32).ap()
    a["out"] = nc.dram_tensor("out", (N, D), F32, kind="ExternalOutput").ap()
    build(nc, a)
    r = run_bass_kernel_spmd(nc, [arrays], core_ids=[0])
    return r.results[0]["out"].reshape(B, T, D)
```

```python
import math
from contextlib import ExitStack

import concourse.bass as bass
from concourse import mybir

F32 = mybir.dt.float32
F32R = mybir.dt.float32r
BF16 = mybir.dt.bfloat16
I32 = mybir.dt.int32
ALU = mybir.AluOpType
ACT = mybir.ActivationFunctionType
AX = mybir.AxisListType

P = 128
B, T, D = 2, 2048, 256
N = B * T
NT = N // P
CH = 512
TC = CH // P
CPB = T // CH
KD = D // P
H, HD = 16, 16
HG = 4
NG = H // HG
E, F, CAP = 8, 512, 1024
F4 = F // 4
KF = F // P
SLOTS = E * CAP
PAIRS = ((0, 0), (0, 1), (0, 2), (1, 0), (1, 1), (2, 0))
KS = len(PAIRS) * HD
KM = KS + 2
R = 2 * HD
WW = 2 * KD * F + KF * D
LN_EPS, RMS_EPS = 1e-5, 1e-6
NEG = -3.0e38


CREDIT = 1


def open_up(eng, *sems):
    for s in sems:
        eng.sem_inc(s, CREDIT)


class Steps:

    def __init__(self, eng, sem):
        self.eng, self.sem, self.k, self.base, self.per, self.i = eng, sem, 0, 0, 0, None

    def mark(self, ins):
        ins.then_inc(self.sem, 1)
        self.k += 1
        return self.k

    def wait(self, k=None):
        k = self.k if k is None else k
        self.eng.wait_ge(self.sem, self.base + k if self.i is None else self.i * self.per + (self.base + k))

    def link(self, ins):
        self.mark(ins)
        self.wait()

    def enter(self, i, per):
        self.base, self.k, self.per, self.i = self.base + self.k, 0, per, i

    def leave(self, turns):
        assert self.k == self.per, (self.k, self.per)
        self.base, self.k, self.per, self.i = self.base + turns * self.per, 0, 0, None


def three_products(pe, out, weights, moving, first, last):
    terms = [(0, 0), (0, 1), (1, 0)]
    for n, (a, b) in enumerate(terms):
        mm = pe.matmul(out, weights[a], moving[b], start=first and n == 0, stop=last and n == 2)
    return mm


def normalise_route_project(nc, a, keep):
    with ExitStack() as ctx:
        def sb(name, shape, dt=F32):
            return ctx.enter_context(nc.sbuf_tensor(name, shape, dt))

        def ps(name, shape, dt=F32):
            return ctx.enter_context(nc.psum_tensor(name, shape, dt))

        def sem(name):
            return ctx.enter_context(nc.semaphore(name))

        xr_all = keep["store"][:].rearrange("p (t d) -> p t d", d=D)
        mv = sb("mv", [P, NT, 2])
        small = sb("small", [P, 6, NT])
        ident = sb("ident1", [P, P])
        wqkv = sb("wqkv", [P, 3, KD, D])
        wqkv_h = sb("wqkv_h", [P, 3, KD, D], F32R)
        wqkv_l = sb("wqkv_l", [P, 3, KD, D], F32R)
        wf = sb("wf", [P, 2, KD, F4])
        wf_h = sb("wf_h", [P, 2, KD, F4], F32R)
        wf_l = sb("wf_l", [P, 2, KD, F4], F32R)
        wfd = sb("wfd", [P, D])
        wfd_h = sb("wfd_h", [P, D], F32R)
        wfd_l = sb("wfd_l", [P, D], F32R)
        wr = sb("wr", [P, KD, E])
        wr_h = sb("wr_h", [P, KD, E], F32R)
        wr_l = sb("wr_l", [P, KD, E], F32R)
        bqk = sb("bqk", [P, 2, KD])
        bqs = sb("bqs", [P, 2, KD])
        bv = sb("bv", [1, D])
        bv_h = sb("bv_h", [1, D], F32R)
        bv_l = sb("bv_l", [1, D], F32R)
        ones_row = sb("ones_row", [1, P])
        ones_rowr = sb("ones_rowr", [1, P], F32R)
        fnorm = sb("fnorm", [P, KD])
        zeros = sb("zeros", [P, 1, D])
        cos = sb("cos", [P, T])
        sin = sb("sin", [P, T])

        idx_m = sb("idx_m", [P, NT * E])
        runs = sb("runs", [P, NT * E])
        tri = sb("tri", [P, P], BF16)
        ones_b = sb("ones_b", [P, P], BF16)
        trash = sb("trash", [P, 2, NT])

        x_loaded = [sem(f"x_loaded{c}") for c in range(4)]
        w_loaded = sem("w_loaded")
        consts_loaded = sem("consts_loaded")
        zeros_set = sem("zeros_set")
        xb_zeroed = sem("xb_zeroed")
        w_high = sem("w_high")
        w_split = sem("w_split")
        stats_sqrt = sem("stats_sqrt")
        dve_steps = sem("dve_steps1")
        var_ready = sem("var_ready")
        ms_ready = sem("ms_ready")
        rr_ready = sem("rr_ready")
        xn_ready = sem("xn_ready")
        xt_turned = sem("xt_turned")
        xt_high = sem("xt_high")
        xt_low = sem("xt_low")
        xt_high_stored = [sem(f"xt_high_stored{u}") for u in range(2)]
        xt_low_stored = [sem(f"xt_low_stored{u}") for u in range(2)]
        lt_zeroed = sem("lt_zeroed")
        routed = sem("routed")
        routed_kept = sem("routed_kept")
        logits_made = sem("logits_made")
        wr_loaded = sem("wr_loaded")
        angles_loaded = sem("angles_loaded")
        xr_ready = sem("xr_ready")
        rc_loaded = sem("rc_loaded")

        x_t = a["x"].rearrange("(t p) d -> p t d", p=P)
        WLOADS = 10

        with ExitStack() as c1:
            xn = [c1.enter_context(nc.sbuf_tensor(f"xn{u}", [P, TC, D], F32)) for u in range(2)]
            xh = [c1.enter_context(nc.sbuf_tensor(f"xh{u}", [P, KD, CH], F32R)) for u in range(2)]
            xl = [c1.enter_context(nc.sbuf_tensor(f"xl{u}", [P, KD, CH], F32R)) for u in range(2)]
            p_xt = [c1.enter_context(nc.psum_tensor(f"p_xt{u}", [P, KD, CH], F32)) for u in range(2)]
            lt = [c1.enter_context(nc.sbuf_tensor(f"lt{u}", [P, CH], F32)) for u in range(2)]
            p_lt = [c1.enter_context(nc.psum_tensor(f"p_lt{u}", [E, CH], F32)) for u in range(2)]
            p_lg = c1.enter_context(nc.psum_tensor("p_lg", [P, CH], F32))
            x_all = c1.enter_context(nc.sbuf_tensor("x_all", [P, NT, D], F32))
            stats = c1.enter_context(nc.sbuf_tensor("stats", [P, NT, 6], F32))
            CHUNKS = N // CH
            ZR = SLOTS // CHUNKS

            def chunks(eng, turn):
                with eng.Fori(0, CHUNKS // 2 - 1) as i:
                    for u in range(2):
                        turn(i, u, True)
                for u in range(2):
                    turn(CHUNKS // 2 - 1, u, u == 0)

            block = c1.enter_context(nc.Block())

            @block.sync
            def _(sp):
                open_up(sp, *xt_high_stored, *xt_low_stored)
                for c in range(4):
                    n = NT // 4
                    sp.dma_start(x_all[:, c * n:(c + 1) * n, :], x_t[:, c * n:(c + 1) * n, :]).then_inc(x_loaded[c], 16)
                sp.dma_start(ident[:], a["ident"]).then_inc(consts_loaded, 16)
                sp.dma_start(wr[:], a["wr"].rearrange("(k p) e -> p k e", p=P)).then_inc(wr_loaded, 16)
                for n, w in enumerate(("wqT", "wkT", "wvT")):
                    sp.dma_start(wqkv[:, n], a[w].rearrange("(k p) o -> p k o", p=P)).then_inc(w_loaded, 16)
                for n, w in enumerate(("fwg", "fwu")):
                    sp.dma_start(wf[:, n], a[w].rearrange("(k p) o -> p k o", p=P)).then_inc(w_loaded, 16)
                sp.dma_start(wfd[:], a["fwd"]).then_inc(w_loaded, 16)
                for n, w in enumerate(("bq", "bk")):
                    sp.dma_start(bqk[:, n], a[w]).then_inc(w_loaded, 16)
                sp.dma_start(bv[:], a["bv"]).then_inc(w_loaded, 16)
                sp.dma_start(fnorm[:], a["fnorm"]).then_inc(w_loaded, 16)
                for dst, src in ((idx_m, "idx_m"), (runs, "runs"), (tri, "tri"), (ones_b, "ones_b"), (trash, "trash")):
                    sp.dma_start(dst[:], a[src]).then_inc(rc_loaded, 16)
                def zero(first):
                    sp.dma_start(a["xb"][bass.ds(first, ZR), :].rearrange("(p r) d -> p r d", p=P),
                                 zeros[:].broadcast_to([P, ZR // P, D])).then_inc(xb_zeroed, 16)

                sp.wait_ge(zeros_set, 1)
                for c in range(CHUNKS // 2):
                    zero(c * ZR)
                with sp.Fori(0, NT // TC // 2) as i:
                    for u in range(2):
                        at = bass.ds(i * (2 * CH) + u * CH, CH)
                        sp.wait_ge(xt_high, i * 2 + (u + 1))
                        sp.dma_start(a["xth"][:, :, at], xh[u][:].bitcast(F32)).then_inc(xt_high_stored[u], 16)
                        sp.wait_ge(xt_low, i * 2 + (u + 1 + CREDIT))
                        sp.dma_start(a["xtl"][:, :, at], xl[u][:].bitcast(F32)).then_inc(xt_low_stored[u], 16)
                    zero(i * ZR + SLOTS // 2)
                sp.dma_start(cos[:], a["cos"]).then_inc(angles_loaded, 16)
                sp.dma_start(sin[:], a["sin"]).then_inc(angles_loaded, 16)
                for u in range(2):
                    sp.wait_ge(xt_high_stored[u], 16 * (NT // TC // 2) + CREDIT)
                    sp.wait_ge(xt_low_stored[u], 16 * (NT // TC // 2) + CREDIT)

            @block.gpsimd
            def _(pool):
                nc.gpsimd.memset(zeros[:], 0.0).then_inc(zeros_set, 1)
                pool.wait_ge(rr_ready, 1)
                for t in range(NT):
                    nc.gpsimd.tensor_scalar(xr_all[:, t], x_all[:, t], keep["mean"][:, t:t + 1], small[:, 5, t:t + 1],
                                            ALU.subtract, ALU.mult).then_inc(xr_ready, 1)
                pool.wait_ge(xr_ready, NT)

            @block.scalar
            def _(act):
                open_up(act, routed_kept)
                act.wait_ge(var_ready, 1)
                nc.scalar.activation(small[:, 1], small[:, 0], ACT.Sqrt).then_inc(stats_sqrt, 1)
                act.wait_ge(ms_ready, 1)
                nc.scalar.activation(small[:, 4], small[:, 3], ACT.Sqrt).then_inc(stats_sqrt, 1)
                act.wait_ge(wr_loaded, 16)
                nc.scalar.copy(wr_h[:], wr[:]).then_inc(w_high, 1)
                act.wait_ge(w_loaded, 16 * WLOADS)
                for h, w in ((wqkv_h, wqkv), (wf_h, wf), (wfd_h, wfd), (bv_h, bv)):
                    nc.scalar.copy(h[:], w[:]).then_inc(w_high, 1)
                act.wait_ge(lt_zeroed, 2)

                def turn(i, u, follows):
                    act.wait_ge(xt_turned, i * 2 + (u + 1 + CREDIT))
                    act.wait_ge(xt_high_stored[u], i * 16 + CREDIT)
                    act.wait_ge(routed, i * 2 + (max(u - 1, 0) + CREDIT))
                    nc.scalar.copy(xh[u][:], p_xt[u][:]).then_inc(xt_high, 1)
                    act.wait_ge(routed, i * 2 + (u + 1 + CREDIT))
                    act.wait_ge(logits_made, i * 2 + (max(u - 1, 0) + CREDIT))
                    nc.scalar.copy(lt[u][0:E, :], p_lt[u][:]).then_inc(routed_kept, 1)

                chunks(act, turn)

            @block.vector
            def _(dve):
                open_up(dve, xt_low)
                v = nc.vector
                st = Steps(dve, dve_steps)
                for u in range(2):
                    v.memset(lt[u][:], 0.0).then_inc(lt_zeroed, 1)
                for c in range(4):
                    dve.wait_ge(x_loaded[c], 16)
                    for t in range(c * NT // 4, (c + 1) * NT // 4):
                        st.mark(v.bn_stats(stats[:, t, :], x_all[:, t, :]))
                st.wait()
                for t in range(NT):
                    st.mark(v.bn_aggr(mv[:, t, :], stats[:, t, :]))
                st.wait()
                var = mv[:, :, 1:2].rearrange("p t o -> p (t o)")
                mean = mv[:, :, 0:1].rearrange("p t o -> p (t o)")
                st.mark(v.tensor_copy(keep["mean"][:], mean))
                v.tensor_scalar(small[:, 0], var, LN_EPS, None, ALU.add).then_inc(var_ready, 1)

                def inverse_root(out, value, root, scratch):
                    st.link(v.reciprocal(out, root))
                    st.link(v.tensor_tensor(scratch, out, out, ALU.mult))
                    st.link(v.tensor_tensor(scratch, scratch, value, ALU.mult))
                    st.link(v.tensor_scalar(scratch, scratch, -0.5, 1.5, ALU.mult, ALU.add))
                    st.link(v.tensor_tensor(out, out, scratch, ALU.mult))

                dve.wait_ge(stats_sqrt, 1)
                dve.wait_ge(var_ready, 1)
                rstd, rr = keep["rstd"], small[:, 5]
                inverse_root(rstd[:], small[:, 0], small[:, 1], small[:, 2])
                st.link(v.tensor_tensor(small[:, 2], rstd[:], rstd[:], ALU.mult))
                st.link(v.tensor_tensor(small[:, 2], small[:, 2], var, ALU.mult))
                v.tensor_scalar(small[:, 3], small[:, 2], RMS_EPS, None, ALU.add).then_inc(ms_ready, 1)
                dve.wait_ge(ms_ready, 1)
                dve.wait_ge(stats_sqrt, 2)
                inverse_root(rr, small[:, 3], small[:, 4], small[:, 2])
                v.tensor_tensor(rr, rr, rstd[:], ALU.mult).then_inc(rr_ready, 1)
                def normalise(i, c):
                    for t in range(TC):
                        tile = i * (2 * TC) + (c * TC + t)
                        cur = x_all[:, bass.ds(tile, 1), :].rearrange("p a d -> p (a d)")
                        v.tensor_scalar(xn[c % 2][:, t, :], cur, keep["mean"][:, bass.ds(tile, 1)],
                                        rstd[:, bass.ds(tile, 1)], ALU.subtract, ALU.mult).then_inc(xn_ready, 1)

                normalise(0, 0)
                for n, (w, h, low) in enumerate(((wr, wr_h, wr_l), (wqkv, wqkv_h, wqkv_l), (wf, wf_h, wf_l),
                                                 (wfd, wfd_h, wfd_l), (bv, bv_h, bv_l))):
                    dve.wait_ge(w_high, n + 1)
                    v.tensor_tensor(low[:], w[:], h[:].bitcast(F32), ALU.subtract).then_inc(w_split, 1)
                v.memset(ones_row[:], 1.0).then_inc(w_split, 1)
                dve.wait_ge(w_split, 6)
                v.tensor_copy(ones_rowr[:], ones_row[:]).then_inc(w_split, 1)
                v.tensor_scalar(bqs[:, 0], bqk[:, 0], 1.0 / math.sqrt(HD), None, ALU.mult).then_inc(w_split, 1)
                v.tensor_copy(bqs[:, 1], bqk[:, 1]).then_inc(w_split, 1)

                def turn(i, u, follows):
                    if follows:
                        dve.wait_ge(xt_turned, i * 2 + (u + CREDIT))
                        normalise(i, u + 1)
                    dve.wait_ge(xt_high, i * 2 + (u + 1))
                    dve.wait_ge(xt_low_stored[u], i * 16 + CREDIT)
                    dve.wait_ge(routed, i * 2 + (max(u - 1, 0) + CREDIT))
                    v.tensor_tensor(xl[u][:], p_xt[u][:], xh[u][:].bitcast(F32), ALU.subtract).then_inc(xt_low, 1)

                chunks(dve, turn)
                dve.wait_ge(logits_made, CHUNKS + CREDIT)
                st.link(v.tensor_copy(keep["logits"][:], p_lg[:, 0:NT * E]))

            @block.tensor
            def _(pe):
                open_up(pe, xt_turned, routed, logits_made)
                t_ = nc.tensor
                pe.wait_ge(consts_loaded, 16)
                pe.wait_ge(w_split, 1)

                def transpose(i, c):
                    u = c % 2
                    pe.wait_ge(xn_ready, i * (2 * TC) + TC * (c + 1))
                    for k in range(KD):
                        for t in range(TC):
                            mm = t_.transpose(p_xt[u][:, k, t * P:(t + 1) * P], xn[u][:, t, k * P:(k + 1) * P], ident[:])
                    mm.then_inc(xt_turned, 1)

                transpose(0, 0)

                def turn(i, u, follows):
                    if follows:
                        pe.wait_ge(xt_low, i * 2 + (u + CREDIT))
                        transpose(i, u + 1)
                    pe.wait_ge(xt_low, i * 2 + (u + 1 + CREDIT))
                    pe.wait_ge(routed_kept, i * 2 + (max(u - 1, 0) + CREDIT))
                    for k in range(KD):
                        mm = three_products(t_, p_lt[u][:], (wr_h[:, k], wr_l[:, k]), (xh[u][:, k], xl[u][:, k]),
                                            k == 0, k == KD - 1)
                    mm.then_inc(routed, 1)
                    pe.wait_ge(routed_kept, i * 2 + (u + 1 + CREDIT))
                    for t in range(TC):
                        mm = t_.matmul(p_lg[:, bass.ds(i * (2 * TC * E) + (u * TC + t) * E, E)],
                                       lt[u][:, t * P:(t + 1) * P], ident[:, 0:E], start=True, stop=True)
                    mm.then_inc(logits_made, 1)

                chunks(pe, turn)

        xh = [sb(f"xh_in{u}", [P, KD, CH], F32R) for u in range(2)]
        xl = [sb(f"xl_in{u}", [P, KD, CH], F32R) for u in range(2)]
        xr = [sb(f"xr_in{u}", [P, TC, D]) for u in range(2)]
        v_out = [sb(f"v_out{u}", [P, TC, H, 2 * HD]) for u in range(2)]
        qf = [sb(f"qf{s}", [P, CH]) for s in range(2)]
        turned = [sb(f"turned{s}", [P, CH]) for s in range(2)]
        with_cos = [sb(f"with_cos{s}", [P, CH]) for s in range(2)]
        with_sin = [sb(f"with_sin{s}", [P, CH]) for s in range(2)]
        q = [sb(f"q{s}", [P, CH]) for s in range(2)]
        q_rest = [sb(f"q_rest{s}", [P, CH]) for s in range(2)]
        q_part = [[sb(f"q_part{m}{s}", [P, CH], BF16) for s in range(2)] for m in range(3)]
        fr_h = sb("fr_h", [P, KD, CH], F32R)
        fr_l = sb("fr_l", [P, KD, CH], F32R)
        gelu = sb("gelu", [P, CH])
        hid = sb("hid", [P, CH])
        hid_h = sb("hid_h", [P, CH], F32R)
        hid_l = sb("hid_l", [P, CH], F32R)
        f_out = sb("f_out", [P, TC, D])
        rt = sb("rt", [P, 10, NT * E])
        taken = sb("taken", [P, NT * E], BF16)
        pick = sb("pick", [P, 12, NT])
        pair = sb("pair", [P, 4, 2, NT])
        send = sb("send", [P, 2, NT], I32)

        p_qk = [ps(f"p_qk{s}", [P, CH]) for s in range(2)]
        p_vd = [ps(f"p_vd{s}", [P, 2, D]) for s in range(2)]
        p_fr = ps("p_fr", [P, KD, CH])
        p_g = ps("p_g", [P, CH])
        p_u = ps("p_u", [P, CH])

        x_in = [sem(f"x_in{u}") for u in range(2)]
        ones_set = sem("ones_set")
        taken_ready = sem("taken_ready")
        counted = sem("counted")
        counts_read = sem("counts_read")
        send_ready = sem("send_ready")
        sent = sem("sent")
        fr_turned = sem("fr_turned")
        fr_high = sem("fr_high")
        fr_low = sem("fr_low")
        qk_made = sem("qk_made")
        qf_ready = sem("qf_ready")
        qf_used = sem("qf_used")
        q_ready = sem("q_ready")
        q_rest_ready = sem("q_rest_ready")
        q_part_ready = [sem(f"q_part_ready{m}") for m in range(3)]
        q_stored = [[sem(f"q_stored{m}{s}") for s in range(2)] for m in range(3)]
        gu_made = sem("gu_made")
        gelu_ready = sem("gelu_ready")
        hid_ready = sem("hid_ready")
        hid_high = sem("hid_high")
        hid_low = sem("hid_low")
        v_made = sem("v_made")
        v_kept = sem("v_kept")
        v_stored = [sem(f"v_stored{u}") for u in range(2)]
        down_made = sem("down_made")
        down_kept = sem("down_kept")
        down_stored = sem("down_stored")
        rope_steps = sem("rope_steps")

        block = ctx.enter_context(nc.Block())

        @block.sync
        def _(sp):
            open_up(sp, *q_stored[0], *q_stored[1], *q_stored[2], *v_stored, down_stored)
            def load(i, n, u):
                tok = bass.ds(i * CH + (n * CH + u * T), CH)
                sp.dma_start(xh[u][:].bitcast(F32), a["xth"][:, :, tok]).then_inc(x_in[u], 16)
                sp.dma_start(xl[u][:].bitcast(F32), a["xtl"][:, :, tok]).then_inc(x_in[u], 16)
                sp.dma_start(xr[u][:], xr_all[:, bass.ds(i * TC + (n * TC + u * (T // P)), TC), :]).then_inc(x_in[u], 16)

            for u in range(2):
                load(0, 0, u)
            load_weights(sp, a, keep["w_first"], 0, 0, keep["w_first_loaded"])

            def turn(i, follows):
                for u in range(2):
                    tok = bass.ds(i * CH + u * T, CH)
                    pairs = bass.ds(i * (CH // 2) + u * (T // 2), CH // 2)
                    for n in range(2 * KD):
                        w, k = divmod(n, KD)
                        piece = i * 8 + (4 * u + n + 1 + CREDIT)
                        for m in range(3):
                            sp.wait_ge(q_part_ready[m], piece)
                            sp.dma_start(a[f"qk{m}"][w, k].rearrange("p (n two) -> p n two", two=2)[:, pairs],
                                         q_part[m][n % 2][:].rearrange("p (n two) -> p n two", two=2)).then_inc(q_stored[m][n % 2], 16)
                    sp.wait_ge(v_kept, i * 4 + (2 * u + 2))
                    sp.dma_start(a["v"][tok, :].rearrange("(t p) c -> p t c", p=P),
                                 v_out[u][:].rearrange("p t h c -> p t (h c)")).then_inc(v_stored[u], 16)
                    if follows:
                        load(i, 1, u)
                    sp.wait_ge(down_kept, i * 4 + (2 * u + 2 + CREDIT))
                    sp.dma_start(a["fd"][tok, :].rearrange("(t p) c -> p t c", p=P), f_out[:]).then_inc(down_stored, 16)

            with sp.Fori(0, CPB - 1) as i:
                turn(i, True)
            turn(CPB - 1, False)
            for s in range(2):
                for m in range(3):
                    sp.wait_ge(q_stored[m][s], 16 * 2 * 2 * CPB + CREDIT)
                sp.wait_ge(v_stored[s], 16 * CPB + CREDIT)
            sp.wait_ge(down_stored, 16 * 2 * CPB + CREDIT)

        @block.gpsimd
        def _(pool):
            open_up(pool, q_part_ready[2])
            for u in range(2):
                nc.gpsimd.memset(v_out[u][:], 1.0).then_inc(ones_set, 1)
            pool.wait_ge(send_ready, 1)
            pool.wait_ge(xb_zeroed, 16 * (N // CH))
            sends = [(k, t) for k in range(2) for t in range(NT)]
            pieces = 2 * KD * 2 * CPB
            for m in range(pieces):
                for k, t in sends[m * len(sends) // pieces:(m + 1) * len(sends) // pieces]:
                    nc.gpsimd.indirect_dma_start(
                        a["xb"], bass.IndirectOffsetOnAxis(ap=send[:, k, t:t + 1], axis=0), xr_all[:, t, :],
                        None).then_inc(sent, 16)
                pool.wait_ge(q_part_ready[1], m + 1 + CREDIT)
                pool.wait_ge(q_stored[2][m % 2], 16 * (m // 2) + CREDIT)
                nc.gpsimd.tensor_tensor(q_part[2][m % 2][:], q_rest[m % 2][:], q_part[1][m % 2][:],
                                        ALU.subtract).then_inc(q_part_ready[2], 1)
            pool.wait_ge(sent, 16 * 2 * NT)

        @block.scalar
        def _(act):
            open_up(act, qf_ready, q_part_ready[0], q_part_ready[1], down_kept)
            s_ = nc.scalar
            act.wait_ge(ones_set, 2)
            s_.activation(gelu[:, 0:1], bqs[:, 0, 0:1], ACT.Gelu)
            with act.Fori(0, CPB) as i:
                for u in range(2):
                    def bias(n):
                        w, k = divmod(n, KD)
                        act.wait_ge(qk_made, i * 8 + (4 * u + n + 1))
                        if n >= 2:
                            act.wait_ge(qf_used, i * 8 + (4 * u + n - 1 + CREDIT))
                        else:
                            act.wait_ge(qf_used, i * 8 + (4 * u + CREDIT))
                        s_.activation(qf[n % 2][:], p_qk[n % 2][:], ACT.Identity, bias=bqs[:, w, k:k + 1],
                                      scale=1.0 / math.sqrt(HD) if w == 0 else 1.0).then_inc(qf_ready, 1)

                    def first(n):
                        act.wait_ge(q_ready, i * 8 + (4 * u + n + 1))
                        act.wait_ge(q_stored[0][n % 2], i * (16 * 4) + (16 * (2 * u + n // 2) + CREDIT))
                        s_.copy(q_part[0][n % 2][:], q[n % 2][:]).then_inc(q_part_ready[0], 1)

                    def second(n, u=u):
                        act.wait_ge(q_rest_ready, i * 8 + (4 * u + n + 1 + CREDIT))
                        act.wait_ge(q_stored[1][n % 2], i * (16 * 4) + (16 * (2 * u + n // 2) + CREDIT))
                        s_.copy(q_part[1][n % 2][:], q_rest[n % 2][:]).then_inc(q_part_ready[1], 1)

                    def values(n):
                        act.wait_ge(v_made, i * 4 + (2 * u + n + 1))
                        act.wait_ge(v_stored[u], i * 16 + CREDIT)
                        s_.copy(v_out[u][:, 2 * n:2 * n + 2, :, 0:HD],
                                p_vd[n][:].rearrange("p t (h c) -> p t h c", c=HD)).then_inc(v_kept, 1)

                    act.wait_ge(fr_turned, i * 2 + (u + 1))
                    act.wait_ge(gu_made, i * 2 + (u + CREDIT))
                    for k in range(KD):
                        s_.activation(fr_h[:, k], p_fr[:, k], ACT.Identity, scale=fnorm[:, k:k + 1]).then_inc(fr_high, 1)
                    bias(0)
                    if u == 1:
                        second(3, u=0)
                    bias(1)
                    first(0)
                    act.wait_ge(gu_made, i * 2 + (u + 1 + CREDIT))
                    act.wait_ge(hid_ready, i * 2 + (u + CREDIT))
                    s_.activation(gelu[:], p_g[:], ACT.Gelu).then_inc(gelu_ready, 1)
                    first(1)
                    bias(2)
                    second(0)
                    act.wait_ge(hid_ready, i * 2 + (u + 1 + CREDIT))
                    act.wait_ge(down_made, i * 4 + (2 * u + CREDIT))
                    s_.copy(hid_h[:], hid[:]).then_inc(hid_high, 1)
                    second(1)
                    bias(3)
                    values(0)
                    first(2)
                    values(1)
                    second(2)
                    first(3)
                    if u == 1:
                        second(3)
                    for n in range(2):
                        act.wait_ge(down_made, i * 4 + (2 * u + n + 1 + CREDIT))
                        act.wait_ge(down_stored, i * 32 + (16 * u + CREDIT))
                        s_.copy(f_out[:, 2 * n:2 * n + 2, :], p_vd[n][:]).then_inc(down_kept, 1)

        @block.vector
        def _(dve):
            open_up(dve, qf_used, q_rest_ready, fr_low, hid_ready, hid_low)
            v = nc.vector
            st = Steps(dve, rope_steps)
            mask = [(j // HD) * HD + (j % HD + HD // 2) % HD for j in range(32)]

            def te(ap):
                return ap.rearrange("p (t e) -> p t e", e=E)

            def et(ap):
                return ap.rearrange("p (e t) -> p t e", e=E)

            def wide(ap):
                return ap.unsqueeze(2).broadcast_to([P, NT, E])

            lg, idx = te(keep["logits"][:]), te(idx_m[:])
            dve.wait_ge(rc_loaded, 16 * 5)
            best, second = pick[:, 0], pick[:, 1]
            st.link(v.tensor_reduce(best, lg, AX.X, ALU.max))
            below = te(rt[:, 0])
            st.link(v.tensor_tensor(below, lg, wide(best), ALU.subtract))

            def one_hot(out, values, top, scratch, low):
                st.link(v.tensor_tensor(scratch, values, wide(top), ALU.is_equal))
                st.link(v.tensor_tensor(scratch, scratch, idx, ALU.mult))
                st.link(v.tensor_reduce(low, scratch, AX.X, ALU.min))
                st.link(v.tensor_tensor(out, idx, wide(low), ALU.is_equal))

            hot1, hot2, scratch, rest = te(rt[:, 1]), te(rt[:, 2]), te(rt[:, 3]), te(rt[:, 4])
            one_hot(hot1, lg, best, scratch, pick[:, 2])
            st.link(v.scalar_tensor_tensor(out=rt[:, 4], in0=rt[:, 1], scalar=NEG, in1=rt[:, 0],
                                           op0=ALU.mult, op1=ALU.add))
            st.link(v.tensor_reduce(second, rest, AX.X, ALU.max))
            one_hot(hot2, rest, second, scratch, pick[:, 3])
            v.tensor_tensor(taken[:].rearrange("p (e t) -> p t e", e=E), hot1, hot2, ALU.add).then_inc(taken_ready, 1)
            dve.wait_ge(counted, 1)
            st.link(v.tensor_copy(rt[:, 5], p_u[:, 0:NT * E]))
            st.link(v.tensor_tensor_scan(rt[:, 6], runs[:], rt[:, 5], 0.0, ALU.mult, ALU.add))
            st.link(v.tensor_tensor(rt[:, 6], rt[:, 6], rt[:, 5], ALU.subtract))
            v.tensor_tensor(rt[:, 7], p_g[:, 0:NT * E], rt[:, 6], ALU.add).then_inc(counts_read, 1)
            dve.wait_ge(counts_read, 1)
            place, expert, kept, slot = pair[:, 0], pair[:, 1], pair[:, 2], pair[:, 3]
            for k, hot in enumerate((hot1, hot2)):
                st.link(v.tensor_tensor(scratch, hot, et(rt[:, 7]), ALU.mult))
                st.link(v.tensor_reduce(place[:, k], scratch, AX.X, ALU.add))
            st.link(v.tensor_scalar(expert, pick[:, 2:4], float(E), float(CAP), ALU.add, ALU.mult))
            st.link(v.tensor_scalar(kept, place, float(CAP), None, ALU.is_lt))
            st.link(v.tensor_scalar(slot, place, float(CAP - 1), None, ALU.min))
            st.link(v.tensor_tensor(slot, slot, expert, ALU.add))
            st.link(v.tensor_copy(keep["fetch"][:], slot))
            st.link(v.tensor_tensor(slot, slot, trash[:], ALU.subtract))
            st.link(v.tensor_tensor(slot, slot, kept, ALU.mult))
            st.link(v.tensor_tensor(slot, slot, trash[:], ALU.add))
            v.tensor_copy(send[:], slot).then_inc(send_ready, 1)
            st.link(v.tensor_tensor(keep["fits"][:], kept[:, 0], kept[:, 1], ALU.mult))
            st.link(v.tensor_copy(keep["second"][:], second))
            st.link(v.tensor_copy(keep["below"][:], rt[:, 0]))

            dve.wait_ge(angles_loaded, 32)
            with dve.Fori(0, CPB) as i:
                st.enter(i, 2 * (2 * KD * 2))
                for u in range(2):
                    pos = bass.ds(i * CH, CH)

                    def rope(n):
                        dve.wait_ge(qf_ready, i * 8 + (4 * u + n + 1 + CREDIT))
                        st.mark(v.tensor_tensor(with_cos[n % 2][:], qf[n % 2][:], cos[:, pos], ALU.mult))
                        v.stream_shuffle(turned[n % 2][:], qf[n % 2][:], mask).then_inc(qf_used, 1)
                        dve.wait_ge(qf_used, i * 8 + (4 * u + n + 1 + CREDIT))
                        st.mark(v.tensor_tensor(with_sin[n % 2][:], turned[n % 2][:], sin[:, pos], ALU.mult))
                        st.wait()
                        dve.wait_ge(q_rest_ready, i * 8 + (4 * u + max(n - 1, 0) + CREDIT))
                        v.tensor_tensor(q[n % 2][:], with_cos[n % 2][:], with_sin[n % 2][:], ALU.add).then_inc(q_ready, 1)

                    def rest(n):
                        dve.wait_ge(q_part_ready[0], i * 8 + (4 * u + n + 1 + CREDIT))
                        dve.wait_ge(q_part_ready[2], i * 8 + (4 * u + max(n - 1, 0) + CREDIT))
                        v.tensor_tensor(q_rest[n % 2][:], q[n % 2][:], q_part[0][n % 2][:],
                                        ALU.subtract).then_inc(q_rest_ready, 1)

                    dve.wait_ge(gu_made, i * 2 + (u + CREDIT))
                    for k in range(KD):
                        dve.wait_ge(fr_high, i * 4 + (2 * u + k + 1))
                        v.scalar_tensor_tensor(out=fr_l[:, k], in0=p_fr[:, k], scalar=fnorm[:, k:k + 1],
                                               in1=fr_h[:, k].bitcast(F32), op0=ALU.mult,
                                               op1=ALU.subtract).then_inc(fr_low, 1)
                    rope(0)
                    rope(1)
                    rest(0)
                    dve.wait_ge(gelu_ready, i * 2 + (u + 1))
                    dve.wait_ge(hid_low, i * 2 + (u + CREDIT))
                    v.tensor_tensor(hid[:], p_u[:], gelu[:], ALU.mult).then_inc(hid_ready, 1)
                    rest(1)
                    rope(2)
                    dve.wait_ge(hid_high, i * 2 + (u + 1))
                    dve.wait_ge(down_made, i * 4 + (2 * u + CREDIT))
                    v.tensor_tensor(hid_l[:], hid[:], hid_h[:].bitcast(F32), ALU.subtract).then_inc(hid_low, 1)
                    rope(3)
                    rest(2)
                    rest(3)
            st.leave(CPB)

        @block.tensor
        def _(pe):
            open_up(pe, gu_made, down_made)
            t_ = nc.tensor
            pe.wait_ge(rc_loaded, 16 * 5)
            pe.wait_ge(taken_ready, 1)
            t_.matmul(p_g[:, 0:NT * E], tri[:], taken[:], start=True, stop=True)
            t_.matmul(p_u[:, 0:NT * E], ones_b[:], taken[:], start=True, stop=True).then_inc(counted, 1)
            pe.wait_ge(counts_read, 1)
            with pe.Fori(0, CPB) as i:
                for u in range(2):
                    xx = [(xh[u][:, k], xl[u][:, k]) for k in range(KD)]

                    def piece(n):
                        w, k = divmod(n, KD)
                        if n >= 2:
                            pe.wait_ge(qf_ready, i * 8 + (4 * u + n - 1 + CREDIT))
                        else:
                            pe.wait_ge(qf_ready, i * 8 + (4 * u + CREDIT))
                        out = slice(k * P, (k + 1) * P)
                        for c in range(KD):
                            mm = three_products(t_, p_qk[n % 2][:], (wqkv_h[:, w, c, out], wqkv_l[:, w, c, out]),
                                                xx[c], c == 0, c == KD - 1)
                        mm.then_inc(qk_made, 1)

                    pe.wait_ge(x_in[u], i * 48 + 48)
                    pe.wait_ge(fr_low, i * 4 + (2 * u + CREDIT))
                    for k in range(KD):
                        for t in range(TC):
                            mm = t_.transpose(p_fr[:, k, t * P:(t + 1) * P], xr[u][:, t, k * P:(k + 1) * P], ident[:])
                    mm.then_inc(fr_turned, 1)
                    piece(0)
                    piece(1)
                    pe.wait_ge(fr_low, i * 4 + (2 * u + 2 + CREDIT))
                    pe.wait_ge(hid_ready, i * 2 + (u + CREDIT))
                    for m, out in enumerate((p_g, p_u)):
                        for c in range(KD):
                            mm = three_products(t_, out[:], (wf_h[:, m, c], wf_l[:, m, c]), (fr_h[:, c], fr_l[:, c]),
                                                c == 0, c == KD - 1)
                    mm.then_inc(gu_made, 1)
                    piece(2)
                    piece(3)
                    for n in range(2):
                        pe.wait_ge(down_kept, i * 4 + (2 * u + CREDIT))
                        for t in range(2):
                            tok = slice((2 * n + t) * P, (2 * n + t + 1) * P)
                            for c in range(KD):
                                three_products(t_, p_vd[n][:, t], (xx[c][0][:, tok], xx[c][1][:, tok]),
                                               (wqkv_h[:, 2, c], wqkv_l[:, 2, c]), c == 0, False)
                            t_.matmul(p_vd[n][:, t], ones_rowr[:], bv_h[:], start=False, stop=False)
                            mm = t_.matmul(p_vd[n][:, t], ones_rowr[:], bv_l[:], start=False, stop=True)
                        mm.then_inc(v_made, 1)
                    pe.wait_ge(hid_low, i * 2 + (u + 1 + CREDIT))
                    for n in range(2):
                        pe.wait_ge(v_kept, i * 4 + (2 * u + n + 1))
                        for t in range(2):
                            tok = slice((2 * n + t) * P, (2 * n + t + 1) * P)
                            mm = three_products(t_, p_vd[n][:, t], (hid_h[:, tok], hid_l[:, tok]),
                                                (wfd_h[:], wfd_l[:]), True, True)
                        mm.then_inc(down_made, 1)


def load_weights(sp, a, w, i, n, sem):
    e = bass.ds(i * 2 + n, 1)
    for m, name in enumerate(("wg", "wu")):
        sp.dma_start(w[:, m * KD * F:(m + 1) * KD * F].rearrange("p (k f) -> p k f", k=KD),
                     a[name][e].rearrange("e (k p) f -> p (e k) f", p=P)).then_inc(sem, 16)
    sp.dma_start(w[:, 2 * KD * F:].rearrange("p (k d) -> p k d", k=KF),
                 a["wd"][e].rearrange("e (k p) d -> p (e k) d", p=P)).then_inc(sem, 16)


def run_experts(nc, a, keep):
    with ExitStack() as ctx:
        def sb(name, shape, dt=F32):
            return ctx.enter_context(nc.sbuf_tensor(name, shape, dt))

        def ps(name, shape, dt=F32):
            return ctx.enter_context(nc.psum_tensor(name, shape, dt))

        def sem(name):
            return ctx.enter_context(nc.semaphore(name))

        RT = CAP // P
        RC = CAP // CH
        ident = sb("ident2", [P, P])
        rows = [sb(f"rows{u}", [P, RT, D]) for u in range(2)]
        w = [keep["w_first"], sb("w1", [P, WW])]
        w_h = [sb(f"w_h{u}", [P, WW], F32R) for u in range(2)]
        w_l = [sb(f"w_l{u}", [P, WW], F32R) for u in range(2)]
        nw = [sb(f"nw{u}", [P, KD]) for u in range(2)]
        xt_h = [sb(f"xt_h{c}", [P, KD, CH], F32R) for c in range(RC)]
        xt_l = [sb(f"xt_l{c}", [P, KD, CH], F32R) for c in range(RC)]
        gelu = [sb(f"gelu_e{s}", [P, CH]) for s in range(2)]
        hid = [sb(f"hid_e{s}", [P, CH]) for s in range(2)]
        hid_h = [sb(f"hid_eh{c}", [P, KF, CH], F32R) for c in range(RC)]
        hid_l = [sb(f"hid_el{c}", [P, KF, CH], F32R) for c in range(RC)]
        e_out = sb("e_out", [P, RT, D])

        p_t = ps("p_t", [P, KD, CH])
        p_g = [ps(f"p_eg{s}", [P, CH]) for s in range(2)]
        p_u = [ps(f"p_eu{s}", [P, CH]) for s in range(2)]
        p_d = [ps(f"p_d{s}", [P, 2, D]) for s in range(2)]

        id_loaded = sem("id_loaded")
        rows_loaded = [sem(f"rows_loaded{u}") for u in range(2)]
        w_loaded = [keep["w_first_loaded"], sem("w_loaded_e1")]
        w_high = sem("w_high_e")
        w_low = sem("w_low_e")
        turned = sem("turned_e")
        xt_high = sem("xt_high_e")
        xt_low = sem("xt_low_e")
        gu_made = sem("gu_made_e")
        gelu_ready = sem("gelu_ready_e")
        hid_ready = sem("hid_ready_e")
        hid_high = sem("hid_high_e")
        hid_low = sem("hid_low_e")
        down_made = sem("down_made_e")
        down_kept = sem("down_kept_e")
        out_stored = sem("out_stored_e")
        block = ctx.enter_context(nc.Block())

        GU, DN = RC * KF, RT // 2

        def count(i, e, per, k, head=0):
            return i * (2 * per) + (head + e * per + k)

        def pairs(eng, pair):
            with eng.Fori(0, E // 2 - 1) as i:
                pair(i, E)
            pair(E // 2 - 1, 2)

        @block.sync
        def _(sp):
            open_up(sp, out_stored)
            sp.dma_start(ident[:], a["ident"]).then_inc(id_loaded, 16)

            def load(i, n, u, weights=True):
                e = i * 2 + n
                sp.dma_start(rows[u][:], a["xb"][bass.ds(i * (2 * CAP) + n * CAP, CAP), :].rearrange("(t p) d -> p t d", p=P)
                             ).then_inc(rows_loaded[u], 16)
                sp.dma_start(nw[u][:], a["normw"][bass.ds(e, 1)].rearrange("e p k -> p (e k)")
                             ).then_inc(rows_loaded[u], 16)
                if weights:
                    load_weights(sp, a, w[u], i, n, w_loaded[u])

            load(0, 0, 0, weights=False)
            load(0, 1, 1)

            def pair(i, left):
                if left == 2:
                    load_heads(sp, a, keep["heads"], keep["heads_loaded"], 0, 0, 0)
                for u in range(2):
                    if u + 2 < left:
                        sp.wait_ge(w_low, count(i, u, 2, 2, CREDIT))
                        sp.wait_ge(xt_low, count(i, u, RC, RC, CREDIT))
                        load(i, u + 2, u)
                    sp.wait_ge(down_kept, count(i, u, DN, DN, CREDIT))
                    sp.dma_start(a["ob"][bass.ds(i * (2 * CAP) + u * CAP, CAP), :].rearrange("(t p) d -> p t d", p=P),
                                 e_out[:]).then_inc(out_stored, 16)

            pairs(sp, pair)
            sp.wait_ge(out_stored, 16 * E + CREDIT)

        @block.gpsimd
        def _(pool):
            open_up(pool, w_low)
            with pool.Fori(0, E // 2) as i:
                for u in range(2):
                    pool.wait_ge(w_high, count(i, u, 1, 1))
                    for cols in (slice(0, 2 * KD * F), slice(2 * KD * F, WW)):
                        nc.gpsimd.tensor_tensor(w_l[u][:, cols], w[u][:, cols], w_h[u][:, cols].bitcast(F32),
                                                ALU.subtract).then_inc(w_low, 1)

        @block.scalar
        def _(act):
            open_up(act, down_kept)
            s_ = nc.scalar

            def rows_high(i, e, c):
                act.wait_ge(turned, count(i, e, RC, c + 1))
                act.wait_ge(gu_made, count(i, e, GU, 0, CREDIT))
                for k in range(KD):
                    s_.activation(xt_h[c][:, k], p_t[:, k], ACT.Identity, scale=nw[e % 2][:, k:k + 1]).then_inc(xt_high, 1)

            act.wait_ge(w_loaded[0], 48)
            s_.copy(w_h[0][:], w[0][:]).then_inc(w_high, 1)
            for c in range(RC):
                rows_high(0, 0, c)
            act.wait_ge(w_loaded[1], 48)
            s_.copy(w_h[1][:], w[1][:]).then_inc(w_high, 1)

            def pair(i, left):
                for u in range(2):
                    for n in range(GU + 1):
                        if n < GU:
                            act.wait_ge(gu_made, count(i, u, GU, n + 1, CREDIT))
                            act.wait_ge(hid_ready, count(i, u, GU, max(n - 1, 0), CREDIT))
                            s_.activation(gelu[n % 2][:], p_g[n % 2][:], ACT.Gelu).then_inc(gelu_ready, 1)
                        if n:
                            c, f = divmod(n - 1, KF)
                            act.wait_ge(hid_ready, count(i, u, GU, n, CREDIT))
                            act.wait_ge(down_made, count(i, u, DN, 0, CREDIT))
                            s_.copy(hid_h[c][:, f], hid[(n - 1) % 2][:]).then_inc(hid_high, 1)
                    for n in range(DN):
                        if n % 2 == 0 and u + 1 < left:
                            rows_high(i, u + 1, n // 2)
                        act.wait_ge(down_made, count(i, u, DN, n + 1, CREDIT))
                        act.wait_ge(out_stored, count(i, u, 16, 0, CREDIT))
                        s_.copy(e_out[:, 2 * n:2 * n + 2, :], p_d[n % 2][:]).then_inc(down_kept, 1)
                    if u + 2 < left:
                        act.wait_ge(w_loaded[u], i * 48 + 96)
                        s_.copy(w_h[u][:], w[u][:]).then_inc(w_high, 1)

            pairs(act, pair)

        @block.vector
        def _(dve):
            open_up(dve, xt_low, hid_ready, hid_low)
            v = nc.vector

            def rows_low(i, e, c):
                dve.wait_ge(xt_high, count(i, e, 2 * RC, 2 * c + 2))
                for k in range(KD):
                    ins = v.scalar_tensor_tensor(out=xt_l[c][:, k], in0=p_t[:, k], scalar=nw[e % 2][:, k:k + 1],
                                                 in1=xt_h[c][:, k].bitcast(F32), op0=ALU.mult, op1=ALU.subtract)
                ins.then_inc(xt_low, 1)

            for c in range(RC):
                rows_low(0, 0, c)

            def pair(i, left):
                for u in range(2):
                    for n in range(GU + 1):
                        if n < GU:
                            dve.wait_ge(gelu_ready, count(i, u, GU, n + 1))
                            dve.wait_ge(hid_low, count(i, u, GU, max(n - 1, 0), CREDIT))
                            v.tensor_tensor(hid[n % 2][:], p_u[n % 2][:], gelu[n % 2][:], ALU.mult).then_inc(hid_ready, 1)
                        if n:
                            c, f = divmod(n - 1, KF)
                            dve.wait_ge(hid_high, count(i, u, GU, n))
                            v.tensor_tensor(hid_l[c][:, f], hid[(n - 1) % 2][:], hid_h[c][:, f].bitcast(F32),
                                            ALU.subtract).then_inc(hid_low, 1)
                    if u + 1 < left:
                        for c in range(RC):
                            rows_low(i, u + 1, c)

            pairs(dve, pair)

        @block.tensor
        def _(pe):
            open_up(pe, gu_made, down_made)
            t_ = nc.tensor

            def turn(i, e, c):
                if c == 0:
                    pe.wait_ge(rows_loaded[e % 2], i * 32 + 32 * (e // 2 + 1))
                pe.wait_ge(xt_low, count(i, e, RC, c, CREDIT))
                for k in range(KD):
                    for t in range(TC):
                        mm = t_.transpose(p_t[:, k, t * P:(t + 1) * P], rows[e % 2][:, c * TC + t, k * P:(k + 1) * P], ident[:])
                mm.then_inc(turned, 1)

            pe.wait_ge(id_loaded, 16)
            for c in range(RC):
                turn(0, 0, c)

            def pair(i, left):
                for u in range(2):
                    wg = [(w_h[u][:, k * F:(k + 1) * F], w_l[u][:, k * F:(k + 1) * F]) for k in range(2 * KD)]
                    wd = [(w_h[u][:, 2 * KD * F + k * D:2 * KD * F + (k + 1) * D],
                           w_l[u][:, 2 * KD * F + k * D:2 * KD * F + (k + 1) * D]) for k in range(KF)]
                    pe.wait_ge(w_low, count(i, u, 2, 1, CREDIT))
                    for n in range(GU):
                        c, f = divmod(n, KF)
                        if f == 0:
                            pe.wait_ge(xt_low, count(i, u, RC, c + 1, CREDIT))
                        pe.wait_ge(hid_ready, count(i, u, GU, max(n - 1, 0), CREDIT))
                        for m, out in enumerate((p_g, p_u)):
                            for k in range(KD):
                                mm = three_products(
                                    t_, out[n % 2][:], tuple(x[:, f * P:(f + 1) * P] for x in wg[m * KD + k]),
                                    (xt_h[c][:, k], xt_l[c][:, k]), k == 0, k == KD - 1)
                        mm.then_inc(gu_made, 1)
                    pe.wait_ge(w_low, count(i, u, 2, 2, CREDIT))
                    for n in range(DN):
                        if n % 2 == 0 and u + 1 < left:
                            turn(i, u + 1, n // 2)
                        c, t0 = divmod(2 * n, TC)
                        pe.wait_ge(hid_low, count(i, u, GU, KF * (c + 1), CREDIT))
                        pe.wait_ge(down_kept, count(i, u, DN, max(n - 1, 0), CREDIT))
                        for t in range(2):
                            tok = slice((t0 + t) * P, (t0 + t + 1) * P)
                            for k in range(KF):
                                mm = three_products(t_, p_d[n % 2][:, t], (hid_h[c][:, k, tok], hid_l[c][:, k, tok]),
                                                    wd[k], k == 0, k == KF - 1)
                        mm.then_inc(down_made, 1)

            pairs(pe, pair)


def load_heads(sp, a, into, sem, i, hg, b):
    for w, dst in enumerate(into):
        for n, pair in enumerate(PAIRS):
            src = a[f"qk{pair[w]}"][w].rearrange("k p n -> (k p) n")
            src = src[bass.ds(i * (HG * HD) + hg * (HG * HD), HG * HD), b * T:(b + 1) * T]
            src = src.rearrange("(h d) n -> d h n", d=HD)
            if w == 1:
                sp.dma_start(dst[n * HD:(n + 1) * HD], src).then_inc(sem, 16)
            else:
                for c in range(CPB):
                    sp.dma_start(dst[n * HD:(n + 1) * HD, c], src[:, :, c * CH:(c + 1) * CH]).then_inc(sem, 16)


def late_in(sp, a, sums, b, sem):
    by_head = a["yt"][(NG - 1) * HG * 2 * HD:, b * T:(b + 1) * T].rearrange("(h r) n -> h r n", r=2 * HD)
    C = P // HG
    for h in range(HG):
        sp.dma_start(sums[h * C:(h + 1) * C, :],
                     by_head[h, HD:HD + 1, :].rearrange("o (c n) -> (o c) n", c=C)).then_inc(sem, 16)


def late_out(sp, a, inv, b, sem):
    C = P // HG
    for h in range(HG):
        sp.dma_start(a["inv"][H - HG + h:H - HG + h + 1, b * T:(b + 1) * T].rearrange("o (c n) -> (o c) n", c=C),
                     inv[h * C:(h + 1) * C, :]).then_inc(sem, 16)


def step_in(sp, a, y, inv, s, sem):
    HK = H // KD
    by_head = a["yt"].rearrange("(h r) n -> h r n", r=R)
    for k in range(KD):
        heads, tokens = slice(k * HK, (k + 1) * HK), slice(s * CH, (s + 1) * CH)
        sp.dma_start(y[:, k], by_head[heads, 0:HD, tokens]).then_inc(sem, 16)
        sp.dma_start(inv[:, k], a["inv"][heads, tokens].unsqueeze(1).broadcast_to([HK, HD, CH])).then_inc(sem, 16)


def attend(nc, a, keep):
    with ExitStack() as ctx:
        def sb(name, shape, dt=F32):
            return ctx.enter_context(nc.sbuf_tensor(name, shape, dt))

        def ps(name, shape, dt=F32):
            return ctx.enter_context(nc.psum_tensor(name, shape, dt))

        def sem(name):
            return ctx.enter_context(nc.semaphore(name))

        LAG = 20
        STEPS = [(j, i) for j in range(CPB) for i in range(TC * (j + 1))]
        MAXES = [(j, TC * j + r, c) for j in range(CPB) for r in range(TC) for c in range(j + 1)]
        S = len(STEPS)
        assert S == len(MAXES)
        ENDS = [n for n in range(S) if n == S - 1 or MAXES[n + 1][0] != MAXES[n][0]]
        assert ENDS == [n for n in range(S) if n == S - 1 or STEPS[n + 1][0] != STEPS[n][0]]
        HEAD_TURNS = sum(e + 1 < LAG for e in ENDS)
        HEAD_UNITS = HG * LAG + HEAD_TURNS
        UNITS = HG * S + CPB

        q0, k0 = keep["heads"]
        qs = [q0, sb("qs1", [KM, CPB, HG, CH], BF16)]
        ks = [k0, sb("ks1", [KM, HG, T], BF16)]
        vs = [sb(f"vs{b}", [P, T // P, HG * R]) for b in range(B)]
        probs = [sb(f"probs{r}", [P, HG, CH]) for r in range(3)]
        tops = [sb(f"tops{r}", [P, HG, TC, CPB]) for r in range(2)]
        neg_top = [sb(f"neg_top{r}", [P, P]) for r in range(2)]
        top_part = [[sb(f"top_part{m}{r}", [HG * TC, P], BF16) for r in range(2)] for m in range(2)]
        ident_f = sb("ident_f", [P, P])
        ident_b = sb("ident_b", [P, P], BF16)
        hide_q = sb("hide_q", [P, P], BF16)
        hide_k = sb("hide_k", [P, P], BF16)
        y = [sb(f"y{r}", [P, CH]) for r in range(2)]
        early = [sb("early_sums", [(H - HG) * P // H, H * N // P]), sb("early_inv", [(H - HG) * P // H, H * N // P])]
        late = [sb("late_sums", [P, HG * T // P]), sb("late_inv", [P, HG * T // P])]
        x_all, mix = keep["x"], keep["mix"]
        ex = sb("ex", [P, NT * E])
        ex2 = sb("ex2", [P, NT])
        cw = sb("cw", [P, 6, NT])
        got = [[sb(f"got{k}{r}", [P, D]) for r in range(2)] for k in range(2)]
        fall = [sb(f"fall{r}", [P, D]) for r in range(2)]
        part = [sb(f"part{n}", [P, D]) for n in range(3)]

        p_s = [ps(f"p_s{r}", [P, 2, CH]) for r in range(2)]
        MB = 3
        p_m = [ps(f"p_m{r}", [P, CH]) for r in range(MB)]
        p_y = ps("p_y", [P, CH])

        c_loaded = sem("c_loaded")
        rows_set = sem("rows_set")
        in_loaded = [keep["heads_loaded"], sem("in_loaded1")]
        v_loaded = [sem(f"v_loaded{b}") for b in range(B)]
        x_loaded = sem("x_loaded_c")
        max_made = sem("max_made")
        max_read = sem("max_read")
        neg_ready = sem("neg_ready")
        top_stored = [sem(f"top_stored{j}") for j in range(CPB)]
        s_made = sem("s_made")
        p_ready = sem("p_ready")
        pv_done = sem("pv_done")
        y_steps = sem("y_steps")
        y_ready = sem("y_ready")
        y_stored = [sem(f"y_stored{r}") for r in range(2)]
        sums_in = [sem(f"sums_in{n}") for n in range(2)]
        inv_ready = sem("inv_ready")
        inv_stored = sem("inv_stored")
        exps = sem("exps")
        cw_steps = sem("cw_steps")
        got_in = [[sem(f"got_in{k}{r}") for r in range(2)] for k in range(2)]
        fall_in = [sem(f"fall_in{r}") for r in range(2)]
        mix_steps = sem("mix_steps")
        block = ctx.enter_context(nc.Block())

        LOADS = (CPB + 1) * len(PAIRS)

        def count(i, b, per, k, head=0):
            return i * (2 * per) + (head + b * per + k)

        def groups(eng, group):
            with eng.Fori(0, NG - 1) as i:
                for b in range(B):
                    group(i, b, True, False)
            for b in range(B):
                group(NG - 1, b, b == 0, True)

        def lead(follows):
            for s in range(S):
                n = s + LAG
                if n < S:
                    yield s, n, True
                elif follows:
                    yield s, n - S, False
                else:
                    yield s, (S if n == S else None), True

        def turns_at(n, own):
            return (n - 1) % S in ENDS and (n > 0 or not own)

        head_turn, group_turn, unit_now = {}, {}, 0
        for n in range(LAG):
            unit_now += HG
            if n - 1 in ENDS:
                unit_now += 1
                head_turn[MAXES[n - 1][0]] = unit_now
        unit_now = 0
        for s, n, own in lead(True):
            unit_now += HG
            if turns_at(n, own):
                unit_now += 1
                group_turn[MAXES[(n - 1) % S][0]] = unit_now
        TOPS = 16 * 2

        @block.sync
        def _(sp):
            open_up(sp, *y_stored)
            for dst, src in ((ident_f, "ident"), (ident_b, "ident_b"), (hide_q, "hide_after_row"),
                             (hide_k, "hide_before_row")):
                sp.dma_start(dst[:], a[src]).then_inc(c_loaded, 16)

            def load_values(i, hg, b):
                sp.dma_start(vs[b][:], a["v"][b * T:(b + 1) * T, bass.ds(i * (HG * R) + hg * (HG * R), HG * R)]
                             .rearrange("(t p) c -> p t c", p=P)).then_inc(v_loaded[b], 16)

            def load(i, hg, b):
                load_heads(sp, a, (qs[b], ks[b]), in_loaded[b], i, hg, b)
                load_values(i, hg, b)

            def tops_in(b, j, value):
                sp.wait_ge(max_read, value)
                for m in range(2):
                    sp.dma_start(qs[b][KS + m:KS + m + 1, j].rearrange("o h (t n) -> o (h t) n", t=TC),
                                 top_part[m][j % 2][:]).then_inc(top_stored[j], 16)

            def y_out(i, b, j):
                sp.wait_ge(y_ready, count(i, b, CPB, j + 1, CREDIT))
                sp.dma_start(a["yt"][bass.ds(i * (HG * R), HG * R), b * T + j * CH:b * T + (j + 1) * CH],
                             y[j % 2][:]).then_inc(y_stored[j % 2], 16)

            load_values(0, 0, 0)
            sp.dma_start(x_all[:], a["x"].rearrange("(t p) d -> p t d", p=P)).then_inc(x_loaded, 16)
            tops_in(0, 0, head_turn[0])
            tops_in(0, 1, head_turn[1])

            def sums_in_early():
                for r in range(2):
                    sp.wait_ge(y_stored[r], 16 * (CPB // 2) * B * (NG - 1) + CREDIT)
                C = P // H
                for h in range(H - HG):
                    sp.dma_start(early[0][h * C:(h + 1) * C, :], a["yt"][h * R + HD:h * R + HD + 1, :]
                                 .rearrange("o (c n) -> (o c) n", c=C)).then_inc(sums_in[0], 16)

            def sums_in_late():
                for r in range(2):
                    sp.wait_ge(y_stored[r], 16 * (CPB // 2) * (B * (NG - 1) + 1) + CREDIT)
                late_in(sp, a, late[0], 0, sums_in[1])

            def group(i, b, follows, last):
                if follows:
                    sp.wait_ge(pv_done, count(i, b, S, 0, CREDIT))
                    load(i, b, 1 - b)
                if last:
                    (sums_in_early, sums_in_late)[b]()
                tops_in(b, 2, count(i, b, UNITS, group_turn[2], HEAD_UNITS))
                y_out(i, b, 0)
                y_out(i, b, 1)
                if last:
                    sp.wait_ge(inv_ready, b + 1)
                    if b == 0:
                        sp.dma_start(a["inv"][0:(H - HG), :].rearrange("h (c n) -> (h c) n", c=P // H),
                                     early[1][:]).then_inc(inv_stored, 16)
                    else:
                        late_out(sp, a, late[1], 0, inv_stored)
                        sp.wait_ge(inv_stored, 16 * (1 + HG))
                        step_in(sp, a, keep["y_first"], keep["inv_first"], 0, keep["first_in"])
                        sp.dma_start(keep["wo"][:], a["woT"].rearrange("(k p) o -> p k o", p=P)).then_inc(keep["wo_in"], 16)
                        sp.dma_start(keep["bo"][:], a["bo"].broadcast_to([P, D])).then_inc(keep["wo_in"], 16)
                tops_in(b, 3, count(i, b, UNITS, group_turn[3] - (0 if follows else HG), HEAD_UNITS))
                if follows:
                    tops_in(1 - b, 0, count(i, b, UNITS, group_turn[0], HEAD_UNITS))
                y_out(i, b, 2)
                if follows:
                    tops_in(1 - b, 1, count(i, b, UNITS, group_turn[1], HEAD_UNITS))
                y_out(i, b, 3)

            groups(sp, group)
            for r in range(2):
                sp.wait_ge(y_stored[r], 16 * (CPB // 2) * B * NG + CREDIT)

        @block.gpsimd
        def _(pool):
            for n, (rows, what) in enumerate([(t[:], 0.0) for t in neg_top] + [(ks[b][KS:KM], 1.0) for b in range(B)]):
                nc.gpsimd.memset(rows, what).then_inc(rows_set, 1)
                pool.wait_ge(rows_set, n + 1)
            st = Steps(pool, mix_steps)
            fd = a["fd"].rearrange("(t p) d -> t p d", p=P)

            def fetch(t):
                for k in range(2):
                    nc.gpsimd.indirect_dma_start(
                        got[k][t % 2][:], None, a["ob"],
                        bass.IndirectOffsetOnAxis(ap=keep["fetch"][:, k, t:t + 1], axis=0)).then_inc(got_in[k][t % 2], 16)
                nc.gpsimd.dma_start(fall[t % 2][:], fd[t]).then_inc(fall_in[t % 2], 16)

            fetch(0)
            pool.wait_ge(x_loaded, 16)
            pool.wait_ge(cw_steps, 9)
            g = nc.gpsimd
            for t in range(NT):
                if t + 1 < NT:
                    fetch(t + 1)
                st.mark(g.tensor_scalar(mix[:, t], x_all[:, t], keep["mean"][:, t:t + 1], cw[:, 5, t:t + 1],
                                        ALU.subtract, ALU.mult))
                for k in range(2):
                    pool.wait_ge(got_in[k][t % 2], 16 * (t // 2 + 1))
                    st.mark(g.tensor_scalar(part[k][:], got[k][t % 2][:], cw[:, 2 + k, t:t + 1], None, ALU.mult))
                pool.wait_ge(fall_in[t % 2], 16 * (t // 2 + 1))
                st.link(g.tensor_scalar(part[2][:], fall[t % 2][:], cw[:, 4, t:t + 1], None, ALU.mult))
                st.mark(g.tensor_tensor(part[0][:], part[0][:], part[1][:], ALU.add))
                st.link(g.tensor_tensor(mix[:, t], mix[:, t], part[2][:], ALU.add))
                st.link(g.tensor_tensor(mix[:, t], mix[:, t], part[0][:], ALU.add))

        @block.scalar
        def _(act):
            open_up(act, p_ready, y_ready)
            s_ = nc.scalar
            s_.activation(ex[:], keep["below"][:], ACT.Exp).then_inc(exps, 1)
            s_.activation(ex2[:], keep["second"][:], ACT.Exp).then_inc(exps, 1)

            def keep_y(i, b, j):
                act.wait_ge(pv_done, count(i, b, S, ENDS[j] + 1, CREDIT))
                act.wait_ge(y_stored[j % 2], i * (16 * B * CPB // 2) + (16 * (b * CPB // 2 + j // 2) + CREDIT))
                s_.copy(y[j % 2][:], p_y[:]).then_inc(y_ready, 1)

            def group(i, b, follows, last):
                for s, (j, k) in enumerate(STEPS):
                    if s - 3 in ENDS:
                        keep_y(i, b, STEPS[s - 3][0])
                    w = CH - P * max(k - TC * j, 0)
                    act.wait_ge(pv_done, count(i, b, S, max(s - 2, 0), CREDIT))
                    for r in range(2):
                        act.wait_ge(s_made, count(i, b, 2 * S, 2 * s + r + 1))
                        s_.activation(probs[s % 3][:, 2 * r:2 * r + 2, 0:w], p_s[r][:, :, 0:w], ACT.Exp).then_inc(p_ready, 1)
                keep_y(i, b, CPB - 1)

            groups(act, group)

        @block.vector
        def _(dve):
            v = nc.vector
            cs = Steps(dve, cw_steps)
            dve.wait_ge(exps, 2)
            z, inv, w1, w2, over, scale = (cw[:, n] for n in range(6))
            cs.link(v.tensor_reduce(z, ex[:].rearrange("p (t e) -> p t e", e=E), AX.X, ALU.add))
            cs.link(v.reciprocal(inv, z))
            cs.link(v.tensor_tensor(inv, inv, keep["fits"][:], ALU.mult))
            cs.link(v.tensor_copy(w1, inv))
            cs.link(v.tensor_tensor(w2, inv, ex2[:], ALU.mult))
            cs.link(v.tensor_scalar(over, keep["fits"][:], -1.0, 1.0, ALU.mult, ALU.add))
            cs.link(v.tensor_tensor(scale, w1, w2, ALU.add))
            cs.link(v.tensor_scalar(scale, scale, 1.0, None, ALU.add))
            cs.link(v.tensor_tensor(scale, scale, keep["rstd"][:], ALU.mult))

            ys = Steps(dve, y_steps)
            unit = [0]

            def value(i, b, k):
                return k if i is None else count(i, b, UNITS, k, HEAD_UNITS)

            def reduce(i, b, n):
                j, t, c = MAXES[n]
                w = min(CH, (t + 1) * P - c * CH)
                for h in range(HG):
                    dve.wait_ge(max_made, value(i, b, unit[0] + 1))
                    v.tensor_reduce(tops[j % 2][:, h, t % TC, c:c + 1], p_m[unit[0] % MB][:, 0:w], AX.X, ALU.max
                                    ).then_inc(max_read, 1)
                    unit[0] += 1
                if n in ENDS:
                    dve.wait_ge(max_read, value(i, b, unit[0]))
                    v.tensor_reduce(neg_top[j % 2][:, 0:HG * TC], tops[j % 2][:, :, :, 0:j + 1].rearrange(
                        "p h t c -> p (h t) c"), AX.X, ALU.max, negate=True).then_inc(neg_ready, 1)

            def turn(i, b, j):
                dve.wait_ge(max_made, value(i, b, unit[0] + 1))
                if i is not None:
                    dve.wait_ge(top_stored[(j - 2) % CPB], count(i, b, TOPS, TOPS))
                top = p_m[unit[0] % MB][0:HG * TC, 0:P]
                ys.link(v.tensor_copy(top_part[0][j % 2][:], top))
                v.tensor_tensor(top_part[1][j % 2][:], top, top_part[0][j % 2][:], ALU.subtract).then_inc(max_read, 1)
                unit[0] += 1

            for n in range(LAG):
                reduce(None, 0, n)
                if n - 1 in ENDS:
                    turn(None, 0, MAXES[n - 1][0])

            def group(i, b, follows, last):
                unit[0] = 0
                for s, n, own in lead(follows):
                    if n is not None:
                        if n < S:
                            reduce(i, b, n)
                        if turns_at(n, own):
                            turn(i, b, MAXES[(n - 1) % S][0])
                    if last and s == ENDS[1]:
                        dve.wait_ge(sums_in[b], 16 * (H - HG if b == 0 else HG))
                        sums, inverse = late if b else early
                        v.reciprocal(inverse[:], sums[:]).then_inc(inv_ready, 1)

            with dve.Fori(0, NG - 1) as i:
                ys.enter(i, B * CPB)
                for b in range(B):
                    group(i, b, True, False)
            ys.leave(NG - 1)
            for b in range(B):
                group(NG - 1, b, b == 0, True)

        @block.tensor
        def _(pe):
            open_up(pe, pv_done)
            t_ = nc.tensor
            unit = [0]

            def value(i, b, k):
                return k if i is None else count(i, b, UNITS, k, HEAD_UNITS)

            def bank_free(i, b):
                if i is not None or unit[0] >= MB:
                    pe.wait_ge(max_read, value(i, b, max(unit[0] - MB + 1, 0)))

            def maxima(i, b, n, bb, h):
                j, t, c = MAXES[n]
                w = min(CH, (t + 1) * P - c * CH)
                diagonal = c == j
                bank_free(i, b)
                out = p_m[unit[0] % MB]
                mm = t_.matmul(out[:, 0:w], qs[bb][0:KS, j, h, (t % TC) * P:(t % TC + 1) * P], ks[bb][0:KS, h, c * CH:c * CH + w],
                               start=True, stop=not diagonal)
                if diagonal:
                    mm = t_.matmul(out[:, w - P:w], ident_b[:], hide_q[:], start=False, stop=True)
                mm.then_inc(max_made, 1)
                unit[0] += 1

            def turn(i, b, j, nth):
                bank_free(i, b)
                pe.wait_ge(neg_ready, nth)
                t_.transpose(p_m[unit[0] % MB][:, 0:P], neg_top[j % 2][:], ident_f[:]).then_inc(max_made, 1)
                unit[0] += 1

            def scores(i, b, s, h):
                j, k = STEPS[s]
                r, hh = divmod(h, 2)
                skip = P * max(k - TC * j, 0)
                diagonal = k >= TC * j
                if hh == 0:
                    pe.wait_ge(p_ready, count(i, b, 2 * S, 2 * (s - 1) + r + 1 if b or s else 0, CREDIT))
                mm = t_.matmul(p_s[r][:, hh, 0:CH - skip], ks[b][:, h, k * P:(k + 1) * P],
                               qs[b][:, j, h, skip:CH], start=True, stop=not diagonal)
                if diagonal:
                    mm = t_.matmul(p_s[r][:, hh, 0:P], ident_b[:], hide_k[:], start=False, stop=True)
                if hh == 1:
                    mm.then_inc(s_made, 1)

            def values(i, b, s):
                j, k = STEPS[s]
                skip = P * max(k - TC * j, 0)
                pe.wait_ge(p_ready, count(i, b, 2 * S, 2 * s + 2, CREDIT))
                if k == 0:
                    pe.wait_ge(y_ready, count(i, b, CPB, j, CREDIT))
                for h in range(HG):
                    mm = t_.matmul(p_y[h * R:(h + 1) * R, skip:CH], vs[b][:, k, h * R:(h + 1) * R],
                                   probs[s % 3][:, h, 0:CH - skip], start=(k == 0), stop=(s in ENDS))
                mm.then_inc(pv_done, 1)

            pe.wait_ge(c_loaded, 16 * 4)
            pe.wait_ge(rows_set, 2)
            pe.wait_ge(in_loaded[0], 16 * LOADS)
            for n in range(LAG):
                for h in range(HG):
                    maxima(None, 0, n, 0, h)
                if n - 1 in ENDS:
                    turn(None, 0, MAXES[n - 1][0], MAXES[n - 1][0] + 1)

            def group(i, b, follows, last):
                unit[0] = 0
                for s, n, own in lead(follows):
                    bb = b if own else 1 - b
                    leads = n is not None and n < S
                    if n == 0:
                        pe.wait_ge(in_loaded[bb], i * (16 * LOADS) + 16 * LOADS * (b + 1 if bb == 0 else 1))
                    if STEPS[s][1] == 0:
                        pe.wait_ge(top_stored[STEPS[s][0]], count(i, b, TOPS, TOPS))
                    if leads:
                        maxima(i, b, n, bb, 0)
                    scores(i, b, s, 0)
                    scores(i, b, s, 1)
                    if leads:
                        maxima(i, b, n, bb, 1)
                    scores(i, b, s, 2)
                    scores(i, b, s, 3)
                    if leads:
                        maxima(i, b, n, bb, 2)
                    if s == 2:
                        pe.wait_ge(v_loaded[b], i * 16 + 16)
                    if s >= 2:
                        values(i, b, s - 2)
                    if leads:
                        maxima(i, b, n, bb, 3)
                    if n is not None and turns_at(n, own):
                        j = MAXES[(n - 1) % S][0]
                        turn(i, b, j, count(i, b, CPB, {2: 1, 3: 2, 0: 3, 1: 4}[j], HEAD_TURNS))
                values(i, b, S - 2)
                values(i, b, S - 1)

            pe.wait_ge(rows_set, 4)
            groups(pe, group)


def finish(nc, a, keep):
    with ExitStack() as ctx:
        def sb(name, shape, dt=F32):
            return ctx.enter_context(nc.sbuf_tensor(name, shape, dt))

        def sem(name):
            return ctx.enter_context(nc.semaphore(name))

        TB = TC
        wo, bo = keep["wo"], keep["bo"]
        RING = 4
        yt = [keep["y_first"]] + [sb(f"y_in{r}", [P, KD, CH]) for r in range(1, RING)]
        inv_wide = [keep["inv_first"]] + [sb(f"inv_wide{r}", [P, KD, CH]) for r in range(1, RING)]
        late = [sb("late_sums_f", [P, HG * T // P]), sb("late_inv_f", [P, HG * T // P])]
        gate = [sb(f"gate{r}", [P, TB, D]) for r in range(2)]
        x_all, mix = keep["x"], keep["mix"]
        p_o = [ctx.enter_context(nc.psum_tensor(f"p_o{r}", [P, TB, D], F32)) for r in range(2)]

        y_in = [keep["first_in"]] + [sem(f"y_in_f{n}") for n in range(1, RING)]
        sums_in = sem("sums_in")
        inv_ready = sem("inv_ready")
        inv_stored = sem("inv_stored")
        y_ready = sem("y_ready_f")
        gate_ready = sem("gate_ready")
        proj_made = sem("proj_made")
        biased = sem("biased")
        scaled = sem("scaled")
        summed = sem("summed")
        out_stored = sem("out_stored_f")
        block = ctx.enter_context(nc.Block())
        NS = NT // TB

        @block.sync
        def _(sp):
            late_in(sp, a, late[0], 1, sums_in)
            for s in range(1, RING):
                step_in(sp, a, yt[s], inv_wide[s], s, y_in[s])
            sp.wait_ge(inv_ready, 1)
            late_out(sp, a, late[1], 1, inv_stored)
            sp.wait_ge(inv_stored, 16 * HG)
            for s in range(NS):
                if s + RING < NS:
                    sp.wait_ge(proj_made, s + 1)
                    step_in(sp, a, yt[s % RING], inv_wide[s % RING], s + RING, y_in[s % RING])
                sp.wait_ge(summed, s + 1)
                sp.dma_start(a["out"][s * TB * P:(s + 1) * TB * P].rearrange("(t p) d -> p t d", p=P),
                             mix[:, s * TB:(s + 1) * TB]).then_inc(out_stored, 16)
            sp.wait_ge(out_stored, 16 * NS)

        @block.tensor
        def _(pe):
            t_ = nc.tensor
            pe.wait_ge(keep["wo_in"], 32)
            for s in range(NS):
                pe.wait_ge(y_ready, s + 1)
                if s >= 2:
                    pe.wait_ge(biased, s - 1)
                for t in range(TB):
                    for k in range(KD):
                        mm = t_.matmul(p_o[s % 2][:, t], yt[s % RING][:, k, t * P:(t + 1) * P], wo[:, k],
                                       start=(k == 0), stop=(k == KD - 1))
                mm.then_inc(proj_made, 1)

        @block.scalar
        def _(act):
            for s in range(NS):
                cur = slice(s * TB, (s + 1) * TB)
                if s >= 2:
                    act.wait_ge(scaled, s - 1)
                nc.scalar.activation(gate[s % 2][:], mix[:, cur], ACT.Silu).then_inc(gate_ready, 1)

        @block.vector
        def _(dve):
            v = nc.vector
            dve.wait_ge(keep["wo_in"], 32)
            bias = bo[:].unsqueeze(1).broadcast_to([P, TB, D])

            def normalise(s):
                dve.wait_ge(y_in[s % RING], 16 * 2 * KD * (s // RING + 1))
                v.tensor_tensor(yt[s % RING][:], yt[s % RING][:], inv_wide[s % RING][:], ALU.mult).then_inc(y_ready, 1)

            normalise(0)
            dve.wait_ge(sums_in, 16 * HG)
            v.reciprocal(late[1][:], late[0][:]).then_inc(inv_ready, 1)
            for s in range(NS):
                cur = slice(s * TB, (s + 1) * TB)
                if s + 1 < NS:
                    normalise(s + 1)
                dve.wait_ge(gate_ready, s + 1)
                dve.wait_ge(proj_made, s + 1)
                v.tensor_tensor(mix[:, cur], p_o[s % 2][:], bias, ALU.add).then_inc(biased, 1)
                dve.wait_ge(biased, s + 1)
                v.tensor_tensor(mix[:, cur], mix[:, cur], gate[s % 2][:], ALU.mult).then_inc(scaled, 1)

        @block.gpsimd
        def _(pool):
            for s in range(NS):
                cur = slice(s * TB, (s + 1) * TB)
                pool.wait_ge(scaled, s + 1)
                nc.gpsimd.tensor_tensor(mix[:, cur], mix[:, cur], x_all[:, cur], ALU.add).then_inc(summed, 1)


def build(nc, a):
    with ExitStack() as ctx:
        def sb(name, shape, dt=F32):
            return ctx.enter_context(nc.sbuf_tensor(name, shape, dt))

        keep = {
            "logits": sb("logits", [P, NT * E]), "below": sb("below", [P, NT * E]),
            "mean": sb("mean", [P, NT]), "rstd": sb("rstd", [P, NT]), "second": sb("second", [P, NT]),
            "fits": sb("fits", [P, NT]), "fetch": sb("fetch", [P, 2, NT], I32),
        }
        keep["store"] = sb("store", [P, NT * D])
        half = NT * D // 2
        q, k = (keep["store"][0:KM, n * half:(n + 1) * half].bitcast(BF16) for n in range(2))
        keep["heads"] = [q.rearrange("p (c h n) -> p c h n", c=CPB, h=HG), k.rearrange("p (h n) -> p h n", h=HG)]
        keep["heads_loaded"] = ctx.enter_context(nc.semaphore("heads_loaded"))
        with ExitStack() as early:
            keep["w_first"] = early.enter_context(nc.sbuf_tensor("w_first", [P, WW], F32))
            keep["w_first_loaded"] = early.enter_context(nc.semaphore("w_first_loaded"))
            normalise_route_project(nc, a, keep)
            run_experts(nc, a, keep)
        keep["wo"], keep["bo"] = sb("wo", [P, KD, D]), sb("bo", [P, D])
        keep["y_first"], keep["inv_first"] = sb("y_first", [P, KD, CH]), sb("inv_first", [P, KD, CH])
        keep["first_in"], keep["wo_in"] = (ctx.enter_context(nc.semaphore(name)) for name in ("first_in", "wo_in"))
        keep["x"], keep["mix"] = sb("x_kept", [P, NT, D]), sb("mix", [P, NT, D])
        attend(nc, a, keep)
        finish(nc, a, keep)


SCRATCH = {
    "xth": (P, KD, N), "xtl": (P, KD, N), "qk0": (2, KD, P, N), "qk1": (2, KD, P, N), "qk2": (2, KD, P, N),
    "v": (N, H * 2 * HD), "fd": (N, D), "xb": (2 * SLOTS, D), "ob": (SLOTS, D), "yt": (2 * D, N), "inv": (H, N),
}


def tables():
    import numpy as np
    theta = (1.0 / np.float32(10000.0) ** (np.arange(0, HD, 2, dtype=np.float32) / np.float32(HD))).astype(np.float32)
    angle = np.arange(1, T + 1, dtype=np.float32)[None, :] * np.tile(theta, P // (HD // 2))[:, None]
    sign = np.where(np.arange(P) % HD < HD // 2, -1.0, 1.0).astype(np.float32)
    row, col = np.arange(P)[:, None], np.arange(P)[None, :]
    bf16 = mybir.dt.np(BF16)
    tok = np.arange(NT)[None, None, :] * P + np.arange(P)[:, None, None]
    return {
        "cos": np.cos(angle).astype(np.float32), "sin": (np.sin(angle) * sign[:, None]).astype(np.float32),
        "ident": np.eye(P, dtype=np.float32), "ident_b": np.eye(P).astype(bf16),
        "tri": (row < col).astype(bf16), "ones_b": np.ones((P, P), bf16),
        "hide_after_row": np.where(col > row, NEG, 0.0).astype(bf16),
        "hide_before_row": np.where(col < row, NEG, 0.0).astype(bf16),
        "idx_m": np.tile(np.arange(E, dtype=np.float32) - E, (P, NT)),
        "runs": np.tile((np.arange(NT * E) % NT != 0).astype(np.float32), (P, 1)),
        "trash": (SLOTS + 2 * tok + np.arange(2)[None, :, None]).astype(np.float32),
    }


def laid_out(i):
    import numpy as np
    c = np.ascontiguousarray
    i = {k: np.asarray(v) for k, v in i.items()}
    col = lambda v: c(v.reshape(KD, P).T)
    return {
        "x": c(i["L0_attn_x"].reshape(N, D)),
        "wqT": c(i["L0_attn_Wq"].T), "wkT": c(i["L0_attn_Wk"].T), "wvT": c(i["L0_attn_Wv"].T), "woT": c(i["L0_attn_Wo"].T),
        "bq": col(i["L0_attn_bq"]), "bk": col(i["L0_attn_bk"]),
        "bv": c(i["L0_attn_bv"][None, :]), "bo": c(i["L0_attn_bo"][None, :]),
        "wr": i["L0_ffn_Wr"], "normw": c(i["L0_ffn_norm_w"].reshape(E, KD, P).transpose(0, 2, 1)),
        "wg": i["L0_ffn_Wg"], "wu": i["L0_ffn_Wu"], "wd": i["L0_ffn_Wd"],
        "fnorm": col(i["L0_ffn_f_norm"]), "fwg": i["L0_ffn_fWg"], "fwu": i["L0_ffn_fWu"], "fwd": i["L0_ffn_fWd"],
    }


def kernel(**inputs):
    import numpy as np
    import concourse.bacc as bacc
    from concourse.bass_utils import run_bass_kernel_spmd

    nc = bacc.Bacc("TRN2", target_bir_lowering=False, num_devices=1)
    arrays, a = {}, {}
    for name, v in {**laid_out(inputs), **tables()}.items():
        v = np.ascontiguousarray(v)
        arrays["in_" + name] = v
        a[name] = nc.dram_tensor("in_" + name, v.shape, mybir.dt.from_np(v.dtype), kind="ExternalInput").ap()
    for name, shape in SCRATCH.items():
        a[name] = nc.dram_tensor(name, shape, BF16 if name.startswith("qk") else F32).ap()
    a["out"] = nc.dram_tensor("out", (N, D), F32, kind="ExternalOutput").ap()
    build(nc, a)
    r = run_bass_kernel_spmd(nc, [arrays], core_ids=[0])
    return r.results[0]["out"].reshape(B, T, D)
```
